# Optimizing a Trainium2 kernel written in Bass

```python
import numpy as np
import jax
import jax.numpy as jnp

def _softmax(x, axis=-1):
    return jax.nn.softmax(x, axis=axis)

def _gelu(x):
    return jax.nn.gelu(x, approximate=True)

def _silu(x):
    return jax.nn.silu(x)

def _sigmoid(x):
    return jax.nn.sigmoid(x)

def _layernorm(x, axis=-1, eps=1e-05):
    m = jnp.mean(x, axis=axis, keepdims=True)
    v = jnp.var(x, axis=axis, keepdims=True)
    return (x - m) / jnp.sqrt(v + eps)

def _scatter_add(tgt, idx, src, axis=0):
    return tgt.at[idx].add(src)

def _segment_sum(src, seg, n):
    return jax.ops.segment_sum(src, seg, n)
kernel_name = 'mk_gnn_preln_d2_gnn_r8_a3139b'

def setup_inputs(seed: int=0):
    np.random.seed(seed)
    _w = jnp.asarray

    def _rec_inputs():
        import jax
        import jax.numpy as jnp
        _gk = jax.random.key(seed)
        x = -0.0003713 + 1 * jax.random.normal(jax.random.fold_in(_gk, 1), (6250, 128), jnp.float32)
        src = jax.random.randint(jax.random.fold_in(_gk, 2), (200000,), 0, 6250, jnp.int32)
        dst = jnp.minimum((6250 * jax.random.uniform(jax.random.fold_in(_gk, 3), (200000,)) ** 2.0).astype(jnp.int32), 49999)
        _o = jnp.argsort(dst, stable=True)
        src = src[_o]
        dst = dst[_o]
        edge_attr_16 = 0.00028786 + 0.999816 * jax.random.normal(jax.random.fold_in(_gk, 11), (200000, 16), jnp.float32)
        return (x, src, dst, edge_attr_16)
    x, src, dst, edge_attr_16 = _rec_inputs()

    def _L0_gnn_setup():
        import jax, jax.numpy as jnp
        import numpy as np
        N = 12500
        E = 80000
        DIN = 128
        DMID = 128
        EPS = 1e-05

        def gcn_conv(x, src, dst, W, b, n_nodes):
            h = x @ W.T
            ones = jnp.ones(src.shape[0], dtype=x.dtype)
            deg = jax.ops.segment_sum(ones, dst, num_segments=n_nodes)
            dinv = jnp.where(deg > 0, jax.lax.rsqrt(deg), 0.0)
            norm = dinv[src] * dinv[dst]
            msg = h[src] * norm[:, None]
            out = jax.ops.segment_sum(msg, dst, num_segments=n_nodes)
            return out + b

        def graph_layernorm(x, gamma, beta):
            mean = jnp.mean(x)
            xc = x - mean
            var = jnp.mean(xc * xc)
            return xc * jax.lax.rsqrt(var + EPS) * gamma + beta
        key = jax.random.key(seed)
        ks = jax.random.split(key, 8)
        x = jax.random.normal(ks[0], (N, DIN), dtype=jnp.float32)
        edge_index = jax.random.randint(ks[1], (2, E), 0, N, dtype=jnp.int64)
        s1 = 1.0 / np.sqrt(DIN)
        s2 = 1.0 / np.sqrt(DMID)
        W1 = jax.random.uniform(ks[2], (DMID, DIN), jnp.float32, -s1, s1)
        b1 = jnp.zeros((DMID,), jnp.float32)
        g1 = jnp.ones((DMID,), jnp.float32)
        be1 = jnp.zeros((DMID,), jnp.float32)
        W2 = jax.random.uniform(ks[3], (DMID, DMID), jnp.float32, -s2, s2)
        b2 = jnp.zeros((DMID,), jnp.float32)
        g2 = jnp.ones((DMID,), jnp.float32)
        be2 = jnp.zeros((DMID,), jnp.float32)
        return {'x': x, 'edge_index': edge_index, 'W1': W1, 'b1': b1, 'g1': g1, 'be1': be1, 'W2': W2, 'b2': b2, 'g2': g2, 'be2': be2}
    _L0_gnn_all = _L0_gnn_setup()
    _L0_gnn_in = {k: v for k, v in _L0_gnn_all.items() if k in ('W1', 'b1', 'g1', 'be1', 'W2', 'b2', 'g2', 'be2')}
    del _L0_gnn_all

    def _L1_gnn_setup():
        import jax, jax.numpy as jnp
        import numpy as np
        BN_EPS = 1e-05

        def _bn(x, gamma, beta):
            m = jnp.mean(x, axis=0)
            v = jnp.var(x, axis=0)
            return (x - m) * jax.lax.rsqrt(v + BN_EPS) * gamma + beta
        key = jax.random.key(seed)
        ks = jax.random.split(key, 12)
        N, E, D, ED = (6250, 75000, 128, 16)
        s = lambda k, sh: jax.random.normal(k, sh, dtype=jnp.float32) * 0.05
        return {'h': jax.random.normal(ks[0], (N, D), dtype=jnp.float32), 'edge_index': jax.random.randint(ks[1], (2, E), 0, N, dtype=jnp.int64), 'edge_attr': jax.random.normal(ks[2], (E, ED), dtype=jnp.float32), 'ee_w1': s(ks[3], (ED, D)), 'ee_b1': jnp.zeros((D,), jnp.float32), 'ee_g1': jnp.ones((D,), jnp.float32), 'ee_bb1': jnp.zeros((D,), jnp.float32), 'ee_w2': s(ks[4], (D, D)), 'ee_b2': jnp.zeros((D,), jnp.float32), 'mlp_w1': s(ks[5], (D, D)), 'mlp_b1': jnp.zeros((D,), jnp.float32), 'mlp_g1': jnp.ones((D,), jnp.float32), 'mlp_bb1': jnp.zeros((D,), jnp.float32), 'mlp_w2': s(ks[6], (D, D)), 'mlp_b2': jnp.zeros((D,), jnp.float32), 'mlp_g2': jnp.ones((D,), jnp.float32), 'mlp_bb2': jnp.zeros((D,), jnp.float32)}
    _L1_gnn_all = _L1_gnn_setup()
    _L1_gnn_in = {k: v for k, v in _L1_gnn_all.items() if k in ('ee_w1', 'ee_b1', 'ee_g1', 'ee_bb1', 'ee_w2', 'ee_b2', 'mlp_w1', 'mlp_b1', 'mlp_g1', 'mlp_bb1', 'mlp_w2', 'mlp_b2', 'mlp_g2', 'mlp_bb2')}
    del _L1_gnn_all
    return {'x': x, 'src': src, 'dst': dst, 'edge_attr_16': edge_attr_16, 'L0_gnn_W1': _L0_gnn_in['W1'], 'L0_gnn_b1': _L0_gnn_in['b1'], 'L0_gnn_g1': _L0_gnn_in['g1'], 'L0_gnn_be1': _L0_gnn_in['be1'], 'L0_gnn_W2': _L0_gnn_in['W2'], 'L0_gnn_b2': _L0_gnn_in['b2'], 'L0_gnn_g2': _L0_gnn_in['g2'], 'L0_gnn_be2': _L0_gnn_in['be2'], 'L1_gnn_ee_w1': _L1_gnn_in['ee_w1'], 'L1_gnn_ee_b1': _L1_gnn_in['ee_b1'], 'L1_gnn_ee_g1': _L1_gnn_in['ee_g1'], 'L1_gnn_ee_bb1': _L1_gnn_in['ee_bb1'], 'L1_gnn_ee_w2': _L1_gnn_in['ee_w2'], 'L1_gnn_ee_b2': _L1_gnn_in['ee_b2'], 'L1_gnn_mlp_w1': _L1_gnn_in['mlp_w1'], 'L1_gnn_mlp_b1': _L1_gnn_in['mlp_b1'], 'L1_gnn_mlp_g1': _L1_gnn_in['mlp_g1'], 'L1_gnn_mlp_bb1': _L1_gnn_in['mlp_bb1'], 'L1_gnn_mlp_w2': _L1_gnn_in['mlp_w2'], 'L1_gnn_mlp_b2': _L1_gnn_in['mlp_b2'], 'L1_gnn_mlp_g2': _L1_gnn_in['mlp_g2'], 'L1_gnn_mlp_bb2': _L1_gnn_in['mlp_bb2']}

def reference(x, src, dst, edge_attr_16, L0_gnn_W1, L0_gnn_b1, L0_gnn_g1, L0_gnn_be1, L0_gnn_W2, L0_gnn_b2, L0_gnn_g2, L0_gnn_be2, L1_gnn_ee_w1, L1_gnn_ee_b1, L1_gnn_ee_g1, L1_gnn_ee_bb1, L1_gnn_ee_w2, L1_gnn_ee_b2, L1_gnn_mlp_w1, L1_gnn_mlp_b1, L1_gnn_mlp_g1, L1_gnn_mlp_bb1, L1_gnn_mlp_w2, L1_gnn_mlp_b2, L1_gnn_mlp_g2, L1_gnn_mlp_bb2):
    import jax
    import jax.numpy as jnp

    def _L0_gnn_ref(x, edge_index, W1, b1, g1, be1, W2, b2, g2, be2):
        import jax, jax.numpy as jnp
        import numpy as np
        N = 12500
        E = 80000
        DIN = 128
        DMID = 128
        EPS = 1e-05

        def gcn_conv(x, src, dst, W, b, n_nodes):
            h = x @ W.T
            ones = jnp.ones(src.shape[0], dtype=x.dtype)
            deg = jax.ops.segment_sum(ones, dst, num_segments=n_nodes)
            dinv = jnp.where(deg > 0, jax.lax.rsqrt(deg), 0.0)
            norm = dinv[src] * dinv[dst]
            msg = h[src] * norm[:, None]
            out = jax.ops.segment_sum(msg, dst, num_segments=n_nodes)
            return out + b

        def graph_layernorm(x, gamma, beta):
            mean = jnp.mean(x)
            xc = x - mean
            var = jnp.mean(xc * xc)
            return xc * jax.lax.rsqrt(var + EPS) * gamma + beta
        n = x.shape[0]
        loops = jnp.arange(n, dtype=edge_index.dtype)
        src = jnp.concatenate([edge_index[0], loops])
        dst = jnp.concatenate([edge_index[1], loops])
        h = gcn_conv(x, src, dst, W1, b1, n)
        h = jax.nn.relu(graph_layernorm(h, g1, be1))
        h = gcn_conv(h, src, dst, W2, b2, n)
        return jax.nn.relu(graph_layernorm(h, g2, be2))

    def _L1_gnn_ref(h, edge_index, edge_attr, ee_w1, ee_b1, ee_g1, ee_bb1, ee_w2, ee_b2, mlp_w1, mlp_b1, mlp_g1, mlp_bb1, mlp_w2, mlp_b2, mlp_g2, mlp_bb2):
        import jax, jax.numpy as jnp
        import numpy as np
        BN_EPS = 1e-05

        def _bn(x, gamma, beta):
            m = jnp.mean(x, axis=0)
            v = jnp.var(x, axis=0)
            return (x - m) * jax.lax.rsqrt(v + BN_EPS) * gamma + beta
        N = h.shape[0]
        src, dst = (edge_index[0], edge_index[1])
        e = jax.nn.relu(_bn(edge_attr @ ee_w1 + ee_b1, ee_g1, ee_bb1)) @ ee_w2 + ee_b2
        agg_edge = jax.ops.segment_sum(e, dst, num_segments=N)
        h = h + agg_edge
        neigh = jax.ops.segment_sum(h[src], dst, num_segments=N)
        z = h + neigh
        z = jax.nn.relu(_bn(z @ mlp_w1 + mlp_b1, mlp_g1, mlp_bb1))
        z = jax.nn.relu(_bn(z @ mlp_w2 + mlp_b2, mlp_g2, mlp_bb2))
        return z
    edge_index = jnp.stack([src, dst])
    h = jnp.maximum(_layernorm(x, axis=-1), 0.0)
    x = x + _L0_gnn_ref(h, edge_index, L0_gnn_W1, L0_gnn_b1, L0_gnn_g1, L0_gnn_be1, L0_gnn_W2, L0_gnn_b2, L0_gnn_g2, L0_gnn_be2)
    h = jnp.maximum(_layernorm(x, axis=-1), 0.0)
    x = x + _L1_gnn_ref(h, edge_index, edge_attr_16, L1_gnn_ee_w1, L1_gnn_ee_b1, L1_gnn_ee_g1, L1_gnn_ee_bb1, L1_gnn_ee_w2, L1_gnn_ee_b2, L1_gnn_mlp_w1, L1_gnn_mlp_b1, L1_gnn_mlp_g1, L1_gnn_mlp_bb1, L1_gnn_mlp_w2, L1_gnn_mlp_b2, L1_gnn_mlp_g2, L1_gnn_mlp_bb2)
    return x

_drawn_inputs = setup_inputs


def setup_inputs(seed=0):
    import zlib

    import numpy as np

    out = dict(_drawn_inputs(seed))
    spreads = {'L0_gnn_b1': (0.0, 0.1),
     'L0_gnn_g1': (1.0, 0.2),
     'L0_gnn_be1': (0.0, 0.1),
     'L0_gnn_b2': (0.0, 0.1),
     'L0_gnn_g2': (1.0, 0.2),
     'L0_gnn_be2': (0.0, 0.1),
     'L1_gnn_ee_b1': (0.0, 0.1),
     'L1_gnn_ee_g1': (1.0, 0.2),
     'L1_gnn_ee_bb1': (0.0, 0.1),
     'L1_gnn_ee_b2': (0.0, 0.1),
     'L1_gnn_mlp_b1': (0.0, 0.1),
     'L1_gnn_mlp_g1': (1.0, 0.2),
     'L1_gnn_mlp_bb1': (0.0, 0.1),
     'L1_gnn_mlp_b2': (0.0, 0.1),
     'L1_gnn_mlp_g2': (1.0, 0.2),
     'L1_gnn_mlp_bb2': (0.0, 0.1)}
    factors = {}
    for name, (base, spread) in spreads.items():
        noise = np.random.default_rng([zlib.crc32(name.encode()), seed]).standard_normal(out[name].shape)
        drawn = base * np.exp(spread * noise) if base else spread * noise
        out[name] = jnp.asarray(drawn.astype(out[name].dtype))
    for name, factor in factors.items():
        out[name] = (out[name] * factor).astype(out[name].dtype)
    return out
```

```python
from contextlib import ExitStack

import concourse.bass as bass
from concourse import mybir

F32 = mybir.dt.float32
BF16 = mybir.dt.bfloat16
I32 = mybir.dt.int32
ALU = mybir.AluOpType
ACT = mybir.ActivationFunctionType
AX = mybir.AxisListType

NODES, DIM, EDGES, EDIM = 6250, 128, 200000, 16
P = 128
WINDOW = 125
WINDOWS = NODES // WINDOW
TILES = -(-EDGES // P)
STEPS = TILES + WINDOWS - 1
HALF = 8
PAIR = 2 * HALF
ITERS = -(-STEPS // PAIR)
BLOCKS = -(-(ITERS + 1) * PAIR // P)
SLOTS = BLOCKS * P
EPS = 1e-5
NOWHERE = SLOTS * WINDOW
HROWS = EDGES // WINDOW
HCOLS = 16
CHUNKS = 10
CROWS = HROWS // CHUNKS
BIASROW = 32
QUAD = 4
GROUPS = -(-WINDOWS // QUAD)
WIDE = 500
ROWS = ("L0_gnn_b1", "L0_gnn_g1", "L0_gnn_be1", "L0_gnn_b2", "L0_gnn_g2", "L0_gnn_be2",
        "L1_gnn_ee_b1", "L1_gnn_ee_g1", "L1_gnn_ee_bb1", "L1_gnn_ee_b2")
COLS = ("L1_gnn_mlp_b1", "L1_gnn_mlp_g1", "L1_gnn_mlp_bb1", "L1_gnn_mlp_b2", "L1_gnn_mlp_g2",
        "L1_gnn_mlp_bb2")
MATS = ("L0_gnn_W1T", "L0_gnn_W2T", "L1_gnn_ee_w2", "L1_gnn_mlp_w1", "L1_gnn_mlp_w2")


def quads():
    return [(g, range(g * QUAD, min((g + 1) * QUAD, WINDOWS))) for g in range(GROUPS)]


def program(nc, A, out):
    ctx = ExitStack()
    with ctx:
        def sb(name, shape, dt=F32):
            return ctx.enter_context(nc.sbuf_tensor(name, shape, dt))

        def sem(name):
            return ctx.enter_context(nc.semaphore(name))

        def dram(name, shape, dt=F32):
            return nc.dram_tensor(name, shape, dt, kind="Internal").ap()

        tables = [dram(f"table{i}", (NODES, DIM)) for i in range(3)]
        wcol_dram = dram("wcol_dram", (BLOCKS, P), I32)
        attr_steps = dram("attr_steps", (SLOTS, EDIM * P))
        x1_dram = dram("x1_dram", (NODES, DIM))

        def by_window(ap):
            return ap.rearrange("(w p) d -> p w d", p=WINDOW)

        bank = [ctx.enter_context(nc.psum_tensor(f"bank{i}", [P, 512], F32)) for i in range(8)]
        ident = sb("ident", [P, P])
        ones = sb("ones", [P, P])
        node_iota = sb("node_iota", [P, WINDOW])
        src_steps = sb("src_steps", [P, SLOTS], I32)
        dst_steps = sb("dst_steps", [P, SLOTS])
        wcol_row = sb("wcol_row", [1, SLOTS], I32)
        acc = sb("acc", [P, NODES])
        acc_edge = sb("acc_edge", [P, NODES])
        nodes = sb("nodes", [WINDOW, WINDOWS, DIM])
        spare = sb("spare", [WINDOW, WINDOWS, DIM])
        dinv = sb("dinv", [WINDOW, WINDOWS])
        indeg = sb("indeg", [WINDOW, WINDOWS])
        stat = sb("stat", [WINDOW, 2, WINDOWS])
        col = sb("col", [P, 16])
        rows = sb("rows", [P, len(ROWS), DIM])
        cols = sb("cols", [P, len(COLS)])
        mats = sb("mats", [P, len(MATS), DIM])
        ew1 = sb("ew1", [EDIM, DIM])
        edge_w = sb("edge_w", [BIASROW + 1, DIM])
        idx = sb("idx", [P, 2, HALF], I32)
        msg = sb("msg", [P, 2, HALF, DIM])
        onehot = sb("onehot", [P, 2, HALF, WINDOW])

        def rowpar(name, parts=WINDOW):
            return rows[0:parts, ROWS.index(name), :]

        def over_windows(ap):
            return ap.unsqueeze(1).broadcast_to([WINDOW, WINDOWS, DIM])

        def over_features(ap):
            return ap.unsqueeze(2).broadcast_to([WINDOW, WINDOWS, DIM])

        s_dve, s_act, s_pe, s_pool, s_dma = (sem(f"s_{n}") for n in ("dve", "act", "pe", "pool", "dma"))
        ended = {}

        def link(eng, chain, ins, by=1):
            ended[chain.name] = ended.get(chain.name, 0) + by
            ins.then_inc(chain, by)
            eng.wait_ge(chain, ended[chain.name])
            return ended[chain.name]


        v = nc.vector
        s_var, s_root = sem("s_var"), sem("s_root")
        roots = []

        def rsqrt(dve, ap, scale):
            v.tensor_scalar(ap, ap, scale, EPS if scale != 1.0 else 0.0, ALU.mult, ALU.add).then_inc(s_var, 1)
            roots.append(ap)
            dve.wait_ge(s_root, len(roots))
            link(dve, s_dve, v.reciprocal(ap, ap))

        def take_roots(act, first):
            for n in range(first, len(roots)):
                act.wait_ge(s_var, n + 1)
                nc.scalar.activation(roots[n], roots[n], ACT.Sqrt).then_inc(s_root, 1)

        def layer_norm_relu(dve, t, tmp, sums, rstd, factor=None):
            link(dve, s_dve, v.tensor_reduce(sums, t, AX.X, ALU.add))
            link(dve, s_dve, v.tensor_scalar(sums, sums, 1.0 / DIM, None, ALU.mult))
            link(dve, s_dve, v.tensor_tensor(t, t, over_features(sums), ALU.subtract))
            link(dve, s_dve, v.tensor_tensor(tmp, t, t, ALU.mult))
            link(dve, s_dve, v.tensor_reduce(rstd, tmp, AX.X, ALU.add))
            rsqrt(dve, rstd, 1.0 / DIM)
            if factor is not None:
                link(dve, s_dve, v.tensor_tensor(rstd, rstd, factor, ALU.mult))
            link(dve, s_dve, v.scalar_tensor_tensor(t, t, 0.0, over_features(rstd), ALU.max, ALU.mult))

        def split_windows(dve, dst, win, rest, whole):
            link(dve, s_dve, v.tensor_scalar(win, dst, 0.5, 1.0 / WINDOW, ALU.add, ALU.mult))
            link(dve, s_dve, v.tensor_copy(whole, win))
            link(dve, s_dve, v.tensor_scalar(win, whole, -1.0, None, ALU.add))
            link(dve, s_dve, v.scalar_tensor_tensor(rest, win, -float(WINDOW), dst, ALU.mult, ALU.add))
            link(dve, s_dve, v.scalar_tensor_tensor(win, rest, float(WINDOW), win, ALU.is_ge, ALU.add))
            link(dve, s_dve, v.scalar_tensor_tensor(rest, win, -float(WINDOW), dst, ALU.mult, ALU.add))

        hold = ExitStack()

        def small(name, shape, dt=F32):
            return hold.enter_context(nc.sbuf_tensor(name, shape, dt))

        dst_all = small("dst_all", [WINDOW, HROWS], I32)
        win_of = small("win_of", [WINDOW, HROWS], BF16)
        node_of = small("node_of", [WINDOW, HROWS], BF16)
        iota_bf = small("iota_bf", [WINDOW, WINDOW], BF16)
        zeros_bf = small("zeros_bf", [WINDOW, WINDOW], BF16)
        hot_node = small("hot_node", [WINDOW, 2, HCOLS, WINDOW], BF16)
        hot_win = small("hot_win", [WINDOW, 2, HCOLS, WINDOWS], BF16)
        step_iota = small("step_iota", [P, BLOCKS])
        tpos = small("tpos", [P, BLOCKS])
        wfirst = small("wfirst", [P, BLOCKS])
        wcol = small("wcol", [P, BLOCKS])
        tile_idx = small("tile_idx", [P, BLOCKS], I32)
        wcol_int = small("wcol_int", [BLOCKS, P], I32)
        block_mask = small("block_mask", [P, P])
        fold = small("fold", [P, EDIM])
        fdst, fwin, frest = (acc[0:WINDOW, k * HROWS:(k + 1) * HROWS] for k in range(3))
        iwin = acc_edge[0:WINDOW, 0:HROWS].bitcast(I32)
        one_row = spare[0:1].rearrange("p w d -> p (w d)")
        last_dst, tile_end, tile_rest, tile_iota = (one_row[:, k * TILES:(k + 1) * TILES] for k in range(4))
        last_int = acc_edge[0:1, HROWS:HROWS + TILES].bitcast(I32)
        tile_whole = acc_edge[0:1, HROWS + TILES:HROWS + 2 * TILES].bitcast(I32)
        end_all, end_cmp = (acc[:, k * TILES:(k + 1) * TILES] for k in range(2))

        def blocks_in(t, k):
            return t[:, k * SLOTS:(k + 1) * SLOTS].rearrange("p (j e) -> p j e", e=P)

        src_rows, dst_rows = blocks_in(acc_edge, 0).bitcast(I32), blocks_in(acc_edge, 1).bitcast(I32)
        src_rows_f = blocks_in(acc_edge, 2)
        dst_rows_f = acc[:, 2 * TILES:2 * TILES + SLOTS].rearrange("p (j e) -> p j e", e=P)
        s_const, s_par, s_x, s_dst = (sem(f"s_{n}") for n in ("const", "par", "x", "dst"))
        with nc.Block() as block:
            @block.sync
            def _(sp):
                sp.dma_start(dst_all[:], A["dst"].rearrange("(p c) -> p c", p=WINDOW)).then_inc(s_dst, 16)
                sp.dma_start(ident[:], A["ident"]).then_inc(s_const, 16)
                sp.dma_start(node_iota[:], A["node_iota"]).then_inc(s_const, 16)
                sp.dma_start(step_iota[:], A["step_iota"]).then_inc(s_const, 16)
                sp.dma_start(block_mask[:], A["block_mask"]).then_inc(s_par, 16)
                sp.dma_start(fold[:], A["fold"]).then_inc(s_par, 16)
                sp.dma_start(tile_iota, A["tile_iota"]).then_inc(s_const, 16)
                sp.dma_start(last_int, A["dst_last"]).then_inc(s_const, 16)
                sp.dma_start(nodes[:], by_window(A["x"])).then_inc(s_x, 16)
                for k, n in enumerate(ROWS):
                    sp.dma_start(rows[:, k, :], A[n].unsqueeze(0).broadcast_to([P, DIM])).then_inc(s_par, 16)
                for k, n in enumerate(COLS):
                    sp.dma_start(cols[:, k:k + 1], A[n].unsqueeze(1)).then_inc(s_par, 16)
                for k, n in enumerate(MATS):
                    sp.dma_start(mats[:, k, :], A[n]).then_inc(s_par, 16)
                sp.dma_start(ew1[:], A["L1_gnn_ee_w1"]).then_inc(s_par, 16)
                sp.wait_ge(s_x, 16)
                sp.wait_ge(s_par, 16 * (len(ROWS) + len(COLS) + len(MATS) + 3))

            @block.vector
            def _(dve):
                v.memset(ones[:], 1.0)
                v.memset(edge_w[:], 0.0)
                v.memset(zeros_bf[:], 0.0)
                dve.wait_ge(s_const, 5 * 16)
                link(dve, s_dve, v.tensor_copy(iota_bf[:], node_iota[0:WINDOW, :]))
                dve.wait_ge(s_dst, 16)
                link(dve, s_dve, v.tensor_copy(fdst, dst_all[:]))
                split_windows(dve, fdst, fwin, frest, iwin)
                link(dve, s_dve, v.tensor_copy(win_of[:], fwin))
                link(dve, s_dve, v.tensor_copy(node_of[:], frest))
                link(dve, s_dve, v.tensor_copy(last_dst, last_int))
                split_windows(dve, last_dst, tile_end, tile_rest, tile_whole)
                link(dve, s_dve, v.tensor_scalar(tile_end, tile_end, float(WINDOWS - 1), None, ALU.min))
                link(dve, s_dve, v.tensor_tensor(tile_end, tile_end, tile_iota, ALU.add))
                link(dve, s_dve, v.memset(tile_end[:, TILES - 1:TILES], float(STEPS - 1)))

        s_endb, s_tpos, s_wt, s_wdone, s_wrow, s_wback = (
            sem(f"s_{n}") for n in ("endb", "tpos", "wt", "wdone", "wrow", "wback"))
        s_rows, s_srcf, s_tr, s_trc = (sem(f"s_{n}") for n in ("rows", "srcf", "tr", "trc"))
        ends = [(k, min(512, TILES - k)) for k in range(0, TILES, 512)]
        with nc.Block() as block:
            @block.tensor
            def _(pe):
                for n, (k, m) in enumerate(ends):
                    nc.tensor.matmul(bank[n][:, 0:m], ones[0:1, :], tile_end[:, k:k + m], start=True,
                                     stop=True).then_inc(s_endb, 1)
                pe.wait_ge(s_wt, 1)
                nc.tensor.transpose(bank[4][0:BLOCKS, 0:P], wcol[:], ident[:]).then_inc(s_wdone, 1)
                for j in range(BLOCKS):
                    for n, rows_f in ((0, dst_rows_f), (1, src_rows_f)):
                        m = 2 * j + n
                        pe.wait_ge(s_srcf, m + 1)
                        if m >= 2:
                            pe.wait_ge(s_trc, m - 1)
                        nc.tensor.transpose(bank[5 + n][:, 0:P], rows_f[:, j, :], ident[:]).then_inc(s_tr, 1)

            @block.vector
            def _(dve):
                for n, (k, m) in enumerate(ends):
                    dve.wait_ge(s_endb, n + 1)
                    link(dve, s_dve, v.tensor_copy(end_all[:, k:k + m], bank[n][:, 0:m]))
                for j in range(BLOCKS):
                    link(dve, s_dve, v.tensor_scalar(end_cmp, end_all, step_iota[:, j:j + 1], None, ALU.is_lt,
                                                     ALU.add, accum_out=tpos[:, j:j + 1]))
                link(dve, s_dve, v.tensor_scalar(tpos[:], tpos[:], float(TILES - 1), None, ALU.min))
                v.tensor_copy(tile_idx[:], tpos[:]).then_inc(s_tpos, 1)
                link(dve, s_dve, v.tensor_tensor(tpos[:], step_iota[:], tpos[:], ALU.subtract))
                link(dve, s_dve, v.tensor_scalar(wfirst[:], tpos[:], float(WINDOW), None, ALU.mult))
                v.tensor_scalar(wcol[:], wfirst[:], float((WINDOWS - 1) * WINDOW), None, ALU.min).then_inc(s_wt, 1)
                dve.wait_ge(s_wdone, 1)
                v.tensor_copy(wcol_int[:], bank[4][0:BLOCKS, 0:P]).then_inc(s_wrow, 1)
                for j in range(BLOCKS + 1):
                    if j < BLOCKS:
                        dve.wait_ge(s_rows, 32 * BLOCKS)
                        v.tensor_scalar(dst_rows_f[:, j, :], dst_rows[:, j, :], wfirst[:, j:j + 1], None,
                                        ALU.subtract).then_inc(s_srcf, 1)
                        v.tensor_copy(src_rows_f[:, j, :], src_rows[:, j, :]).then_inc(s_srcf, 1)
                    if j >= 1:
                        for n, steps in ((0, dst_steps), (1, src_steps)):
                            dve.wait_ge(s_tr, 2 * (j - 1) + n + 1)
                            v.tensor_copy(steps[:, (j - 1) * P:j * P], bank[5 + n][:, 0:P]).then_inc(s_trc, 1)

            @block.gpsimd
            def _(pool):
                pool.wait_ge(s_tpos, 1)
                for j in range(BLOCKS):
                    for a, r in (("src_tiles", src_rows), ("dst_tiles", dst_rows)):
                        nc.gpsimd.indirect_dma_start(
                            r[:, j, :], None, A[a], bass.IndirectOffsetOnAxis(ap=tile_idx[:, j:j + 1], axis=0)
                        ).then_inc(s_rows, 16)
                pool.wait_ge(s_rows, 32 * BLOCKS)

            @block.sync
            def _(sp):
                sp.wait_ge(s_wrow, 1)
                sp.dma_start(wcol_dram, wcol_int[:]).then_inc(s_wback, 16)
                sp.wait_ge(s_wback, 16)
                sp.dma_start(wcol_row[:], wcol_dram.rearrange("j p -> (j p)").unsqueeze(0)).then_inc(s_wback, 16)
                sp.wait_ge(s_wback, 32)

        s_hot, s_hist = ([sem(f"s_{n}{h}") for h in range(2)] for n in ("hot", "hist"))
        s_hist_end = sem("s_hist_end")
        s_attr = [sem(f"s_attr{k}") for k in range(2)]
        s_attr_out = [sem(f"s_attr_out{k}") for k in range(2)]
        attr_buf = [t[:, 0:EDIM * P] for t in (acc, acc_edge)]
        with nc.Block() as block:
            @block.gpsimd
            def _(pool):
                for j in range(BLOCKS):
                    if j >= 2:
                        pool.wait_ge(s_attr_out[j % 2], 16 * (j // 2))
                    nc.gpsimd.indirect_dma_start(
                        attr_buf[j % 2], None, A["attr_tiles"],
                        bass.IndirectOffsetOnAxis(ap=tile_idx[:, j:j + 1], axis=0)).then_inc(s_attr[j % 2], 16)

            @block.sync
            def _(sp):
                for j in range(BLOCKS):
                    sp.wait_ge(s_attr[j % 2], 16 * (j // 2 + 1))
                    sp.dma_start(attr_steps[j * P:(j + 1) * P, :], attr_buf[j % 2]).then_inc(s_attr_out[j % 2], 16)
                for k in range(2):
                    sp.wait_ge(s_attr_out[k], 16 * len(range(k, BLOCKS, 2)))

            @block.vector
            def _(dve):
                with dve.Fori(0, HROWS // HCOLS // 2) as i:
                    for h in range(2):
                        dve.wait_ge(s_hist[h], i + 1)
                        at = bass.ds(i * (2 * HCOLS) + h * HCOLS, HCOLS)
                        v.tensor_tensor(hot_node[:, h], iota_bf[:].unsqueeze(1).broadcast_to([WINDOW, HCOLS, WINDOW]),
                                        node_of[:, at].unsqueeze(2).broadcast_to([WINDOW, HCOLS, WINDOW]),
                                        ALU.is_equal).then_inc(s_hot[h], 1)
                        v.tensor_tensor(hot_win[:, h],
                                        iota_bf[:, 0:WINDOWS].unsqueeze(1).broadcast_to([WINDOW, HCOLS, WINDOWS]),
                                        win_of[:, at].unsqueeze(2).broadcast_to([WINDOW, HCOLS, WINDOWS]),
                                        ALU.is_equal).then_inc(s_hot[h], 1)
                dve.wait_ge(s_hist_end, 1)
                link(dve, s_dve, v.tensor_copy(indeg[:], bank[0][0:WINDOW, 0:WINDOWS]))
                link(dve, s_dve, v.tensor_scalar(dinv[:], indeg[:], 1.0, None, ALU.add))
                rsqrt(dve, dinv[:], 1.0)
                layer_norm_relu(dve, nodes[:], spare[:], stat[:, 0, :], stat[:, 1, :], dinv[:])

            @block.scalar
            def _(act):
                take_roots(act, 0)

            @block.tensor
            def _(pe):
                degrees = bank[0][0:WINDOW, 0:WINDOWS]
                for s in s_hist:
                    pe.sem_inc(s, 1)
                nc.tensor.matmul(degrees, zeros_bf[:], zeros_bf[:, 0:WINDOWS], start=True, stop=False)
                with pe.Fori(0, HROWS // HCOLS // 2) as i:
                    for h in range(2):
                        pe.wait_ge(s_hot[h], i * 2 + 2)
                        for c in range(HCOLS):
                            last = nc.tensor.matmul(degrees, hot_node[:, h, c, :], hot_win[:, h, c, :],
                                                    start=False, stop=False)
                        last.then_inc(s_hist[h], 1)
                nc.tensor.matmul(degrees, zeros_bf[:], zeros_bf[:, 0:WINDOWS], start=False,
                                 stop=True).then_inc(s_hist_end, 1)

        s_tab = [sem(f"s_tab{k}") for k in range(3)]
        s_feat = [sem(f"s_feat{k}") for k in range(2)]
        s_shift, s_gram, s_gram_m, s_sum, s_stat = (sem(f"s_{n}") for n in ("shift", "gram", "gram_m", "sum", "stat"))
        feat = [hold.enter_context(nc.sbuf_tensor(f"feat{k}", [WINDOW, CROWS, EDIM], F32)) for k in range(2)]
        featsum = small("featsum", [WINDOW, CHUNKS, EDIM])
        featmean = small("featmean", [WINDOW, EDIM])
        gram = small("gram", [P, P])
        gram_fold = small("gram_fold", [P, EDIM])
        cov = small("cov", [EDIM, EDIM])
        cov_w = small("cov_w", [EDIM, DIM])
        mean_col = small("mean_col", [EDIM, 1])
        mean_cols = small("mean_cols", [EDIM, P])
        scale_rows = small("scale_rows", [BIASROW + 1, DIM])
        shift_rows = small("shift_rows", [BIASROW + 1, DIM])
        PACK = P // EDIM
        GRAMS = CROWS // PACK
        attr_by_part = A["edge_attr_16"].rearrange("(p c r) f -> p c r f", p=WINDOW, c=CHUNKS)
        with nc.Block() as block:
            @block.sync
            def _(sp):
                for n in range(2 * CHUNKS):
                    if n >= 2:
                        if n - 2 < CHUNKS:
                            sp.wait_ge(s_sum, n - 1)
                        else:
                            sp.wait_ge(s_gram, n - 1 - CHUNKS)
                    sp.dma_start(feat[n % 2][:], attr_by_part[:, n % CHUNKS]).then_inc(s_feat[n % 2], 16)

            @block.vector
            def _(dve):
                for n in range(CHUNKS):
                    dve.wait_ge(s_feat[n % 2], 16 * (n // 2 + 1))
                    v.tensor_reduce(featsum[:, n, :], feat[n % 2][:].rearrange("p r f -> p f r"), AX.X,
                                    ALU.add).then_inc(s_sum, 1)
                dve.wait_ge(s_sum, CHUNKS)
                link(dve, s_dve, v.tensor_reduce(featmean[:], featsum[:].rearrange("p c f -> p f c"), AX.X, ALU.add))
                link(dve, s_dve, v.tensor_copy(featsum[:, 0, :], featmean[:]))
                v.tensor_scalar(featmean[:], featmean[:], 1.0 / EDGES, None, ALU.mult).then_inc(s_stat, 1)
                dve.wait_ge(s_gram_m, 2)
                link(dve, s_dve, v.tensor_copy(featmean[:], bank[1][0:WINDOW, 0:EDIM]))
                link(dve, s_dve, v.tensor_copy(mean_col[:], bank[2][0:EDIM, 0:1]))
                v.tensor_copy(mean_cols[:], mean_col[:].broadcast_to([EDIM, P])).then_inc(s_stat, 1)
                for n in range(CHUNKS, 2 * CHUNKS):
                    dve.wait_ge(s_feat[n % 2], 16 * (n // 2 + 1))
                    v.tensor_tensor(feat[n % 2][:], feat[n % 2][:],
                                    featmean[:].unsqueeze(1).broadcast_to([WINDOW, CROWS, EDIM]),
                                    ALU.subtract).then_inc(s_shift, 1)
                dve.wait_ge(s_gram, CHUNKS)
                v.tensor_tensor(gram[:], bank[0][:, 0:P], block_mask[:], ALU.mult).then_inc(s_stat, 1)
                dve.wait_ge(s_gram_m, 3)
                v.tensor_copy(gram_fold[:], bank[1][:, 0:EDIM]).then_inc(s_stat, 1)
                dve.wait_ge(s_gram_m, 4)
                v.tensor_scalar(cov[:], bank[2][0:EDIM, 0:EDIM], 1.0 / EDGES, None, ALU.mult).then_inc(s_stat, 1)
                dve.wait_ge(s_gram_m, 5)
                v.tensor_tensor(cov_w[:], bank[1][0:EDIM, 0:DIM], ew1[:], ALU.mult).then_inc(s_stat, 1)
                dve.wait_ge(s_gram_m, 7)
                r = slice(0, BIASROW + 1)
                b1, g1, bb1 = (rowpar(n, BIASROW + 1) for n in ("L1_gnn_ee_b1", "L1_gnn_ee_g1", "L1_gnn_ee_bb1"))
                link(dve, s_dve, v.tensor_scalar(scale_rows[:], bank[2][r, 0:DIM], 1.0, EPS, ALU.mult, ALU.add))
                rsqrt(dve, scale_rows[:], 1.0)
                link(dve, s_dve, v.tensor_tensor(scale_rows[:], scale_rows[:], g1, ALU.mult))
                link(dve, s_dve, v.tensor_tensor(shift_rows[:], bank[3][r, 0:DIM], b1, ALU.add))
                link(dve, s_dve, v.tensor_tensor(shift_rows[:], b1, shift_rows[:], ALU.subtract))
                link(dve, s_dve, v.tensor_tensor(shift_rows[:], shift_rows[:], scale_rows[:], ALU.mult))
                link(dve, s_dve, v.tensor_tensor(shift_rows[:], shift_rows[:], bb1, ALU.add))
                link(dve, s_dve, v.tensor_tensor(edge_w[0:EDIM, :], ew1[:], scale_rows[0:EDIM, :], ALU.mult))
                link(dve, s_dve, v.tensor_copy(edge_w[BIASROW:BIASROW + 1, :], shift_rows[BIASROW:BIASROW + 1, :]))

            @block.scalar
            def _(act):
                take_roots(act, 2)

            @block.tensor
            def _(pe):
                pe.wait_ge(s_stat, 1)
                nc.tensor.matmul(bank[1][0:WINDOW, 0:EDIM], ones[0:WINDOW, 0:WINDOW], featmean[:], start=True,
                                 stop=True).then_inc(s_gram_m, 1)
                nc.tensor.matmul(bank[2][0:EDIM, 0:1], featmean[:], ones[0:WINDOW, 0:1], start=True,
                                 stop=True).then_inc(s_gram_m, 1)
                for n in range(CHUNKS):
                    pe.wait_ge(s_shift, n + 1)
                    for k in range(GRAMS):
                        part = feat[n % 2][:, k * PACK:(k + 1) * PACK, :].rearrange("p r f -> p (r f)")
                        last = nc.tensor.matmul(bank[0][:, 0:P], part, part, start=(n == k == 0),
                                                stop=(n == CHUNKS - 1 and k == GRAMS - 1))
                    last.then_inc(s_gram, 1)
                pe.wait_ge(s_stat, 3)
                nc.tensor.matmul(bank[1][:, 0:EDIM], gram[:], fold[:], start=True, stop=True).then_inc(s_gram_m, 1)
                pe.wait_ge(s_stat, 4)
                nc.tensor.matmul(bank[2][0:EDIM, 0:EDIM], fold[:], gram_fold[:], start=True,
                                 stop=True).then_inc(s_gram_m, 1)
                pe.wait_ge(s_stat, 5)
                nc.tensor.matmul(bank[1][0:EDIM, 0:DIM], cov[:], ew1[:], start=True, stop=True).then_inc(s_gram_m, 1)
                pe.wait_ge(s_stat, 6)
                nc.tensor.matmul(bank[2][:, 0:DIM], ones[0:EDIM, :], cov_w[:], start=True, stop=True).then_inc(s_gram_m, 1)
                nc.tensor.matmul(bank[3][:, 0:DIM], mean_cols[:], ew1[:], start=True, stop=True).then_inc(s_gram_m, 1)

        hold.close()
        attr_ring = sb("attr_ring", [BIASROW + 1, 2, HALF, P])
        edge_msg = sb("edge_msg", [P, HALF, DIM])

        def edge_pass(layer, with_edges):
            s_gather, s_onehot, s_used, s_taken, s_ein, s_prod, s_emsg, s_eused, s_etaken = (
                [sem(f"s_{n}{layer}_{h}") for h in range(2)]
                for n in ("gather", "onehot", "used", "taken", "ein", "prod", "emsg", "eused", "etaken"))
            s_idx, s_go, s_addn, s_adde = (sem(f"s_{n}{layer}") for n in ("idx", "go", "addn", "adde"))
            DONE = 16 * HALF

            with nc.Block() as block:
                @block.gpsimd
                def _(pool):
                    with pool.Fori(0, ITERS) as i:
                        for h in range(2):
                            pool.wait_ge(s_used[h], i + 1)
                            nc.gpsimd.tensor_copy(
                                idx[:, h, :], src_steps[:, bass.ds(i * PAIR + h * HALF, HALF)]).then_inc(s_idx, 1)
                            pool.wait_ge(s_idx, i * 2 + (h + 1))
                            pool.sem_inc(s_go, 1)
                            for k in range(HALF):
                                nc.gpsimd.indirect_dma_start(
                                    msg[:, h, k, :], None, tables[layer],
                                    bass.IndirectOffsetOnAxis(ap=idx[:, h, k:k + 1], axis=0)
                                ).then_inc(s_gather[h], 16)

                if with_edges:
                    @block.sync
                    def _(sp):
                        with sp.Fori(0, ITERS) as i:
                            for h in range(2):
                                sp.wait_ge(s_prod[h], i + 1)
                                sp.dma_start(
                                    attr_ring[0:EDIM, h],
                                    attr_steps[bass.ds(i * PAIR + h * HALF, HALF), :]
                                    .rearrange("s (f e) -> f s e", f=EDIM)).then_inc(s_ein[h], 16)

                    @block.scalar
                    def _(act):
                        for s in s_emsg:
                            act.sem_inc(s, 1)
                        with act.Fori(0, ITERS) as i:
                            for h in range(2):
                                act.wait_ge(s_prod[h], i + 2)
                                act.wait_ge(s_eused[1 - h], i + (h + 1))
                                for q in range(2):
                                    nc.scalar.activation(
                                        edge_msg[:, 4 * q:4 * q + 4, :].rearrange("p k d -> p (k d)"),
                                        bank[4 + q][:, :], ACT.Relu).then_inc(s_emsg[h], 1)

                @block.tensor
                def _(pe):
                    for s in s_used + (s_prod + s_eused if with_edges else []):
                        pe.sem_inc(s, 1)
                    with pe.Fori(0, ITERS) as i:
                        for h in range(2):
                            if with_edges:
                                pe.wait_ge(s_ein[h], i * 16 + 16)
                                pe.wait_ge(s_emsg[1 - h], i * 2 + (2 * h + 1))
                                for k in range(HALF):
                                    last = nc.tensor.matmul(bank[4 + k // 4][:, (k % 4) * P:(k % 4 + 1) * P],
                                                            attr_ring[:, h, k, :], edge_w[:], start=True, stop=True)
                                last.then_inc(s_prod[h], 1)
                            pe.wait_ge(s_gather[h], i * DONE + DONE)
                            pe.wait_ge(s_onehot[h], i + 1)
                            pe.wait_ge(s_taken[h], i + 1)
                            for k in range(HALF):
                                last = nc.tensor.matmul(
                                    bank[2 * h + k // 4][:, (k % 4) * P:(k % 4) * P + WINDOW],
                                    msg[:, h, k, :], onehot[:, h, k, :], start=True, stop=True)
                            last.then_inc(s_used[h], 1)
                            if with_edges:
                                pe.wait_ge(s_emsg[h], i * 2 + 3)
                                pe.wait_ge(s_etaken[1 - h], i + (h + 1))
                                for k in range(HALF):
                                    last = nc.tensor.matmul(
                                        bank[6 + k // 4][:, (k % 4) * P:(k % 4) * P + WINDOW],
                                        edge_msg[:, k, :], onehot[:, h, k, :], start=True, stop=True)
                                last.then_inc(s_eused[h], 1)

                @block.vector
                def _(dve):
                    def make_onehot(h, first):
                        v.tensor_tensor(
                            onehot[:, h], node_iota[:].unsqueeze(1).broadcast_to([P, HALF, WINDOW]),
                            dst_steps[:, first].unsqueeze(2).broadcast_to([P, HALF, WINDOW]),
                            ALU.is_equal).then_inc(s_onehot[h], 1)

                    for s in [s_addn] + s_taken + ([s_adde] + s_etaken if with_edges else []):
                        dve.sem_inc(s, 1)
                    for h in range(2):
                        make_onehot(h, slice(h * HALF, (h + 1) * HALF))
                    regs = [[dve.alloc_register(f"wcol{layer}_{h}_{k}") for k in range(HALF)] for h in range(2)]
                    with dve.Fori(0, ITERS) as i:
                        for h in range(2):
                            dve.reg_load(regs[h], wcol_row[0:1, bass.ds(i * PAIR + h * HALF, HALF)])
                            at = [dve.snap(r, min_val=0, max_val=NODES - WINDOW) for r in regs[h]]
                            dve.wait_ge(s_used[h], i + 2)
                            done = i * PAIR + h * HALF
                            for k in range(HALF):
                                part = acc[:, bass.ds(at[k], WINDOW)]
                                dve.wait_ge(s_addn, done + (k + 1))
                                v.tensor_tensor(part, part, bank[2 * h + k // 4][:, (k % 4) * P:(k % 4) * P + WINDOW],
                                                ALU.add).then_inc(s_addn, 1)
                                if with_edges:
                                    if k == 0:
                                        dve.wait_ge(s_eused[h], i + 2)
                                    part = acc_edge[:, bass.ds(at[k], WINDOW)]
                                    dve.wait_ge(s_adde, done + (k + 1))
                                    v.tensor_tensor(part, part,
                                                    bank[6 + k // 4][:, (k % 4) * P:(k % 4) * P + WINDOW],
                                                    ALU.add).then_inc(s_adde, 1)
                            dve.wait_ge(s_addn, done + (HALF + 1))
                            dve.sem_inc(s_taken[h], 1)
                            if with_edges:
                                dve.wait_ge(s_adde, done + (HALF + 1))
                                dve.sem_inc(s_etaken[h], 1)
                            make_onehot(h, bass.ds(i * PAIR + PAIR + h * HALF, HALF))

        def gcn_nodes(layer):
            b, g, be = (rowpar(f"L0_gnn_{n}{layer + 1}") for n in ("b", "g", "be"))
            s_prod, s_took, s_sums, s_total, s_x1, s_x1_out, s_ready = (
                sem(f"s_{n}_gcn{layer}") for n in ("prod", "took", "sums", "total", "x1", "x1_out", "ready"))
            spare_x = spare[:]
            first_root = len(roots)
            with nc.Block() as block:
                @block.tensor
                def _(pe):
                    for k, ws in quads():
                        if k >= 2:
                            pe.wait_ge(s_took, ws[0] - QUAD)
                        for q, w in enumerate(ws):
                            nc.tensor.matmul(bank[k % 2][0:WINDOW, q * DIM:(q + 1) * DIM],
                                             acc[:, w * WINDOW:(w + 1) * WINDOW], mats[:, layer, :],
                                             start=True, stop=True).then_inc(s_prod, 1)
                    for n in range(2):
                        pe.wait_ge(s_sums, n + 1)
                        nc.tensor.matmul(bank[2][0:WINDOW, n:n + 1], ones[0:WINDOW, 0:WINDOW], col[0:WINDOW, n:n + 1],
                                         start=True, stop=True).then_inc(s_total, 1)

                @block.vector
                def _(dve):
                    flat = nodes[:].rearrange("p w d -> p (w d)")
                    for w in range(WINDOWS):
                        dve.wait_ge(s_prod, min((w // QUAD + 1) * QUAD, WINDOWS))
                        v.scalar_tensor_tensor(nodes[:, w, :],
                                               bank[w // QUAD % 2][0:WINDOW, (w % QUAD) * DIM:(w % QUAD + 1) * DIM],
                                               dinv[:, w:w + 1], b, ALU.mult, ALU.add).then_inc(s_took, 1)
                    dve.wait_ge(s_took, WINDOWS)
                    v.tensor_reduce(col[0:WINDOW, 0:1], flat, AX.X, ALU.add).then_inc(s_sums, 1)
                    dve.wait_ge(s_total, 1)
                    link(dve, s_dve, v.tensor_scalar(col[0:WINDOW, 2:3], bank[2][0:WINDOW, 0:1], 1.0 / (NODES * DIM),
                                                     None, ALU.mult))
                    link(dve, s_dve, v.tensor_scalar(flat, flat, col[0:WINDOW, 2:3], None, ALU.subtract))
                    link(dve, s_dve, v.tensor_tensor(spare[:], nodes[:], nodes[:], ALU.mult))
                    v.tensor_reduce(col[0:WINDOW, 1:2], spare[:].rearrange("p w d -> p (w d)"), AX.X,
                                    ALU.add).then_inc(s_sums, 1)
                    dve.wait_ge(s_total, 2)
                    link(dve, s_dve, v.tensor_copy(col[0:WINDOW, 3:4], bank[2][0:WINDOW, 1:2]))
                    rsqrt(dve, col[0:WINDOW, 3:4], 1.0 / (NODES * DIM))
                    link(dve, s_dve, v.scalar_tensor_tensor(nodes[:], nodes[:], col[0:WINDOW, 3:4], over_windows(g),
                                                            ALU.mult, ALU.mult))
                    link(dve, s_dve, v.tensor_tensor(nodes[:], nodes[:], over_windows(be), ALU.add))
                    if layer == 0:
                        link(dve, s_dve, v.scalar_tensor_tensor(nodes[:], nodes[:], 0.0, over_features(dinv[:]),
                                                                ALU.max, ALU.mult))
                    else:
                        dve.wait_ge(s_x1, 16)
                        link(dve, s_dve, v.scalar_tensor_tensor(nodes[:], nodes[:], 0.0, spare_x, ALU.max, ALU.add))
                        dve.sem_inc(s_ready, 1)
                        dve.wait_ge(s_x1_out, 16)
                        layer_norm_relu(dve, nodes[:], spare[:], stat[:, 0, :], stat[:, 1, :])

                @block.scalar
                def _(act):
                    take_roots(act, first_root)

                if layer == 1:
                    @block.sync
                    def _(sp):
                        sp.wait_ge(s_sums, 2)
                        sp.dma_start(spare_x, by_window(A["x"])).then_inc(s_x1, 16)
                        sp.wait_ge(s_ready, 1)
                        sp.dma_start(by_window(x1_dram), nodes[:]).then_inc(s_x1_out, 16)
                        sp.wait_ge(s_x1_out, 16)

        def add_edges():
            s_prod, s_took = sem("s_prod_edges"), sem("s_took_edges")
            with nc.Block() as block:
                @block.tensor
                def _(pe):
                    for k, ws in quads():
                        if k >= 2:
                            pe.wait_ge(s_took, ws[0] - QUAD)
                        for q, w in enumerate(ws):
                            nc.tensor.matmul(bank[k % 2][0:WINDOW, q * DIM:(q + 1) * DIM],
                                             acc_edge[:, w * WINDOW:(w + 1) * WINDOW], mats[:, MATS.index("L1_gnn_ee_w2"), :],
                                             start=True, stop=True).then_inc(s_prod, 1)

                @block.vector
                def _(dve):
                    link(dve, s_dve, v.tensor_copy(spare[:], over_windows(rowpar("L1_gnn_ee_b2"))))
                    link(dve, s_dve, v.tensor_tensor(spare[:], spare[:], over_features(indeg[:]), ALU.mult))
                    link(dve, s_dve, v.tensor_tensor(nodes[:], nodes[:], spare[:], ALU.add))
                    for k, ws in quads():
                        dve.wait_ge(s_prod, ws[-1] + 1)
                        part = nodes[:, ws[0]:ws[-1] + 1, :]
                        v.tensor_tensor(part, part, bank[k % 2][0:WINDOW, 0:len(ws) * DIM]
                                        .rearrange("p (w d) -> p w d", d=DIM), ALU.add).then_inc(s_took, len(ws))
                    dve.wait_ge(s_took, WINDOWS)

        def start_layer(layer):
            s_turned, s_copied = sem(f"s_turned{layer}"), sem(f"s_copied{layer}")
            with nc.Block() as block:
                @block.sync
                def _(sp):
                    sp.dma_start(by_window(tables[layer]), nodes[:]).then_inc(s_tab[layer], 16)
                    sp.wait_ge(s_tab[layer], 16)

                @block.tensor
                def _(pe):
                    for k, ws in quads():
                        if k >= 2:
                            pe.wait_ge(s_copied, k - 1)
                        for q, w in enumerate(ws):
                            last = nc.tensor.transpose(bank[6 + k % 2][:, q * WINDOW:(q + 1) * WINDOW], nodes[:, w, :],
                                                       ident[0:WINDOW, 0:WINDOW])
                        last.then_inc(s_turned, 1)

                @block.scalar
                def _(act):
                    for k, ws in quads():
                        act.wait_ge(s_turned, k + 1)
                        nc.scalar.activation(acc[:, ws[0] * WINDOW:(ws[-1] + 1) * WINDOW],
                                             bank[6 + k % 2][:, 0:len(ws) * WINDOW], ACT.Copy).then_inc(s_copied, 1)

        def gin_mlp(n):
            s_prod, s_took = sem(f"s_prod_mlp{n}"), sem(f"s_took_mlp{n}")
            w = mats[:, MATS.index(f"L1_gnn_mlp_w{n}"), :]
            b, g, bb = (cols[:, k:k + 1] for k in range(3 * n - 3, 3 * n))
            pieces = range(0, NODES, WIDE)
            y = acc_edge
            first_root = len(roots)
            with nc.Block() as block:
                @block.tensor
                def _(pe):
                    for k, at in enumerate(pieces):
                        m = min(WIDE, NODES - at)
                        if k >= 4:
                            pe.wait_ge(s_took, k - 3)
                        nc.tensor.matmul(bank[k % 4][:, 0:m], w, acc[:, at:at + m], start=True,
                                         stop=True).then_inc(s_prod, 1)

                @block.scalar
                def _(act):
                    for k, at in enumerate(pieces):
                        m = min(WIDE, NODES - at)
                        act.wait_ge(s_prod, k + 1)
                        nc.scalar.activation(y[:, at:at + m], bank[k % 4][:, 0:m], ACT.Identity,
                                             bias=b).then_inc(s_took, 1)

            with nc.Block() as block:
                @block.vector
                def _(dve):
                    link(dve, s_dve, v.tensor_reduce(col[:, 0:1], y[:], AX.X, ALU.add))
                    link(dve, s_dve, v.tensor_scalar(col[:, 0:1], col[:, 0:1], 1.0 / NODES, None, ALU.mult))
                    link(dve, s_dve, v.tensor_scalar(y[:], y[:], col[:, 0:1], None, ALU.subtract))
                    link(dve, s_dve, v.tensor_tensor(acc[:], y[:], y[:], ALU.mult))
                    link(dve, s_dve, v.tensor_reduce(col[:, 1:2], acc[:], AX.X, ALU.add))
                    rsqrt(dve, col[:, 1:2], 1.0 / NODES)
                    link(dve, s_dve, v.tensor_tensor(col[:, 1:2], col[:, 1:2], g, ALU.mult))

                @block.scalar
                def _(act):
                    take_roots(act, first_root)

            with nc.Block() as block:
                @block.scalar
                def _(act):
                    nc.scalar.activation(acc[:], y[:], ACT.Relu, scale=col[:, 1:2], bias=bb)

        def finish():
            s_x1, s_turned, s_added, s_out = (sem(f"s_{n}_end") for n in ("x1", "turned", "added", "out"))
            with nc.Block() as block:
                @block.sync
                def _(sp):
                    sp.dma_start(nodes[:], by_window(x1_dram)).then_inc(s_x1, 16)
                    parts = 5
                    for k in range(parts):
                        ws = slice(k * WINDOWS // parts, (k + 1) * WINDOWS // parts)
                        sp.wait_ge(s_added, ws.stop)
                        sp.dma_start(by_window(out)[:, ws, :], nodes[:, ws, :]).then_inc(s_out, 16)
                    sp.wait_ge(s_out, 16 * parts)

                @block.tensor
                def _(pe):
                    for k, ws in quads():
                        if k >= 2:
                            pe.wait_ge(s_added, ws[0] - QUAD)
                        for q, w in enumerate(ws):
                            last = nc.tensor.transpose(bank[k % 2][0:WINDOW, q * DIM:(q + 1) * DIM],
                                                       acc[:, w * WINDOW:(w + 1) * WINDOW], ident[:])
                        last.then_inc(s_turned, 1)

                @block.vector
                def _(dve):
                    dve.wait_ge(s_x1, 16)
                    for k, ws in quads():
                        dve.wait_ge(s_turned, k + 1)
                        part = nodes[:, ws[0]:ws[-1] + 1, :]
                        v.tensor_tensor(part, part, bank[k % 2][0:WINDOW, 0:len(ws) * DIM]
                                        .rearrange("p (w d) -> p w d", d=DIM), ALU.add).then_inc(s_added, len(ws))

        with nc.Block() as block:
            @block.vector
            def _(dve):
                v.memset(attr_ring[:], 1.0)
                v.memset(acc_edge[:], 0.0)

        start_layer(0)
        edge_pass(0, with_edges=False)
        gcn_nodes(0)
        start_layer(1)
        edge_pass(1, with_edges=True)
        gcn_nodes(1)
        add_edges()
        start_layer(2)
        edge_pass(2, with_edges=False)
        gin_mlp(1)
        gin_mlp(2)
        finish()


def kernel(x, src, dst, edge_attr_16, **params):
    import numpy as np
    import concourse.bacc as bacc
    from concourse.bass_utils import run_bass_kernel_spmd

    x, src, dst, attr = (np.asarray(a) for a in (x, src, dst, edge_attr_16))
    pad = TILES * P - EDGES
    src_tiles = np.concatenate([src, np.zeros(pad, src.dtype)]).reshape(TILES, P)
    dst_tiles = np.concatenate([dst, np.full(pad, NOWHERE, dst.dtype)]).reshape(TILES, P)
    attr_tiles = np.concatenate([attr, np.zeros((pad, EDIM), attr.dtype)]).reshape(TILES, P, EDIM)
    arrays = {
        "x": x, "dst": dst, "edge_attr_16": attr, "src_tiles": src_tiles, "dst_tiles": dst_tiles,
        "dst_last": dst_tiles[:, P - 1][None, :],
        "attr_tiles": attr_tiles.transpose(0, 2, 1).reshape(TILES, EDIM * P),
        "L0_gnn_W1T": np.asarray(params["L0_gnn_W1"]).T, "L0_gnn_W2T": np.asarray(params["L0_gnn_W2"]).T,
        "ident": np.eye(P, dtype=np.float32),
        "node_iota": np.tile(np.arange(WINDOW, dtype=np.float32), (P, 1)),
        "step_iota": np.arange(SLOTS, dtype=np.float32).reshape(BLOCKS, P).T,
        "tile_iota": np.arange(TILES, dtype=np.float32)[None, :],
        "block_mask": np.kron(np.eye(P // EDIM), np.ones((EDIM, EDIM))).astype(np.float32),
        "fold": np.tile(np.eye(EDIM, dtype=np.float32), (P // EDIM, 1)),
    }
    for name in ROWS + COLS + MATS[2:] + ("L1_gnn_ee_w1",):
        arrays[name] = np.asarray(params[name])
    arrays = {n: np.ascontiguousarray(a) for n, a in arrays.items()}

    nc = bacc.Bacc("TRN2", target_bir_lowering=False, num_devices=1)
    A = {n: nc.dram_tensor(f"in_{n}", a.shape, mybir.dt.from_np(a.dtype), kind="ExternalInput").ap()
         for n, a in arrays.items()}
    out = nc.dram_tensor("out", (NODES, DIM), F32, kind="ExternalOutput").ap()
    program(nc, A, out)
    r = run_bass_kernel_spmd(nc, [{f"in_{n}": a for n, a in arrays.items()}], core_ids=[0])
    return r.results[0]["out"]
```

```python
from contextlib import ExitStack

import concourse.bass as bass
from concourse import mybir

F32 = mybir.dt.float32
BF16 = mybir.dt.bfloat16
I32 = mybir.dt.int32
U8 = mybir.dt.uint8
F8 = mybir.dt.float8e4
ALU = mybir.AluOpType
ACT = mybir.ActivationFunctionType
AX = mybir.AxisListType

NODES, DIM, EDGES, EDIM = 6250, 128, 200000, 16
P = 128
EPS = 1e-5
SUPER = 2 * P
TILES = -(-EDGES // SUPER)
SLICES = 2 * TILES
ALL_SLICES = SLICES + 2 * -(-NODES // (2 * P))
WINDOW = 125
WINDOWS = NODES // WINDOW
STEPS = TILES + WINDOWS - 1
NARROW = 8
NARROWS = -(-NODES // NARROW)
BSTEPS = TILES + NARROWS - 1
COLS = NARROWS * NARROW
SRCS = -(-NODES // P)
BLOCK = SRCS * NARROW
GROUP = 4
BGROUP = 8
RING = 4
ITERS = max(-(-STEPS // (2 * GROUP)), -(-BSTEPS // (2 * BGROUP)))
SLOTS = -(-(ITERS + 1) * 2 * GROUP // P) * P
BSLOTS = -(-ITERS * 2 * BGROUP // P) * P
NOWHERE = 2 * (SLOTS + BSLOTS) * WINDOW
FAR = 1.0e6
MIDDLE = BLOCK // 2
GWIN = 46
GCOLS = GWIN * NARROW
GROUPS = NARROWS // GWIN
SPLIT = 7
F8_15 = 0x57
CHUNK = 500
CHUNKS = -(-NODES // CHUNK)
HROWS = EDGES // WINDOW
HCOLS = 16
DEGWIN = 25
FCHUNKS = 10
FROWS = HROWS // FCHUNKS
BIASROW = 32
QUAD = 4
WIDE = 500
ROWS = ("L0_gnn_b1", "L0_gnn_g1", "L0_gnn_be1", "L0_gnn_b2", "L0_gnn_g2", "L0_gnn_be2",
        "L1_gnn_ee_b1", "L1_gnn_ee_g1", "L1_gnn_ee_bb1", "L1_gnn_ee_b2")
COLPARS = ("L1_gnn_mlp_b1", "L1_gnn_mlp_g1", "L1_gnn_mlp_bb1", "L1_gnn_mlp_b2", "L1_gnn_mlp_g2",
           "L1_gnn_mlp_bb2")
MATS = ("L0_gnn_W1T", "L0_gnn_W2T", "L1_gnn_ee_w2", "L1_gnn_mlp_w1", "L1_gnn_mlp_w2")
assert GROUPS * GWIN == NARROWS and WINDOWS % DEGWIN == 0


def quads():
    return [(g, range(g * QUAD, min((g + 1) * QUAD, WINDOWS))) for g in range(-(-WINDOWS // QUAD))]


def program(nc, A, out):
    whole = ExitStack()
    with whole:
        def sb(name, shape, dt=F32, scope=whole):
            return scope.enter_context(nc.sbuf_tensor(name, shape, dt))

        phase_sems = []

        def sem(name):
            phase_sems.append(nc.alloc_semaphore(name=name))
            return phase_sems[-1]

        def end_phase():
            nc.clear_and_free_semaphores(phase_sems)
            nc.all_engine_barrier()
            phase_sems.clear()

        def sems(*names):
            return [sem(f"s_{n}") for n in names]

        def dram(name, shape, dt=F32):
            return nc.dram_tensor(name, shape, dt, kind="Internal").ap()

        tables = [dram(f"table{i}", (NODES, DIM)) for i in range(3)]
        wcol_dram = dram("wcol_dram", (SLOTS // P, P), I32)
        ccol_dram = dram("ccol_dram", (BSLOTS // P, P), I32)
        attr_steps = dram("attr_steps", (SLOTS, EDIM * SUPER))
        x1_dram = dram("x1_dram", (NODES, DIM))
        counts = dram("counts", (P, (NARROWS + 1) * BLOCK), U8)

        def by_window(ap):
            return ap.rearrange("(w p) d -> p w d", p=WINDOW)

        bank = [whole.enter_context(nc.psum_tensor(f"bank{i}", [P, 512], F32)) for i in range(8)]
        ident = sb("ident", [P, P])
        ones = sb("ones", [P, P])
        node_iota = sb("node_iota", [P, CHUNK])
        acc2 = sb("acc2", [P, 2, COLS])
        acc, acc_edge = acc2[:, 0, :], acc2[:, 1, :]
        dinv = sb("dinv", [WINDOW, WINDOWS])
        indeg = sb("indeg", [WINDOW, WINDOWS])
        stat = sb("stat", [WINDOW, 2, WINDOWS])
        col = sb("col", [P, 16])
        rows = sb("rows", [P, len(ROWS), DIM])
        cols = sb("cols", [P, len(COLPARS)])
        mats = sb("mats", [P, len(MATS), DIM])
        ew1 = sb("ew1", [EDIM, DIM])
        edge_w = sb("edge_w", [BIASROW + 1, DIM])
        flags = sb("flags", [1, 2], I32)
        zeros_bf = sb("zeros_bf", [P, 4 * WINDOW], BF16)
        general_shift = sb("general_shift", [P, CHUNKS])

        def rowpar(name, parts=WINDOW):
            return rows[0:parts, ROWS.index(name), :]

        def over_windows(ap):
            return ap.unsqueeze(1).broadcast_to([WINDOW, WINDOWS, DIM])

        def over_features(ap):
            return ap.unsqueeze(2).broadcast_to([WINDOW, WINDOWS, DIM])

        s_dve, s_var, s_root = (whole.enter_context(nc.semaphore(n)) for n in ("s_dve", "s_var", "s_root"))
        ended = {}

        def link(dve, ins, chain=s_dve):
            ended[chain.name] = ended.get(chain.name, 0) + 1
            ins.then_inc(chain, 1)
            dve.wait_ge(chain, ended[chain.name])

        v = nc.vector
        roots = []

        def rsqrt(dve, ap, scale, eps=EPS):
            v.tensor_scalar(ap, ap, scale, eps, ALU.mult, ALU.add).then_inc(s_var, 1)
            roots.append(ap)
            dve.wait_ge(s_root, len(roots))
            link(dve, v.reciprocal(ap, ap))

        def take_roots(act, first):
            for n in range(first, len(roots)):
                act.wait_ge(s_var, n + 1)
                nc.scalar.activation(roots[n], roots[n], ACT.Sqrt).then_inc(s_root, 1)

        def center(dve, t, tmp, sums, rstd):
            link(dve, v.tensor_reduce(sums, t, AX.X, ALU.add))
            link(dve, v.tensor_scalar(sums, sums, 1.0 / DIM, None, ALU.mult))
            link(dve, v.tensor_tensor(t, t, over_features(sums), ALU.subtract))
            link(dve, v.tensor_tensor(tmp, t, t, ALU.mult))
            link(dve, v.tensor_reduce(rstd, tmp, AX.X, ALU.add))
            rsqrt(dve, rstd, 1.0 / DIM)

        def relu_times(dve, t, factor):
            link(dve, v.scalar_tensor_tensor(t, t, 0.0, over_features(factor), ALU.max, ALU.mult))

        def split_windows(dve, dst, win, rest, whole_win, chain=s_dve):
            link(dve, v.tensor_scalar(win, dst, 0.5, 1.0 / WINDOW, ALU.add, ALU.mult), chain)
            link(dve, v.tensor_copy(whole_win, win), chain)
            link(dve, v.tensor_scalar(win, whole_win, -1.0, None, ALU.add), chain)
            link(dve, v.scalar_tensor_tensor(rest, win, -float(WINDOW), dst, ALU.mult, ALU.add), chain)
            link(dve, v.scalar_tensor_tensor(win, rest, float(WINDOW), win, ALU.is_ge, ALU.add), chain)
            link(dve, v.scalar_tensor_tensor(rest, win, -float(WINDOW), dst, ALU.mult, ALU.add), chain)

        first = ExitStack()
        wcol_row = sb("wcol_row", [1, GROUP + SLOTS], I32, first)
        ccol_row = sb("ccol_row", [1, BSLOTS], I32, first)
        src_steps = sb("src_steps", [P, SLOTS, 2], I32, first)
        dst_steps = sb("dst_steps", [P, SLOTS, 2], F32, first)
        low_steps = sb("low_steps", [P, BSLOTS, 2], F32, first)
        key_steps = sb("key_steps", [P, BSLOTS, 2], F32, first)
        keep_steps = sb("keep_steps", [P, BSLOTS], F32, first)

        prelude = ExitStack()
        nodes = sb("nodes", [WINDOW, WINDOWS, DIM], F32, prelude)
        spare = sb("spare", [WINDOW, WINDOWS, DIM], F32, prelude)
        step_iota = sb("step_iota", [P, BSLOTS // P], F32, prelude)
        node_id = sb("node_id", [WINDOW, WINDOWS], F32, prelude)
        lookup = sb("lookup", [WINDOW, WINDOWS + 1], F32, prelude)
        next_node = sb("next_node", [WINDOW, 2, WINDOW], F32, prelude)
        tile_of = sb("tile_of", [WINDOW, WINDOWS], F32, prelude)
        tile_of_int = sb("tile_of_int", [WINDOW, WINDOWS], I32, prelude)

        dst_all = acc[0:WINDOW, 0:HROWS].bitcast(I32)
        dst_next = acc[0:WINDOW, HROWS:2 * HROWS].bitcast(I32)
        falls = acc[0:WINDOW, 2 * HROWS:3 * HROWS]
        one_row = spare[0:1].rearrange("p w d -> p (w d)")
        last_dst, end_wide, end_rest, end_narrow, tile_iota = (
            one_row[:, k * TILES:(k + 1) * TILES] for k in range(5))
        last_int, end_int = (acc_edge[0:1, k * TILES:(k + 1) * TILES].bitcast(I32) for k in range(2))
        s_const, s_par, s_x, s_dst, s_falls, s_falls_all = sems("const", "par", "x", "dst", "falls", "falls_all")
        with nc.Block() as block:
            @block.sync
            def _(sp):
                sp.dma_start(last_int, A["dst_last"]).then_inc(s_const, 16)
                sp.dma_start(tile_iota, A["tile_iota"]).then_inc(s_const, 16)
                sp.dma_start(dst_all, A["dst"].rearrange("(p c) -> p c", p=WINDOW)).then_inc(s_dst, 16)
                sp.dma_start(dst_next, A["dst_next"].rearrange("(p c) -> p c", p=WINDOW)).then_inc(s_dst, 16)
                for n, t in (("ident", ident), ("node_iota", node_iota), ("step_iota", step_iota),
                             ("node_id", node_id), ("next_node", next_node), ("general_shift", general_shift)):
                    sp.dma_start(t[:], A[n]).then_inc(s_par, 16)
                for k, n in enumerate(ROWS):
                    sp.dma_start(rows[:, k, :], A[n].unsqueeze(0).broadcast_to([P, DIM])).then_inc(s_par, 16)
                for k, n in enumerate(MATS):
                    sp.dma_start(mats[:, k, :], A[n]).then_inc(s_par, 16)
                sp.dma_start(ew1[:], A["L1_gnn_ee_w1"]).then_inc(s_par, 16)
                for k, n in enumerate(COLPARS):
                    sp.dma_start(cols[:, k:k + 1], A[n].unsqueeze(1)).then_inc(s_par, 16)
                sp.wait_ge(s_par, 16 * (6 + len(ROWS) + len(MATS) + 1 + len(COLPARS)))

            @block.vector
            def _(dve):
                v.memset(ones[:], 1.0)
                v.memset(edge_w[:], 0.0)
                link(dve, v.memset(zeros_bf[:], 0.0))
                dve.wait_ge(s_const, 32)
                link(dve, v.tensor_copy(last_dst, last_int))
                link(dve, v.tensor_scalar(last_dst, last_dst, float(NODES - 1), None, ALU.min))
                split_windows(dve, last_dst, end_wide, end_rest, end_int)
                link(dve, v.tensor_tensor(end_wide, end_wide, tile_iota, ALU.add))
                link(dve, v.memset(end_wide[:, TILES - 1:TILES], float(STEPS - 1)))
                link(dve, v.tensor_scalar(end_int, last_int, NARROW.bit_length() - 1, None, ALU.arith_shift_right))
                link(dve, v.tensor_copy(end_narrow, end_int))
                link(dve, v.tensor_tensor(end_narrow, end_narrow, tile_iota, ALU.add))
                link(dve, v.memset(end_narrow[:, TILES - 1:TILES], float(BSTEPS - 1)))
                dve.wait_ge(s_dst, 32)
                link(dve, v.tensor_tensor(falls, dst_all, dst_next, ALU.is_gt))
                v.tensor_reduce(col[0:WINDOW, 0:1], falls, AX.X, ALU.add).then_inc(s_falls, 1)
                dve.wait_ge(s_falls_all, 1)
                v.tensor_scalar(flags[:, 0:1], bank[0][0:1, 0:1], 0.0, None, ALU.is_equal)

            @block.tensor
            def _(pe):
                pe.wait_ge(s_falls, 1)
                nc.tensor.matmul(bank[0][0:1, 0:1], col[0:WINDOW, 0:1], ones[0:WINDOW, 0:1], start=True,
                                 stop=True).then_inc(s_falls_all, 1)

        last_all, wide_all, narrow_all = (acc[:, k * TILES:(k + 1) * TILES] for k in range(3))
        compared = acc[:, 3 * TILES:4 * TILES]
        plan = ExitStack()
        WB, CB = SLOTS // P, BSLOTS // P
        t_wide = sb("t_wide", [P, WB], F32, plan)
        t_narrow = sb("t_narrow", [P, 3, CB], F32, plan)
        step_next = sb("step_next", [P, CB], F32, plan)
        step_last = sb("step_last", [P, CB], F32, plan)
        keep = sb("keep", [P, CB], F32, plan)
        w_wide = sb("w_wide", [P, WB], F32, plan)
        w_narrow = sb("w_narrow", [P, CB], F32, plan)
        wcol = sb("wcol", [P, WB], F32, plan)
        ccol = sb("ccol", [P, CB], F32, plan)
        wide_idx = sb("wide_idx", [P, WB], I32, plan)
        narrow_idx = sb("narrow_idx", [P, CB], I32, plan)
        col_int = sb("col_int", [CB, 2, P], I32, plan)
        deg_rows = acc2[0:WINDOW].rearrange("p a n -> p (a n)")[:, 4 * TILES:4 * TILES + DEGWIN * SUPER]\
            .rearrange("p (w e) -> p w e", e=SUPER)
        x_sums, x_rstd = stat[:, 0, :], stat[:, 1, :]
        s_all, s_tiles, s_degrows, s_degused, s_shift, s_deg, s_wide, s_wt, s_wturn, s_wrow, s_back = sems(
            "all", "tiles", "degrows", "degused", "shift", "deg", "wide", "wt", "wturn", "wrow", "back")
        s_idx_ready = sem("s_idx_ready")
        pieces = [(k, min(512, TILES - k)) for k in range(0, TILES, 512)]
        assert len(pieces) == 2
        with nc.Block() as block:
            @block.sync
            def _(sp):
                sp.dma_start(nodes[:], by_window(A["x"])).then_inc(s_x, 16)
                for n, (r, t, blocks) in enumerate(((wcol_dram, 0, WB), (ccol_dram, 1, CB))):
                    sp.wait_ge(s_wrow, n + 1)
                    sp.dma_start(r, col_int[0:blocks, t, :]).then_inc(s_back, 16)
                sp.wait_ge(s_back, 32)
                sp.dma_start(wcol_row[:, GROUP:], wcol_dram.rearrange("j p -> (j p)").unsqueeze(0)).then_inc(s_back, 16)
                sp.dma_start(ccol_row[:], ccol_dram.rearrange("j p -> (j p)").unsqueeze(0)).then_inc(s_back, 16)
                sp.wait_ge(s_back, 64)

            @block.tensor
            def _(pe):
                for n, row in enumerate((last_dst, end_wide, end_narrow)):
                    for m, (k, size) in enumerate(pieces):
                        nc.tensor.matmul(bank[2 * n + m][:, 0:size], ones[0:1, :], row[:, k:k + size], start=True,
                                         stop=True).then_inc(s_all, 1)
                for n, (c, blocks) in enumerate(((wcol, WB), (ccol, CB))):
                    pe.wait_ge(s_wt, n + 1)
                    nc.tensor.transpose(bank[6][0:blocks, n * P:(n + 1) * P], c[:], ident[:]).then_inc(s_wturn, 1)
                pe.wait_ge(s_shift, 1)
                nc.tensor.matmul(bank[7][0:WINDOW, 0:WINDOWS], next_node[:, 0, :], lookup[:, 0:WINDOWS],
                                 start=True, stop=False)
                nc.tensor.matmul(bank[7][0:WINDOW, 0:WINDOWS], next_node[:, 1, :], lookup[:, 1:WINDOWS + 1],
                                 start=False, stop=True).then_inc(s_deg, 1)

            @block.vector
            def _(dve):
                for n, t in enumerate((last_all, wide_all, narrow_all)):
                    for m, (k, size) in enumerate(pieces):
                        dve.wait_ge(s_all, 2 * n + m + 1)
                        v.tensor_copy(t[:, k:k + size], bank[2 * n + m][:, 0:size])
                v.tensor_scalar(step_last[:], step_iota[:], -1.0, None, ALU.add)
                link(dve, v.tensor_scalar(step_next[:], step_iota[:], 1.0, None, ALU.add))

                def count_tiles(table, parts, x, into):
                    link(dve, v.tensor_scalar(compared[0:parts], table[0:parts], x, None, ALU.is_lt, ALU.add,
                                              accum_out=into))

                for w in range(WINDOWS):
                    count_tiles(last_all, WINDOW, node_id[:, w:w + 1], tile_of[:, w:w + 1])
                link(dve, v.tensor_scalar(tile_of[:], tile_of[:], float(TILES - 1), None, ALU.min))
                v.tensor_copy(tile_of_int[:], tile_of[:]).then_inc(s_tiles, 1)
                for j in range(WB):
                    count_tiles(wide_all, P, step_iota[:, j:j + 1], t_wide[:, j:j + 1])
                link(dve, v.tensor_scalar(t_wide[:], t_wide[:], float(TILES - 1), None, ALU.min))
                link(dve, v.tensor_copy(wide_idx[:], t_wide[:]))
                link(dve, v.tensor_tensor(w_wide[:], step_iota[:, 0:WB], t_wide[:], ALU.subtract))
                link(dve, v.tensor_scalar(w_wide[:], w_wide[:], float(WINDOW), None, ALU.mult))
                v.tensor_scalar(wcol[:], w_wide[:], float((WINDOWS - 1) * WINDOW), None, ALU.min).then_inc(s_wt, 1)
                for j in range(CB):
                    count_tiles(narrow_all, P, step_iota[:, j:j + 1], t_narrow[:, 0, j:j + 1])
                    count_tiles(narrow_all, P, step_next[:, j:j + 1], t_narrow[:, 1, j:j + 1])
                    count_tiles(narrow_all, P, step_last[:, j:j + 1], t_narrow[:, 2, j:j + 1])
                link(dve, v.tensor_scalar(t_narrow[:], t_narrow[:], float(TILES - 1), None, ALU.min))
                v.tensor_copy(narrow_idx[:], t_narrow[:, 0, :]).then_inc(s_idx_ready, 1)
                link(dve, v.tensor_tensor(w_narrow[:], step_iota[:], t_narrow[:, 0, :], ALU.subtract))
                link(dve, v.tensor_tensor(keep[:], t_narrow[:, 0, :], t_narrow[:, 2, :], ALU.not_equal))
                link(dve, v.tensor_tensor(ccol[:], t_narrow[:, 1, :], t_narrow[:, 0, :], ALU.not_equal))
                link(dve, v.scalar_tensor_tensor(ccol[:], ccol[:], float(NARROWS), w_narrow[:], ALU.mult, ALU.add))
                link(dve, v.tensor_scalar(ccol[:], ccol[:], float(NARROWS), float(BLOCK), ALU.min, ALU.mult))
                v.tensor_scalar(w_narrow[:], w_narrow[:], float(NARROW), None, ALU.mult).then_inc(s_wt, 1)
                v.memset(wcol_row[:, 0:GROUP], 0)
                for n, blocks in ((0, WB), (1, CB)):
                    dve.wait_ge(s_wturn, n + 1)
                    if n == 0:
                        dve.wait_ge(s_wturn, 2)
                    v.tensor_copy(col_int[0:blocks, n, :], bank[6][0:blocks, n * P:(n + 1) * P]).then_inc(s_wrow, 1)
                dve.wait_ge(s_x, 16)
                center(dve, nodes[:], spare[:], x_sums, x_rstd)
                for k in range(WINDOWS // DEGWIN):
                    ws = slice(k * DEGWIN, (k + 1) * DEGWIN)
                    dve.wait_ge(s_degrows, 16 * DEGWIN * (k + 1))
                    link(dve, v.tensor_tensor(deg_rows, deg_rows.bitcast(I32), node_id[:, ws].unsqueeze(2)
                                              .broadcast_to([WINDOW, DEGWIN, SUPER]), ALU.is_lt))
                    v.tensor_reduce(lookup[:, ws], deg_rows, AX.X, ALU.add).then_inc(s_degused, 1)
                dve.wait_ge(s_degused, WINDOWS // DEGWIN)
                link(dve, v.memset(lookup[:, WINDOWS:], float(EDGES)))
                v.scalar_tensor_tensor(lookup[:, 0:WINDOWS], tile_of[:], float(SUPER), lookup[:, 0:WINDOWS],
                                       ALU.mult, ALU.add).then_inc(s_shift, 1)
                dve.wait_ge(s_deg, 1)
                link(dve, v.tensor_copy(indeg[:], bank[7][0:WINDOW, 0:WINDOWS]))

            @block.scalar
            def _(act):
                take_roots(act, 0)

            @block.gpsimd
            def _(pool):
                pool.wait_ge(s_tiles, 1)
                for k in range(WINDOWS // DEGWIN):
                    if k:
                        pool.wait_ge(s_degused, k)
                    for w in range(DEGWIN):
                        at = tile_of_int[:, k * DEGWIN + w:k * DEGWIN + w + 1]
                        nc.gpsimd.indirect_dma_start(
                            deg_rows[:, w, :].bitcast(I32), None, A["dst_tiles"],
                            bass.IndirectOffsetOnAxis(ap=at, axis=0)).then_inc(s_degrows, 16)
                pool.wait_ge(s_degrows, 16 * WINDOWS)

        arena = acc2[:].rearrange("p a n -> p (a n)")
        RB = 3

        def arena_part(at, shape):
            size = 1
            for n in shape:
                size *= n
            t = arena[:, at:at + size]
            return t.rearrange("p (a b c) -> p a b c", a=shape[0], b=shape[1]), at + size

        got_rows, at = arena_part(0, (RB, 2, SUPER))
        got_rows = got_rows.bitcast(I32)
        made_rows, at = arena_part(at, (RB, 2, SUPER))
        bits_rows, at = arena_part(at, (1, 2, SUPER))
        bits_rows = bits_rows.bitcast(I32)
        keep_rows, at = arena_part(at, (RB, 1, P))
        keep_rows = keep_rows[:, :, 0, :]
        attr_buf = [arena[:, at + k * EDIM * SUPER:at + (k + 1) * EDIM * SUPER] for k in range(2)]
        assert at + 2 * EDIM * SUPER <= 2 * COLS
        blocks = [("wide", j) for j in range(WB)] + [("narrow", j) for j in range(CB)]
        s_got = [sem(f"s_got{k}") for k in range(RB)]
        s_attr, s_attr_out = ([sem(f"s_{n}{k}") for k in range(2)] for n in ("attr", "attr_out"))
        s_made, s_rowturn, s_rowcopy = sems("made", "rowturn", "rowcopy")
        with nc.Block() as block:
            @block.gpsimd
            def _(pool):
                for n, (kind, j) in enumerate(blocks):
                    idx_all = wide_idx if kind == "wide" else narrow_idx
                    if n >= RB:
                        pool.wait_ge(s_made, n - RB + 1)
                    for m, a in enumerate(("src_tiles", "dst_tiles")):
                        nc.gpsimd.indirect_dma_start(
                            got_rows[:, n % RB, m, :], None, A[a],
                            bass.IndirectOffsetOnAxis(ap=idx_all[:, j:j + 1], axis=0)).then_inc(s_got[n % RB], 16)
                for j in range(WB):
                    if j >= 2:
                        pool.wait_ge(s_attr_out[j % 2], 16 * (j // 2))
                    nc.gpsimd.indirect_dma_start(
                        attr_buf[j % 2], None, A["attr_tiles"],
                        bass.IndirectOffsetOnAxis(ap=wide_idx[:, j:j + 1], axis=0)).then_inc(s_attr[j % 2], 16)

            @block.sync
            def _(sp):
                for j in range(WB):
                    sp.wait_ge(s_attr[j % 2], 16 * (j // 2 + 1))
                    sp.dma_start(attr_steps[j * P:(j + 1) * P, :], attr_buf[j % 2]).then_inc(s_attr_out[j % 2], 16)
                for k in range(2):
                    sp.wait_ge(s_attr_out[k], 16 * len(range(k, WB, 2)))

            @block.vector
            def _(dve):
                for n, (kind, j) in enumerate(blocks):
                    b = n % RB
                    src, dst = got_rows[:, b, 0, :], got_rows[:, b, 1, :]
                    first_out, second_out = made_rows[:, b, 0, :], made_rows[:, b, 1, :]
                    dve.wait_ge(s_got[b], 32 * (n // RB + 1))
                    if n >= RB:
                        dve.wait_ge(s_rowturn, n - RB + 1)
                    if kind == "wide":
                        v.tensor_copy(first_out, src)
                        v.tensor_scalar(second_out, dst, w_wide[:, j:j + 1], None, ALU.subtract).then_inc(s_made, 1)
                        continue
                    low, high = bits_rows[:, 0, 0, :], bits_rows[:, 0, 1, :]
                    dve.wait_ge(s_made, n)
                    link(dve, v.tensor_scalar(low, src, P - 1, None, ALU.bitwise_and))
                    link(dve, v.tensor_scalar(high, src, P.bit_length() - 1, None, ALU.arith_shift_right))
                    link(dve, v.tensor_scalar(second_out, dst, w_narrow[:, j:j + 1], None, ALU.subtract))
                    link(dve, v.scalar_tensor_tensor(first_out, second_out, -(NARROW - 1.0), second_out, ALU.add, ALU.mult))
                    link(dve, v.tensor_scalar(first_out, first_out, 0.0, FAR, ALU.is_gt, ALU.mult))
                    link(dve, v.scalar_tensor_tensor(second_out, second_out, -float(MIDDLE), first_out, ALU.add, ALU.add))
                    link(dve, v.scalar_tensor_tensor(second_out, high, float(NARROW), second_out, ALU.mult, ALU.add))
                    v.tensor_copy(keep_rows[:, b, :], keep[:, j:j + 1].broadcast_to([P, P]))
                    v.tensor_copy(first_out, low).then_inc(s_made, 1)

            @block.tensor
            def _(pe):
                for n in range(len(blocks)):
                    pe.wait_ge(s_made, n + 1)
                    if n >= 2:
                        pe.wait_ge(s_rowcopy, 2 * (n - 1))
                    for m in range(2):
                        for c in range(2):
                            last = nc.tensor.transpose(bank[n % 2][:, (2 * m + c) * P:(2 * m + c + 1) * P],
                                                       made_rows[:, n % RB, m, c * P:(c + 1) * P], ident[:])
                    if blocks[n][0] == "narrow":
                        last = nc.tensor.transpose(bank[2 + n % 2][:, 0:P], keep_rows[:, n % RB, :], ident[:])
                    last.then_inc(s_rowturn, 1)

            @block.scalar
            def _(act):
                for n, (kind, j) in enumerate(blocks):
                    act.wait_ge(s_rowturn, n + 1)
                    if kind == "narrow":
                        nc.scalar.activation(keep_steps[:, j * P:(j + 1) * P], bank[2 + n % 2][:, 0:P], ACT.Copy)
                    for m, steps in enumerate((src_steps, dst_steps) if kind == "wide" else (low_steps, key_steps)):
                        nc.scalar.activation(steps[:, j * P:(j + 1) * P, :].rearrange("p s c -> p c s"),
                                             bank[n % 2][:, 2 * m * P:2 * (m + 1) * P].rearrange("p (c s) -> p c s", c=2),
                                             ACT.Copy).then_inc(s_rowcopy, 1)
        plan.close()

        tail = ExitStack()
        feat = [sb(f"feat{k}", [WINDOW, FROWS, EDIM], F32, tail) for k in range(2)]
        featsum = sb("featsum", [WINDOW, FCHUNKS, EDIM], F32, tail)
        featmean = sb("featmean", [WINDOW, EDIM], F32, tail)
        block_mask = sb("block_mask", [P, P], F32, tail)
        fold = sb("fold", [P, EDIM], F32, tail)
        gram = sb("gram", [P, P], F32, tail)
        gram_fold = sb("gram_fold", [P, EDIM], F32, tail)
        cov = sb("cov", [EDIM, EDIM], F32, tail)
        cov_w = sb("cov_w", [EDIM, DIM], F32, tail)
        mean_col = sb("mean_col", [EDIM, 1], F32, tail)
        mean_cols = sb("mean_cols", [EDIM, P], F32, tail)
        scale_rows = sb("scale_rows", [BIASROW + 1, DIM], F32, tail)
        shift_rows = sb("shift_rows", [BIASROW + 1, DIM], F32, tail)
        PACK = P // EDIM
        GRAMS = FROWS // PACK
        attr_by_part = A["edge_attr_16"].rearrange("(p c r) f -> p c r f", p=WINDOW, c=FCHUNKS)
        s_feat = [sem(f"s_feat{k}") for k in range(2)]
        s_sum, s_cent, s_gram, s_gmat, s_gval, s_mask = sems("sum", "cent", "gram", "gmat", "gval", "mask")
        first_root = len(roots)
        with nc.Block() as block:
            @block.sync
            def _(sp):
                sp.dma_start(block_mask[:], A["block_mask"]).then_inc(s_mask, 16)
                sp.dma_start(fold[:], A["fold"]).then_inc(s_mask, 16)
                for n in range(2 * FCHUNKS):
                    if 2 <= n < FCHUNKS + 2:
                        sp.wait_ge(s_sum, n - 1)
                    elif n >= FCHUNKS + 2:
                        sp.wait_ge(s_gram, n - 1 - FCHUNKS)
                    sp.dma_start(feat[n % 2][:], attr_by_part[:, n % FCHUNKS]).then_inc(s_feat[n % 2], 16)
                sp.wait_ge(s_mask, 32)

            @block.vector
            def _(dve):
                for n in range(FCHUNKS):
                    dve.wait_ge(s_feat[n % 2], 16 * (n // 2 + 1))
                    v.tensor_reduce(featsum[:, n, :], feat[n % 2][:].rearrange("p r f -> p f r"), AX.X,
                                    ALU.add).then_inc(s_sum, 1)
                dve.wait_ge(s_sum, FCHUNKS)
                link(dve, v.tensor_reduce(featmean[:], featsum[:].rearrange("p c f -> p f c"), AX.X, ALU.add))
                v.tensor_scalar(featmean[:], featmean[:], 1.0 / EDGES, None, ALU.mult).then_inc(s_gval, 1)
                dve.wait_ge(s_gmat, 2)
                link(dve, v.tensor_copy(featmean[:], bank[1][0:WINDOW, 0:EDIM]))
                link(dve, v.tensor_copy(mean_col[:], bank[2][0:EDIM, 0:1]))
                v.tensor_copy(mean_cols[:], mean_col[:].broadcast_to([EDIM, P])).then_inc(s_gval, 1)
                for n in range(FCHUNKS, 2 * FCHUNKS):
                    dve.wait_ge(s_feat[n % 2], 16 * (n // 2 + 1))
                    v.tensor_tensor(feat[n % 2][:], feat[n % 2][:],
                                    featmean[:].unsqueeze(1).broadcast_to([WINDOW, FROWS, EDIM]),
                                    ALU.subtract).then_inc(s_cent, 1)
                dve.wait_ge(s_gram, FCHUNKS)
                dve.wait_ge(s_mask, 32)
                v.tensor_tensor(gram[:], bank[0][:, 0:P], block_mask[:], ALU.mult).then_inc(s_gval, 1)
                dve.wait_ge(s_gmat, 3)
                v.tensor_copy(gram_fold[:], bank[1][:, 0:EDIM]).then_inc(s_gval, 1)
                dve.wait_ge(s_gmat, 4)
                v.tensor_scalar(cov[:], bank[2][0:EDIM, 0:EDIM], 1.0 / EDGES, None, ALU.mult).then_inc(s_gval, 1)
                dve.wait_ge(s_gmat, 5)
                v.tensor_tensor(cov_w[:], bank[1][0:EDIM, 0:DIM], ew1[:], ALU.mult).then_inc(s_gval, 1)
                dve.wait_ge(s_gmat, 7)
                r = slice(0, BIASROW + 1)
                b1, g1, bb1 = (rowpar(n, BIASROW + 1) for n in ("L1_gnn_ee_b1", "L1_gnn_ee_g1", "L1_gnn_ee_bb1"))
                link(dve, v.tensor_copy(scale_rows[:], bank[2][r, 0:DIM]))
                rsqrt(dve, scale_rows[:], 1.0)
                link(dve, v.tensor_tensor(scale_rows[:], scale_rows[:], g1, ALU.mult))
                link(dve, v.tensor_tensor(shift_rows[:], bank[3][r, 0:DIM], b1, ALU.add))
                link(dve, v.tensor_tensor(shift_rows[:], b1, shift_rows[:], ALU.subtract))
                link(dve, v.tensor_tensor(shift_rows[:], shift_rows[:], scale_rows[:], ALU.mult))
                link(dve, v.tensor_tensor(shift_rows[:], shift_rows[:], bb1, ALU.add))
                link(dve, v.tensor_tensor(edge_w[0:EDIM, :], ew1[:], scale_rows[0:EDIM, :], ALU.mult))
                link(dve, v.tensor_copy(edge_w[BIASROW:BIASROW + 1, :], shift_rows[BIASROW:BIASROW + 1, :]))

            @block.scalar
            def _(act):
                take_roots(act, first_root)

            @block.tensor
            def _(pe):
                pe.wait_ge(s_gval, 1)
                nc.tensor.matmul(bank[1][0:WINDOW, 0:EDIM], ones[0:WINDOW, 0:WINDOW], featmean[:], start=True,
                                 stop=True).then_inc(s_gmat, 1)
                nc.tensor.matmul(bank[2][0:EDIM, 0:1], featmean[:], ones[0:WINDOW, 0:1], start=True,
                                 stop=True).then_inc(s_gmat, 1)
                for n in range(FCHUNKS):
                    pe.wait_ge(s_cent, n + 1)
                    for k in range(GRAMS):
                        part = feat[n % 2][:, k * PACK:(k + 1) * PACK, :].rearrange("p r f -> p (r f)")
                        last = nc.tensor.matmul(bank[0][:, 0:P], part, part, start=(n == k == 0),
                                                stop=(n == FCHUNKS - 1 and k == GRAMS - 1))
                    last.then_inc(s_gram, 1)
                pe.wait_ge(s_gval, 3)
                nc.tensor.matmul(bank[1][:, 0:EDIM], gram[:], fold[:], start=True, stop=True).then_inc(s_gmat, 1)
                pe.wait_ge(s_gval, 4)
                nc.tensor.matmul(bank[2][0:EDIM, 0:EDIM], fold[:], gram_fold[:], start=True,
                                 stop=True).then_inc(s_gmat, 1)
                pe.wait_ge(s_gval, 5)
                nc.tensor.matmul(bank[1][0:EDIM, 0:DIM], cov[:], ew1[:], start=True, stop=True).then_inc(s_gmat, 1)
                pe.wait_ge(s_gval, 6)
                nc.tensor.matmul(bank[2][:, 0:DIM], ones[0:EDIM, :], cov_w[:], start=True, stop=True).then_inc(s_gmat, 1)
                nc.tensor.matmul(bank[3][:, 0:DIM], mean_cols[:], ew1[:], start=True, stop=True).then_inc(s_gmat, 1)
        tail.close()

        tail = ExitStack()
        hot_node = sb("hot_node", [WINDOW, 2, HCOLS, WINDOW], BF16, tail)
        hot_win = sb("hot_win", [WINDOW, 2, HCOLS, WINDOWS], BF16, tail)
        node_of = sb("node_of", [WINDOW, HROWS], BF16, tail)
        win_of = sb("win_of", [WINDOW, HROWS], BF16, tail)
        iota_bf = sb("iota_bf", [WINDOW, WINDOW], BF16, tail)
        fdst, fwin, frest, iwin = (arena[0:WINDOW, k * HROWS:(k + 1) * HROWS] for k in range(4))
        iwin = iwin.bitcast(I32)
        s_dall, s_hist_end, s_gsplit = sems("dall", "hist_end", "gsplit")
        s_hot, s_hist = ([sem(f"s_{n}{h}") for h in range(2)] for n in ("hot", "hist"))

        def is_sorted(eng):
            return eng.value_load(flags[0:1, 0:1], min_val=0, max_val=1)

        def counts_fit(eng):
            return eng.value_load(flags[0:1, 1:2], min_val=0, max_val=1)

        with nc.Block() as block:
            @block.sync
            def _(sp):
                with sp.If(is_sorted(sp) < 1):
                    sp.dma_start(iwin, A["dst"].rearrange("(p c) -> p c", p=WINDOW)).then_inc(s_dall, 16)
                    sp.wait_ge(s_dall, 16)

            @block.vector
            def _(dve):
                with dve.If(is_sorted(dve) < 1):
                    g = s_gsplit
                    dve.wait_ge(s_dall, 16)
                    link(dve, v.tensor_copy(iota_bf[:], node_iota[0:WINDOW, 0:WINDOW]), g)
                    link(dve, v.tensor_copy(fdst, iwin), g)
                    split_windows(dve, fdst, fwin, frest, iwin, g)
                    link(dve, v.tensor_copy(win_of[:], fwin), g)
                    link(dve, v.tensor_copy(node_of[:], frest), g)
                    with dve.Fori(0, HROWS // HCOLS // 2) as i:
                        for h in range(2):
                            dve.wait_ge(s_hist[h], i + 1)
                            at = bass.ds(i * (2 * HCOLS) + h * HCOLS, HCOLS)
                            v.tensor_tensor(hot_node[:, h],
                                            iota_bf[:].unsqueeze(1).broadcast_to([WINDOW, HCOLS, WINDOW]),
                                            node_of[:, at].unsqueeze(2).broadcast_to([WINDOW, HCOLS, WINDOW]),
                                            ALU.is_equal).then_inc(s_hot[h], 1)
                            v.tensor_tensor(hot_win[:, h],
                                            iota_bf[:, 0:WINDOWS].unsqueeze(1).broadcast_to([WINDOW, HCOLS, WINDOWS]),
                                            win_of[:, at].unsqueeze(2).broadcast_to([WINDOW, HCOLS, WINDOWS]),
                                            ALU.is_equal).then_inc(s_hot[h], 1)
                    dve.wait_ge(s_hist_end, 1)
                    link(dve, v.tensor_copy(indeg[:], bank[0][0:WINDOW, 0:WINDOWS]), g)

            @block.tensor
            def _(pe):
                with pe.If(is_sorted(pe) < 1):
                    degrees = bank[0][0:WINDOW, 0:WINDOWS]
                    for s in s_hist:
                        pe.sem_inc(s, 1)
                    nc.tensor.matmul(degrees, zeros_bf[0:WINDOW, 0:WINDOW], zeros_bf[0:WINDOW, 0:WINDOWS], start=True,
                                     stop=False)
                    with pe.Fori(0, HROWS // HCOLS // 2) as i:
                        for h in range(2):
                            pe.wait_ge(s_hot[h], i * 2 + 2)
                            for c in range(HCOLS):
                                last = nc.tensor.matmul(degrees, hot_node[:, h, c, :], hot_win[:, h, c, :],
                                                        start=False, stop=False)
                            last.then_inc(s_hist[h], 1)
                    nc.tensor.matmul(degrees, zeros_bf[0:WINDOW, 0:WINDOW], zeros_bf[0:WINDOW, 0:WINDOWS], start=False,
                                     stop=True).then_inc(s_hist_end, 1)
        tail.close()

        def start_layer(layer, nodes):
            s_tab, s_turned, s_copied = sems(f"tab{layer}", f"turned{layer}", f"copied{layer}")
            with nc.Block() as block:
                @block.sync
                def _(sp):
                    sp.dma_start(by_window(tables[layer]), nodes[:]).then_inc(s_tab, 16)
                    sp.wait_ge(s_tab, 16)

                @block.tensor
                def _(pe):
                    for k, ws in quads():
                        if k >= 2:
                            pe.wait_ge(s_copied, k - 1)
                        for q, w in enumerate(ws):
                            last = nc.tensor.transpose(bank[6 + k % 2][:, q * WINDOW:(q + 1) * WINDOW], nodes[:, w, :],
                                                       ident[0:WINDOW, 0:WINDOW])
                        last.then_inc(s_turned, 1)

                @block.scalar
                def _(act):
                    for k, ws in quads():
                        act.wait_ge(s_turned, k + 1)
                        nc.scalar.activation(acc[:, ws[0] * WINDOW:(ws[-1] + 1) * WINDOW],
                                             bank[6 + k % 2][:, 0:len(ws) * WINDOW], ACT.Copy).then_inc(s_copied, 1)

                @block.vector
                def _(dve):
                    if layer == 0:
                        v.memset(acc_edge, 0.0)
                    v.memset(acc[:, NODES:], 0.0)

        first_root = len(roots)
        with nc.Block() as block:
            @block.vector
            def _(dve):
                link(dve, v.tensor_scalar(dinv[:], indeg[:], 1.0, None, ALU.add))
                rsqrt(dve, dinv[:], 1.0, 0.0)
                link(dve, v.tensor_tensor(x_rstd, x_rstd, dinv[:], ALU.mult))
                relu_times(dve, nodes[:], x_rstd)

            @block.scalar
            def _(act):
                take_roots(act, first_root)
        start_layer(0, nodes)
        prelude.close()
        end_phase()

        def general_buffers(scope, layer):
            return {n: sb(f"{n}_{layer}", shape, dt, scope) for n, shape, dt in (
                ("g_src", [P, 2, 1], I32), ("g_dst", [P, 2, 1], I32), ("g_row", [P, 2, DIM], F32),
                ("g_shift", [P, 2, CHUNKS], F32), ("g_dstf", [P, 2, 1], F32), ("g_hot", [P, 2, CHUNK], F32),
                ("g_attr", [BIASROW + 1, 2, P], F32), ("g_edge", [P, 2, DIM], F32))}

        def general_pass(layer, with_edges, B):
            g_src, g_dst, g_row, g_shift, g_dstf, g_hot, g_attr, g_edge = (
                B[n] for n in ("g_src", "g_dst", "g_row", "g_shift", "g_dstf", "g_hot", "g_attr", "g_edge"))
            s_in, s_row, s_free, s_scal, s_hotg = ([sem(f"s_g{n}{layer}_{h}") for h in range(2)]
                                                   for n in ("in", "row", "free", "scal", "hot"))
            s_go, s_prod, s_edge, s_sum, s_add, s_chain, s_zero = sems(*(f"g{n}{layer}" for n in (
                "go", "prod", "edge", "sum", "add", "chain", "zero")))
            loads = 3 if with_edges else 2
            PAIRS = (SLICES if with_edges else ALL_SLICES) // 2
            widths = [min(CHUNK, NODES - c * CHUNK) for c in range(CHUNKS)]

            def gpsimd(pool):
                with pool.Fori(0, PAIRS) as i:
                    for h in range(2):
                        pool.wait_ge(s_in[h], i * (16 * loads) + 16 * loads)
                        pool.sem_inc(s_go, 1)
                        nc.gpsimd.indirect_dma_start(
                            g_row[:, h, :], None, tables[layer],
                            bass.IndirectOffsetOnAxis(ap=g_src[:, h, :], axis=0)).then_inc(s_row[h], 16)

            def sync(sp):
                with sp.Fori(0, PAIRS) as i:
                    for h in range(2):
                        sp.wait_ge(s_free[h], i + 1)
                        t = i * 2 + h
                        sp.dma_start(g_src[:, h, :], A["src_slices"][bass.ds(t, 1), :].rearrange("o e -> e o"))\
                            .then_inc(s_in[h], 16)
                        sp.dma_start(g_dst[:, h, :], A["dst_slices"][bass.ds(t, 1), :].rearrange("o e -> e o"))\
                            .then_inc(s_in[h], 16)
                        if with_edges:
                            sp.dma_start(g_attr[0:EDIM, h, :], A["attr_tiles"].rearrange(
                                "t (f c e) -> t c f e", f=EDIM, c=2)[bass.ds(i, 1), h]
                                .rearrange("o f e -> f (o e)")).then_inc(s_in[h], 16)

            def tensor(pe):
                with pe.Fori(0, PAIRS) as i:
                    for h in range(2):
                        pe.wait_ge(s_row[h], i * 16 + 16)
                        if with_edges:
                            nc.tensor.matmul(bank[4 + h][:, 0:DIM], g_attr[:, h, :], edge_w[:], start=True,
                                             stop=True).then_inc(s_prod, 1)
                            pe.wait_ge(s_edge, i * 2 + (h + 1))
                        for c, width in enumerate(widths):
                            n = CHUNKS * h + c
                            pe.wait_ge(s_hotg[n % 2], i * CHUNKS + (n // 2 + 1))
                            last = nc.tensor.matmul(bank[n % 2][:, 0:width], g_row[:, h, :], g_hot[:, n % 2, 0:width],
                                                    start=True, stop=True)
                            if with_edges:
                                last = nc.tensor.matmul(bank[2 + n % 2][:, 0:width], g_edge[:, h, :],
                                                        g_hot[:, n % 2, 0:width], start=True, stop=True)
                            last.then_inc(s_sum, 1)

            def scalar(act):
                if with_edges:
                    with act.Fori(0, PAIRS) as i:
                        for h in range(2):
                            act.wait_ge(s_prod, i * 2 + (h + 1))
                            nc.scalar.activation(g_edge[:, h, :], bank[4 + h][:, 0:DIM], ACT.Relu).then_inc(s_edge, 1)

            def vector(dve):
                for s in s_free:
                    dve.sem_inc(s, 1)
                if not with_edges:
                    v.memset(acc, 0.0).then_inc(s_zero, 1)
                    dve.wait_ge(s_zero, 1)
                with dve.Fori(0, PAIRS) as i:
                    for h in range(2):
                        dve.wait_ge(s_in[h], i * (16 * loads) + 16 * loads)
                        v.tensor_copy(g_dstf[:, h, :], g_dst[:, h, :]).then_inc(s_chain, 1)
                        dve.wait_ge(s_chain, i * 4 + (2 * h + 1))
                        v.tensor_scalar(g_shift[:, h, :], general_shift[:], g_dstf[:, h, :], None,
                                        ALU.add).then_inc(s_chain, 1)
                        dve.wait_ge(s_chain, i * 4 + (2 * h + 2))
                        for c, width in enumerate(widths):
                            n = CHUNKS * h + c
                            v.tensor_scalar(g_hot[:, n % 2, 0:width], node_iota[:, 0:width], g_shift[:, h, c:c + 1],
                                            None, ALU.is_equal).then_inc(s_hotg[n % 2], 1)
                            dve.wait_ge(s_sum, i * (2 * CHUNKS) + (n + 1))
                            part = acc[:, c * CHUNK:c * CHUNK + width]
                            last = v.tensor_tensor(part, part, bank[n % 2][:, 0:width], ALU.add)
                            if with_edges:
                                part = acc_edge[:, c * CHUNK:c * CHUNK + width]
                                last = v.tensor_tensor(part, part, bank[2 + n % 2][:, 0:width], ALU.add)
                            last.then_inc(s_add, 1)
                            dve.wait_ge(s_add, i * (2 * CHUNKS) + (n + 1))
                        dve.sem_inc(s_free[h], 1)

            return dict(gpsimd=gpsimd, sync=sync, tensor=tensor, scalar=scalar, vector=vector)

        tail = ExitStack()
        B = general_buffers(tail, 0)
        idx = sb("idx", [P, 2, 2 * GROUP], I32, tail)
        msg = sb("msg", [P, 2, 2 * GROUP, DIM], F32, tail)
        onehot = sb("onehot", [P, 2, 2 * GROUP, WINDOW], F32, tail)
        attr_ring = sb("attr_ring", [BIASROW + 1, 2, GROUP, SUPER], F32, tail)
        edge_msg = sb("edge_msg", [P, 2 * GROUP, DIM], F32, tail)
        hot_low = sb("hot_low", [P, RING, 2, P], BF16, tail)
        hot_key = sb("hot_key", [P, RING, 2, BLOCK], BF16, tail)
        staged = sb("staged", [P, 2, BGROUP, BLOCK], F8, tail)
        key_iota = sb("key_iota", [P, BLOCK], BF16, tail)
        low_iota = sb("low_iota", [P, P], BF16, tail)
        ident_bf = sb("ident_bf", [P, P], BF16, tail)
        hot_keep = sb("hot_keep", [P, RING, P], BF16, tail)
        with nc.Block() as block:
            @block.vector
            def _(dve):
                v.memset(attr_ring[:], 1.0)
                v.memset(B["g_attr"][:], 1.0)
                v.memset(staged[:, 1, BGROUP - 1, :].bitcast(U8), 0)
                v.tensor_copy(ident_bf[:], ident[:])
                v.tensor_copy(low_iota[:], node_iota[:, 0:P])
                v.tensor_scalar(key_iota[:], node_iota[:, 0:BLOCK], -float(MIDDLE), None, ALU.add)

        s_used, s_gather, s_attr_in, s_out = ([sem(f"s_{n}1_{h}") for h in range(2)]
                                              for n in ("used", "gather", "attr_in", "out"))
        s_idx, s_go, s_prod, s_emsg, s_eused, s_onehot, s_taken, s_add, s_hotb, s_run, s_copy, s_copygo, s_keepgo = sems(
            "idx1", "go1", "prod1", "emsg1", "eused1", "onehot1", "taken1", "add1", "hotb", "run", "copy",
            "copygo", "keepgo")
        general = general_pass(0, True, B)
        with nc.Block() as block:
            @block.gpsimd
            def _(pool):
                with pool.If(is_sorted(pool) > 0):
                    with pool.Fori(0, ITERS) as i:
                        for h in range(2):
                            pool.wait_ge(s_used[h], i + 1)
                            nc.gpsimd.tensor_copy(
                                idx[:, h, :], src_steps[:, bass.ds(i * (2 * GROUP) + h * GROUP, GROUP), :]
                                .rearrange("p s c -> p (s c)")).then_inc(s_idx, 1)
                            pool.wait_ge(s_idx, i * 2 + (h + 1))
                            pool.sem_inc(s_go, 1)
                            for k in range(2 * GROUP):
                                nc.gpsimd.indirect_dma_start(
                                    msg[:, h, k, :], None, tables[0],
                                    bass.IndirectOffsetOnAxis(ap=idx[:, h, k:k + 1], axis=0)
                                ).then_inc(s_gather[h], 16)
                with pool.Else():
                    general["gpsimd"](pool)

            @block.sync
            def _(sp):
                def load_features(h, at):
                    sp.dma_start(attr_ring[0:EDIM, h], attr_steps[at, :].rearrange("s (f e) -> f s e", f=EDIM))\
                        .then_inc(s_attr_in[h], 16)

                with sp.If(is_sorted(sp) > 0):
                    load_features(0, slice(0, GROUP))
                    regs = [sp.alloc_register(f"ccol_{k}") for k in range(BGROUP)]
                    with sp.Fori(0, ITERS) as i:
                        for h in range(2):
                            sp.reg_load(regs, ccol_row[0:1, bass.ds(i * (2 * BGROUP) + h * BGROUP, BGROUP)])
                            sp.wait_ge(s_prod, i * 4 + (2 * h + 1))
                            load_features(1 - h, bass.ds(i * (2 * GROUP) + (h + 1) * GROUP, GROUP))
                            for k in range(BGROUP):
                                to = sp.snap(regs[k], min_val=0, max_val=NARROWS * BLOCK)
                                window_ends = sp.snap(to < NARROWS * BLOCK)
                                sp.wait_ge(s_copy, i * (2 * BGROUP) + (h * BGROUP + k + 2))
                                sp.dma_start(counts[:, bass.ds(to, BLOCK)], staged[:, h, k, :].bitcast(U8),
                                             cond=window_ends).then_inc(s_out[h], 16)
                    for h in range(2):
                        sp.wait_ge(s_out[h], ITERS * BGROUP * 16 + 1)
                    sp.wait_ge(s_attr_in[0], (ITERS + 1) * 16)
                with sp.Else():
                    general["sync"](sp)

            @block.scalar
            def _(act):
                with act.If(is_sorted(act) > 0):
                    for s, n in ((s_copy, 1), (s_emsg, 2), (s_out[0], 1), (s_out[1], 1)):
                        act.sem_inc(s, n)
                    with act.Fori(0, ITERS) as i:
                        for h in range(2):
                            act.wait_ge(s_out[h], i * (BGROUP * 16) + 1)
                            for k in range(BGROUP):
                                n = h * BGROUP + k + 1
                                act.wait_ge(s_run, i * (2 * BGROUP) + (n + RING))
                                act.sem_inc(s_copygo, 1)
                                nc.scalar.activation(staged[:, h, k, :], bank[k % 2][:, 0:BLOCK], ACT.Copy,
                                                     saturate=True).then_inc(s_copy, 1)
                                if k in (1, 3):
                                    q = k // 2
                                    act.wait_ge(s_prod, i * 4 + (2 * h + q + 2))
                                    act.wait_ge(s_eused, i * 4 + (2 * h + q + 1))
                                    nc.scalar.activation(
                                        edge_msg[:, 4 * q:4 * q + 4, :].rearrange("p k d -> p (k d)"),
                                        bank[2 + q][:, :], ACT.Relu).then_inc(s_emsg, 1)
                with act.Else():
                    general["scalar"](act)

            @block.tensor
            def _(pe):
                def add_counts(i, h, k):
                    n = h * BGROUP + k + 1
                    pe.wait_ge(s_hotb, i * (2 * BGROUP) + n)
                    for c in range(2):
                        nc.tensor.matmul(bank[k % 2][:, 0:BLOCK], hot_low[:, k % RING, c, :],
                                         hot_key[:, k % RING, c, :], start=(c == 0), stop=False)
                    pe.wait_ge(s_copy, i * (2 * BGROUP) + n)
                    pe.sem_inc(s_keepgo, 1)
                    before = staged[:, h, k - 1, :] if k else staged[:, 1 - h, BGROUP - 1, :]
                    nc.tensor.matmul(bank[k % 2][:, 0:BLOCK], hot_keep[:, k % RING, :], before, start=False,
                                     stop=True).then_inc(s_run, 1)

                def feature_products(i, h, q):
                    if q == 0:
                        pe.wait_ge(s_attr_in[h], i * 16 + 16)
                    pe.wait_ge(s_emsg, i * 4 + (2 * h + q + 1))
                    for k in range(4):
                        last = nc.tensor.matmul(bank[2 + q][:, k * P:(k + 1) * P],
                                                attr_ring[:, h, 2 * q + k // 2, (k % 2) * P:(k % 2 + 1) * P], edge_w[:],
                                                start=True, stop=True)
                    last.then_inc(s_prod, 1)

                def sum_rows(i, h, q):
                    if q == 0:
                        pe.wait_ge(s_gather[h], i * (32 * GROUP) + 32 * GROUP)
                        pe.wait_ge(s_onehot, i * 2 + (h + 1))
                        pe.wait_ge(s_taken, i * 2 + (h + 1))
                    for s in (0, 1):
                        for c in range(2):
                            k = 4 * q + 2 * s + c
                            last = nc.tensor.matmul(bank[4 + 2 * h + q][:, 2 * s * WINDOW:(2 * s + 1) * WINDOW],
                                                    msg[:, h, k, :], onehot[:, h, k, :], start=(c == 0), stop=(c == 1))
                    if q == 1:
                        last.then_inc(s_used[h], 1)

                def sum_messages(i, h, q):
                    pe.wait_ge(s_emsg, i * 4 + (2 * h + q + 3))
                    for s in (0, 1):
                        for c in range(2):
                            k = 4 * q + 2 * s + c
                            last = nc.tensor.matmul(bank[4 + 2 * h + q][:, (2 * s + 1) * WINDOW:(2 * s + 2) * WINDOW],
                                                    edge_msg[:, k, :], onehot[:, h, k, :], start=(c == 0),
                                                    stop=(c == 1))
                    last.then_inc(s_eused, 1)

                with pe.If(is_sorted(pe) > 0):
                    for s, n in ((s_used[0], 1), (s_used[1], 1), (s_prod, 1), (s_run, RING)):
                        pe.sem_inc(s, n)
                    for b in range(2):
                        nc.tensor.matmul(bank[6 + b][:, 0:4 * WINDOW], zeros_bf[:, 0:P], zeros_bf[:], start=True,
                                         stop=True).then_inc(s_eused, 1)
                    with pe.Fori(0, ITERS) as i:
                        for h in range(2):
                            add_counts(i, h, 0)
                            feature_products(i, h, 0)
                            add_counts(i, h, 1)
                            feature_products(i, h, 1)
                            add_counts(i, h, 2)
                            sum_rows(i, h, 0)
                            add_counts(i, h, 3)
                            sum_rows(i, h, 1)
                            add_counts(i, h, 4)
                            sum_messages(i, h, 0)
                            add_counts(i, h, 5)
                            sum_messages(i, h, 1)
                            add_counts(i, h, 6)
                            add_counts(i, h, 7)
                with pe.Else():
                    general["tensor"](pe)

            @block.vector
            def _(dve):
                def make_onehot(h, steps):
                    v.tensor_tensor(
                        onehot[:, h], node_iota[:, 0:WINDOW].unsqueeze(1).broadcast_to([P, 2 * GROUP, WINDOW]),
                        dst_steps[:, steps, :].rearrange("p s c -> p (s c)").unsqueeze(2)
                        .broadcast_to([P, 2 * GROUP, WINDOW]), ALU.is_equal).then_inc(s_onehot, 1)

                def make_count_onehots(i, h, k):
                    dve.wait_ge(s_run, i * (2 * BGROUP) + (h * BGROUP + k + 1))
                    step = i * (2 * BGROUP) + (h * BGROUP + k)
                    v.tensor_scalar(hot_keep[:, k % RING, :], ident_bf[:], keep_steps[:, bass.ds(step, 1)], None,
                                    ALU.mult)
                    for c in range(2):
                        v.tensor_scalar(hot_low[:, k % RING, c, :], low_iota[:],
                                        low_steps[:, bass.ds(step, 1), c], None, ALU.is_equal)
                        last = v.tensor_scalar(hot_key[:, k % RING, c, :], key_iota[:],
                                               key_steps[:, bass.ds(step, 1), c], None, ALU.is_equal)
                    last.then_inc(s_hotb, 1)

                def add_sums(done, h, at):
                    for s in range(GROUP):
                        part = acc2[:, :, at[s]]
                        dve.wait_ge(s_add, done + (s + 1))
                        v.tensor_tensor(part, part, bank[4 + 2 * h + s // 2][:, 2 * (s % 2) * WINDOW:(2 * (s % 2) + 2) * WINDOW]
                                        .rearrange("p (a n) -> p a n", a=2), ALU.add).then_inc(s_add, 1)

                with dve.If(is_sorted(dve) > 0):
                    for s in (s_add, s_taken):
                        dve.sem_inc(s, 1)
                    make_onehot(0, slice(0, GROUP))
                    regs = [dve.alloc_register(f"wcol_{k}") for k in range(GROUP)]
                    with dve.Fori(0, ITERS) as i:
                        for h in range(2):
                            make_count_onehots(i, h, 0)
                            make_count_onehots(i, h, 1)
                            dve.reg_load(regs, wcol_row[0:1, bass.ds(i * (2 * GROUP) + h * GROUP, GROUP)])
                            at = [bass.ds(dve.snap(r, min_val=0, max_val=NODES - WINDOW), WINDOW) for r in regs]
                            dve.wait_ge(s_eused, i * 4 + (2 * h + 2))
                            add_sums(i * (2 * GROUP) + h * GROUP, 1 - h, at)
                            dve.wait_ge(s_add, i * (2 * GROUP) + (h * GROUP + GROUP + 1))
                            dve.sem_inc(s_taken, 1)
                            make_onehot(1 - h, bass.ds(i * (2 * GROUP) + (h + 1) * GROUP, GROUP))
                            for k in range(2, BGROUP):
                                make_count_onehots(i, h, k)
                    dve.reg_load(regs, wcol_row[0:1, ITERS * 2 * GROUP:ITERS * 2 * GROUP + GROUP])
                    at = [bass.ds(dve.snap(r, min_val=0, max_val=NODES - WINDOW), WINDOW) for r in regs]
                    dve.wait_ge(s_eused, ITERS * 4 + 2)
                    add_sums(ITERS * 2 * GROUP, 1, at)
                with dve.Else():
                    general["vector"](dve)
        tail.close()
        first.close()
        end_phase()

        def dense_pass(layer):
            tail = ExitStack()
            raw = [sb(f"raw{h}_{layer}", [P, GWIN * BLOCK], U8, tail) for h in range(2)]
            packed = sb(f"packed_{layer}", [P, 2, SRCS, GCOLS], U8, tail)
            table = sb(f"table_sb{layer}", [P, SRCS, DIM], F32, tail)
            parts = sb(f"parts{layer}", [P, SRCS, 3, DIM], BF16, tail)
            rest = packed[:].rearrange("p b s c -> p (b s c)").bitcast(F32)[:, 0:SRCS * DIM]\
                .rearrange("p (s d) -> p s d", d=DIM)
            top = sb(f"top{layer}", [P, GROUPS + 1], F32, tail)
            s_raw = [sem(f"s_raw{h}_{layer}") for h in range(2)]
            s_tabin, s_pad, s_high, s_mid, s_left, s_parts, s_packed, s_summed, s_into, s_go, s_start, s_top, s_topt = sems(
                *(f"{n}{layer}" for n in ("tabin", "pad", "high", "mid", "left", "parts", "packed", "summed", "into",
                                          "dense_go", "sum_start", "top", "topt")))
            pieces = [slice(k, min(k + SPLIT, SRCS)) for k in range(0, SRCS, SPLIT)]
            PAIRS = (GROUPS - 1) // 2
            whole_rows = (NODES // P) * P
            assert GROUPS % 2 == 1
            goes = is_sorted if layer == 1 else counts_fit

            with nc.Block() as block:
                @block.sync
                def _(sp):
                    with sp.If(goes(sp) > 0):
                        sp.wait_ge(s_pad, 1)
                        for k, ss in enumerate(pieces):
                            full = min(ss.stop, NODES // P)
                            sp.dma_start(table[:, ss.start:full, :], tables[layer][ss.start * P:full * P, :]
                                         .rearrange("(s p) d -> p s d", p=P)).then_inc(s_tabin, 16)
                            sp.wait_ge(s_tabin, 16 * (k + 1))
                        sp.dma_start(table[0:NODES - whole_rows, SRCS - 1, :], tables[layer][whole_rows:, :])\
                            .then_inc(s_tabin, 16)
                        sp.dma_start(raw[0][:], counts[:, 0:GWIN * BLOCK]).then_inc(s_raw[0], 16)
                        with sp.Fori(0, PAIRS) as i:
                            for b in (1, 0):
                                start = i * (2 * GWIN * BLOCK) + (2 - b) * GWIN * BLOCK
                                sp.wait_ge(s_packed, i * 2 + (2 - b))
                                sp.sem_inc(s_go, 1)
                                sp.dma_start(raw[b][:], counts[:, bass.ds(start, GWIN * BLOCK)]).then_inc(s_raw[b], 16)

                @block.scalar
                def _(act):
                    with act.If(goes(act) > 0):
                        for k, ss in enumerate(pieces):
                            act.wait_ge(s_tabin, 16 * (k + 1) if ss.stop < SRCS else 16 * (len(pieces) + 1))
                            nc.scalar.activation(parts[:, ss, 0, :], table[:, ss, :], ACT.Copy).then_inc(s_high, 1)
                            if k:
                                act.wait_ge(s_left, k)
                                before = pieces[k - 1]
                                nc.scalar.activation(parts[:, before, 1, :], rest[:, before, :],
                                                     ACT.Copy).then_inc(s_mid, 1)
                        act.wait_ge(s_left, len(pieces))
                        nc.scalar.activation(parts[:, pieces[-1], 1, :], rest[:, pieces[-1], :], ACT.Copy).then_inc(s_mid, 1)

                @block.vector
                def _(dve):
                    def pack(g, b):
                        if g is not None:
                            dve.wait_ge(s_summed, g)
                        v.tensor_copy(packed[:, b].bitcast(I32).rearrange("p s (u n) -> p s u n", u=GWIN),
                                      raw[b][:].bitcast(I32).rearrange("p (u s n) -> p s u n", u=GWIN, s=SRCS))\
                            .then_inc(s_packed, 1)
                        if layer == 1:
                            at = top[:, bass.ds(g + 1, 1)] if g is not None else top[:, 1:2]
                            dve.wait_ge(s_packed, g + 2 if g is not None else 2)
                            v.tensor_reduce(at, packed[:, b].rearrange("p s c -> p (s c)"), AX.X, ALU.max)

                    def add_group(g, b):
                        dve.wait_ge(s_summed, g + 2)
                        part = acc[:, bass.ds(g * GCOLS, GCOLS)]
                        v.tensor_tensor(part, part, bank[b][:, 0:GCOLS], ALU.add).then_inc(s_into, 1)

                    with dve.If(goes(dve) > 0):
                        v.memset(table[P - 32:, SRCS - 1, :], 0.0).then_inc(s_pad, 1)
                        for k, ss in enumerate(pieces):
                            dve.wait_ge(s_high, k + 1)
                            v.tensor_tensor(rest[:, ss, :], table[:, ss, :], parts[:, ss, 0, :],
                                            ALU.subtract).then_inc(s_left, 1)
                            if k:
                                before = pieces[k - 1]
                                dve.wait_ge(s_mid, k)
                                v.tensor_tensor(parts[:, before, 2, :], rest[:, before, :], parts[:, before, 1, :],
                                                ALU.subtract).then_inc(s_parts, 1)
                        dve.wait_ge(s_mid, len(pieces))
                        v.tensor_tensor(parts[:, pieces[-1], 2, :], rest[:, pieces[-1], :], parts[:, pieces[-1], 1, :],
                                        ALU.subtract).then_inc(s_parts, 1)
                        dve.wait_ge(s_parts, len(pieces))
                        dve.sem_inc(s_packed, 1)
                        dve.sem_inc(s_into, 1)
                        dve.wait_ge(s_raw[0], 16)
                        pack(None, 0)
                        with dve.Fori(0, PAIRS) as i:
                            dve.wait_ge(s_raw[1], i * 16 + 16)
                            pack(i * 2 + 1, 1)
                            add_group(i * 2, 0)
                            dve.wait_ge(s_raw[0], i * 16 + 32)
                            pack(i * 2 + 2, 0)
                            add_group(i * 2 + 1, 1)
                        dve.wait_ge(s_summed, GROUPS + 1)
                        part = acc[:, (GROUPS - 1) * GCOLS:]
                        v.tensor_tensor(part, part, bank[0][:, 0:GCOLS], ALU.add).then_inc(s_into, 1)
                        if layer == 1:
                            dve.wait_ge(s_into, GROUPS + 1)
                            v.tensor_reduce(top[:, 0:1], top[:, 1:], AX.X, ALU.max).then_inc(s_top, 1)
                            dve.wait_ge(s_topt, 1)
                            v.tensor_reduce(col[0:1, 0:1], bank[2][0:1, 0:P], AX.X, ALU.max).then_inc(s_top, 1)
                            dve.wait_ge(s_top, 2)
                            v.tensor_scalar(flags[:, 1:2], col[0:1, 0:1], float(F8_15), None, ALU.is_le)
                    if layer == 1:
                        with dve.Else():
                            v.memset(flags[:, 1:2], 0)

                @block.tensor
                def _(pe):
                    def sum_group(b):
                        counts_8 = packed[:, b].bitcast(F8)
                        for s in range(SRCS):
                            for part in range(3):
                                last = nc.tensor.matmul(bank[b][:, 0:GCOLS], parts[:, s, part, :], counts_8[:, s, :],
                                                        start=(s == part == 0), stop=(s == SRCS - 1 and part == 2))
                        last.then_inc(s_summed, 1)

                    with pe.If(goes(pe) > 0):
                        pe.sem_inc(s_summed, 1)
                        pe.wait_ge(s_packed, 2)
                        sum_group(0)
                        with pe.Fori(0, PAIRS) as i:
                            for b in (1, 0):
                                pe.wait_ge(s_packed, i * 2 + (4 - b))
                                pe.wait_ge(s_into, i * 2 + (2 - b))
                                pe.sem_inc(s_start, 1)
                                sum_group(b)
                        if layer == 1:
                            pe.wait_ge(s_top, 1)
                            nc.tensor.transpose(bank[2][0:1, 0:P], top[:, 0:1], ident[:]).then_inc(s_topt, 1)
            tail.close()

            tail = ExitStack()
            general = general_pass(layer, False, general_buffers(tail, layer))
            with nc.Block() as block:
                @block.sync
                def _(sp):
                    with sp.If(counts_fit(sp) < 1):
                        general["sync"](sp)

                @block.gpsimd
                def _(pool):
                    with pool.If(counts_fit(pool) < 1):
                        general["gpsimd"](pool)

                @block.vector
                def _(dve):
                    with dve.If(counts_fit(dve) < 1):
                        general["vector"](dve)

                @block.tensor
                def _(pe):
                    with pe.If(counts_fit(pe) < 1):
                        general["tensor"](pe)
            tail.close()
            end_phase()

        def gcn_nodes(layer, nodes, spare, x_rows):
            b, g, be = (rowpar(f"L0_gnn_{n}{layer + 1}") for n in ("b", "g", "be"))
            s_prod, s_took, s_sums, s_total, s_x1, s_x1_out, s_ready = (
                sem(f"s_{n}_gcn{layer}") for n in ("prod", "took", "sums", "total", "x1", "x1_out", "ready"))
            first_root = len(roots)
            with nc.Block() as block:
                @block.tensor
                def _(pe):
                    for k, ws in quads():
                        if k >= 2:
                            pe.wait_ge(s_took, ws[0] - QUAD)
                        for q, w in enumerate(ws):
                            nc.tensor.matmul(bank[k % 2][0:WINDOW, q * DIM:(q + 1) * DIM],
                                             acc[:, w * WINDOW:(w + 1) * WINDOW], mats[:, layer, :],
                                             start=True, stop=True).then_inc(s_prod, 1)
                    for n in range(2):
                        pe.wait_ge(s_sums, n + 1)
                        nc.tensor.matmul(bank[2][0:WINDOW, n:n + 1], ones[0:WINDOW, 0:WINDOW], col[0:WINDOW, n:n + 1],
                                         start=True, stop=True).then_inc(s_total, 1)

                @block.vector
                def _(dve):
                    flat = nodes[:].rearrange("p w d -> p (w d)")
                    for w in range(WINDOWS):
                        dve.wait_ge(s_prod, min((w // QUAD + 1) * QUAD, WINDOWS))
                        v.scalar_tensor_tensor(nodes[:, w, :],
                                               bank[w // QUAD % 2][0:WINDOW, (w % QUAD) * DIM:(w % QUAD + 1) * DIM],
                                               dinv[:, w:w + 1], b, ALU.mult, ALU.add).then_inc(s_took, 1)
                    dve.wait_ge(s_took, WINDOWS)
                    v.tensor_reduce(col[0:WINDOW, 0:1], flat, AX.X, ALU.add).then_inc(s_sums, 1)
                    dve.wait_ge(s_total, 1)
                    link(dve, v.tensor_scalar(col[0:WINDOW, 2:3], bank[2][0:WINDOW, 0:1], 1.0 / (NODES * DIM),
                                                     None, ALU.mult))
                    link(dve, v.tensor_scalar(flat, flat, col[0:WINDOW, 2:3], None, ALU.subtract))
                    link(dve, v.tensor_tensor(spare[:], nodes[:], nodes[:], ALU.mult))
                    v.tensor_reduce(col[0:WINDOW, 1:2], spare[:].rearrange("p w d -> p (w d)"), AX.X,
                                    ALU.add).then_inc(s_sums, 1)
                    dve.wait_ge(s_total, 2)
                    link(dve, v.tensor_copy(col[0:WINDOW, 3:4], bank[2][0:WINDOW, 1:2]))
                    rsqrt(dve, col[0:WINDOW, 3:4], 1.0 / (NODES * DIM))
                    link(dve, v.scalar_tensor_tensor(nodes[:], nodes[:], col[0:WINDOW, 3:4], over_windows(g),
                                                            ALU.mult, ALU.mult))
                    link(dve, v.tensor_tensor(nodes[:], nodes[:], over_windows(be), ALU.add))
                    if layer == 0:
                        link(dve, v.scalar_tensor_tensor(nodes[:], nodes[:], 0.0, over_features(dinv[:]),
                                                                ALU.max, ALU.mult))
                    else:
                        dve.wait_ge(s_x1, 16)
                        link(dve, v.scalar_tensor_tensor(nodes[:], nodes[:], 0.0, x_rows[:], ALU.max, ALU.add))
                        dve.sem_inc(s_ready, 1)
                        dve.wait_ge(s_x1_out, 16)
                        center(dve, nodes[:], spare[:], stat[:, 0, :], stat[:, 1, :])
                        relu_times(dve, nodes[:], stat[:, 1, :])

                @block.scalar
                def _(act):
                    take_roots(act, first_root)

                if layer == 1:
                    @block.sync
                    def _(sp):
                        sp.dma_start(x_rows[:], by_window(A["x"])).then_inc(s_x1, 16)
                        sp.wait_ge(s_ready, 1)
                        sp.dma_start(by_window(x1_dram), nodes[:]).then_inc(s_x1_out, 16)
                        sp.wait_ge(s_x1_out, 16)

        def add_edges(nodes, spare):
            s_prod, s_took = sem("s_prod_edges"), sem("s_took_edges")
            with nc.Block() as block:
                @block.tensor
                def _(pe):
                    for k, ws in quads():
                        if k >= 2:
                            pe.wait_ge(s_took, ws[0] - QUAD)
                        for q, w in enumerate(ws):
                            nc.tensor.matmul(bank[k % 2][0:WINDOW, q * DIM:(q + 1) * DIM],
                                             acc_edge[:, w * WINDOW:(w + 1) * WINDOW], mats[:, MATS.index("L1_gnn_ee_w2"), :],
                                             start=True, stop=True).then_inc(s_prod, 1)

                @block.vector
                def _(dve):
                    link(dve, v.tensor_copy(spare[:], over_windows(rowpar("L1_gnn_ee_b2"))))
                    link(dve, v.tensor_tensor(spare[:], spare[:], over_features(indeg[:]), ALU.mult))
                    link(dve, v.tensor_tensor(nodes[:], nodes[:], spare[:], ALU.add))
                    for k, ws in quads():
                        dve.wait_ge(s_prod, ws[-1] + 1)
                        part = nodes[:, ws[0]:ws[-1] + 1, :]
                        v.tensor_tensor(part, part, bank[k % 2][0:WINDOW, 0:len(ws) * DIM]
                                        .rearrange("p (w d) -> p w d", d=DIM), ALU.add).then_inc(s_took, len(ws))
                    dve.wait_ge(s_took, WINDOWS)

        def gin_mlp(n):
            s_prod, s_took = sem(f"s_prod_mlp{n}"), sem(f"s_took_mlp{n}")
            w = mats[:, MATS.index(f"L1_gnn_mlp_w{n}"), :]
            b, g, bb = (cols[:, k:k + 1] for k in range(3 * n - 3, 3 * n))
            pieces = range(0, NODES, WIDE)
            z, y = acc[:, 0:NODES], acc_edge[:, 0:NODES]
            first_root = len(roots)
            with nc.Block() as block:
                @block.tensor
                def _(pe):
                    for k, at in enumerate(pieces):
                        m = min(WIDE, NODES - at)
                        if k >= 4:
                            pe.wait_ge(s_took, k - 3)
                        nc.tensor.matmul(bank[k % 4][:, 0:m], w, z[:, at:at + m], start=True,
                                         stop=True).then_inc(s_prod, 1)

                @block.scalar
                def _(act):
                    for k, at in enumerate(pieces):
                        m = min(WIDE, NODES - at)
                        act.wait_ge(s_prod, k + 1)
                        nc.scalar.activation(y[:, at:at + m], bank[k % 4][:, 0:m], ACT.Identity,
                                             bias=b).then_inc(s_took, 1)

            with nc.Block() as block:
                @block.vector
                def _(dve):
                    link(dve, v.tensor_reduce(col[:, 0:1], y, AX.X, ALU.add))
                    link(dve, v.tensor_scalar(col[:, 0:1], col[:, 0:1], 1.0 / NODES, None, ALU.mult))
                    link(dve, v.tensor_scalar(y, y, col[:, 0:1], None, ALU.subtract))
                    link(dve, v.tensor_tensor(z, y, y, ALU.mult))
                    link(dve, v.tensor_reduce(col[:, 1:2], z, AX.X, ALU.add))
                    rsqrt(dve, col[:, 1:2], 1.0 / NODES)
                    link(dve, v.tensor_tensor(col[:, 1:2], col[:, 1:2], g, ALU.mult))

                @block.scalar
                def _(act):
                    take_roots(act, first_root)

            with nc.Block() as block:
                @block.scalar
                def _(act):
                    nc.scalar.activation(z, y, ACT.Relu, scale=col[:, 1:2], bias=bb)

        def finish(nodes):
            s_x1, s_turned, s_added, s_out = (sem(f"s_{n}_end") for n in ("x1", "turned", "added", "out"))
            with nc.Block() as block:
                @block.sync
                def _(sp):
                    sp.dma_start(nodes[:], by_window(x1_dram)).then_inc(s_x1, 16)
                    parts = 5
                    for k in range(parts):
                        ws = slice(k * WINDOWS // parts, (k + 1) * WINDOWS // parts)
                        sp.wait_ge(s_added, ws.stop)
                        sp.dma_start(by_window(out)[:, ws, :], nodes[:, ws, :]).then_inc(s_out, 16)
                    sp.wait_ge(s_out, 16 * parts)

                @block.tensor
                def _(pe):
                    for k, ws in quads():
                        if k >= 2:
                            pe.wait_ge(s_added, ws[0] - QUAD)
                        for q, w in enumerate(ws):
                            last = nc.tensor.transpose(bank[k % 2][0:WINDOW, q * DIM:(q + 1) * DIM],
                                                       acc[:, w * WINDOW:(w + 1) * WINDOW], ident[:])
                        last.then_inc(s_turned, 1)

                @block.vector
                def _(dve):
                    dve.wait_ge(s_x1, 16)
                    for k, ws in quads():
                        dve.wait_ge(s_turned, k + 1)
                        part = nodes[:, ws[0]:ws[-1] + 1, :]
                        v.tensor_tensor(part, part, bank[k % 2][0:WINDOW, 0:len(ws) * DIM]
                                        .rearrange("p (w d) -> p w d", d=DIM), ALU.add).then_inc(s_added, len(ws))

        for layer in (0, 1):
            tail = ExitStack()
            nodes = sb(f"nodes{layer}", [WINDOW, WINDOWS, DIM], F32, tail)
            spare = sb(f"spare{layer}", [WINDOW, WINDOWS, DIM], F32, tail)
            x_rows = sb(f"x_rows{layer}", [WINDOW, WINDOWS, DIM], F32, tail)
            gcn_nodes(layer, nodes, spare, x_rows)
            if layer == 1:
                add_edges(nodes, spare)
            start_layer(layer + 1, nodes)
            tail.close()
            dense_pass(layer + 1)
        gin_mlp(1)
        gin_mlp(2)
        tail = ExitStack()
        finish(sb("out_rows", [WINDOW, WINDOWS, DIM], F32, tail))
        tail.close()


def kernel(x, src, dst, edge_attr_16, **params):
    import numpy as np
    import concourse.bacc as bacc
    from concourse.bass_utils import run_bass_kernel_spmd

    x, src, dst, attr = (np.asarray(a) for a in (x, src, dst, edge_attr_16))
    pad = TILES * SUPER - EDGES
    src_pad = np.concatenate([src, np.zeros(pad, src.dtype)])
    dst_pad = np.concatenate([dst, np.full(pad, NOWHERE, dst.dtype)])
    attr_tiles = np.concatenate([attr, np.zeros((pad, EDIM), attr.dtype)]).reshape(TILES, SUPER, EDIM)
    more = (ALL_SLICES - SLICES) * P - NODES
    own = [np.concatenate([np.arange(NODES, dtype=src.dtype), np.full(more, fill, src.dtype)]) for fill in (0, NOWHERE)]
    next_node = np.zeros((WINDOW, 2, WINDOW), np.float32)
    next_node[:, 0, :] = np.eye(WINDOW, k=-1) - np.eye(WINDOW)
    next_node[0, 1, WINDOW - 1] = 1.0
    arrays = {
        "x": x, "dst": dst, "dst_next": dst_pad[1:EDGES + 1], "edge_attr_16": attr,
        "src_tiles": src_pad.reshape(TILES, SUPER), "dst_tiles": dst_pad.reshape(TILES, SUPER),
        "src_slices": np.concatenate([src_pad, own[0]]).reshape(ALL_SLICES, P),
        "dst_slices": np.concatenate([dst_pad, own[1]]).reshape(ALL_SLICES, P),
        "dst_last": dst_pad[SUPER - 1::SUPER][None, :],
        "attr_tiles": attr_tiles.transpose(0, 2, 1).reshape(TILES, EDIM * SUPER),
        "L0_gnn_W1T": np.asarray(params["L0_gnn_W1"]).T, "L0_gnn_W2T": np.asarray(params["L0_gnn_W2"]).T,
        "ident": np.eye(P, dtype=np.float32),
        "node_iota": np.tile(np.arange(CHUNK, dtype=np.float32), (P, 1)),
        "step_iota": np.arange(BSLOTS, dtype=np.float32).reshape(BSLOTS // P, P).T,
        "node_id": np.arange(NODES, dtype=np.float32).reshape(WINDOWS, WINDOW).T,
        "next_node": next_node,
        "tile_iota": np.arange(TILES, dtype=np.float32)[None, :],
        "general_shift": np.tile(-CHUNK * np.arange(CHUNKS, dtype=np.float32), (P, 1)),
        "block_mask": np.kron(np.eye(P // EDIM), np.ones((EDIM, EDIM))).astype(np.float32),
        "fold": np.tile(np.eye(EDIM, dtype=np.float32), (P // EDIM, 1)),
    }
    for name in ROWS + COLPARS + MATS[2:] + ("L1_gnn_ee_w1",):
        arrays[name] = np.asarray(params[name])
    arrays = {n: np.ascontiguousarray(a) for n, a in arrays.items()}

    nc = bacc.Bacc("TRN2", target_bir_lowering=False, num_devices=1)
    A = {n: nc.dram_tensor(f"in_{n}", a.shape, mybir.dt.from_np(a.dtype), kind="ExternalInput").ap()
         for n, a in arrays.items()}
    out = nc.dram_tensor("out", (NODES, DIM), F32, kind="ExternalOutput").ap()
    program(nc, A, out)
    r = run_bass_kernel_spmd(nc, [{f"in_{n}": a for n, a in arrays.items()}], core_ids=[0])
    return r.results[0]["out"]
```

```python
from contextlib import ExitStack

import concourse.bass as bass
from concourse import mybir

F32 = mybir.dt.float32
BF16 = mybir.dt.bfloat16
I32 = mybir.dt.int32
U8 = mybir.dt.uint8
F8 = mybir.dt.float8e4
ALU = mybir.AluOpType
ACT = mybir.ActivationFunctionType
AX = mybir.AxisListType

NODES, DIM, EDGES, EDIM = 6250, 128, 200000, 16
P = 128
EPS = 1e-5
SUPER = 2 * P
TILES = -(-EDGES // SUPER)
SLICES = 2 * TILES
ALL_SLICES = SLICES + 2 * -(-NODES // (2 * P))
WINDOW = 125
WINDOWS = NODES // WINDOW
STEPS = TILES + WINDOWS - 1
NARROW = 8
NARROWS = -(-NODES // NARROW)
BSTEPS = TILES + NARROWS - 1
COLS = NARROWS * NARROW
SRCS = -(-NODES // P)
BLOCK = SRCS * NARROW
GROUP = 4
BGROUP = 8
KEEPS = ((0,), (1,), (), (2, 3), (), (4, 5), (6,), (7,))
RING = 8
ITERS = max(-(-STEPS // (2 * GROUP)), -(-BSTEPS // (2 * BGROUP)))
SLOTS = -(-(ITERS + 1) * 2 * GROUP // P) * P
BSLOTS = -(-ITERS * 2 * BGROUP // P) * P
NOWHERE = 2 * (SLOTS + BSLOTS) * WINDOW
FAR = 1.0e6
MIDDLE = BLOCK // 2
GWIN = 46
GCOLS = GWIN * NARROW
GROUPS = NARROWS // GWIN
SPLIT = 7
F8_15 = 0x57
CHUNK = 500
CHUNKS = -(-NODES // CHUNK)
HROWS = EDGES // WINDOW
HCOLS = 16
DEGBUFS = 3
DEGWIN = 10
FCHUNKS = 20
FROWS = HROWS // FCHUNKS
FBUFS = 4
BIASROW = 32
QUAD = 4
WIDE = 500
ROWS = ("L0_gnn_b1", "L0_gnn_g1", "L0_gnn_be1", "L0_gnn_b2", "L0_gnn_g2", "L0_gnn_be2",
        "L1_gnn_ee_b1", "L1_gnn_ee_g1", "L1_gnn_ee_bb1", "L1_gnn_ee_b2")
COLPARS = ("L1_gnn_mlp_b1", "L1_gnn_mlp_g1", "L1_gnn_mlp_bb1", "L1_gnn_mlp_b2", "L1_gnn_mlp_g2",
           "L1_gnn_mlp_bb2")
MATS = ("L0_gnn_W1T", "L0_gnn_W2T", "L1_gnn_ee_w2", "L1_gnn_mlp_w1", "L1_gnn_mlp_w2")
assert GROUPS * GWIN == NARROWS and WINDOWS % DEGWIN == 0


def quads():
    return [(g, range(g * QUAD, min((g + 1) * QUAD, WINDOWS))) for g in range(-(-WINDOWS // QUAD))]


def program(nc, A, out):
    whole = ExitStack()
    with whole:
        def sb(name, shape, dt=F32, scope=whole):
            return scope.enter_context(nc.sbuf_tensor(name, shape, dt))

        phase_sems = []

        def sem(name):
            phase_sems.append(nc.alloc_semaphore(name=name))
            return phase_sems[-1]

        def end_phase():
            nc.clear_and_free_semaphores(phase_sems)
            nc.all_engine_barrier()
            phase_sems.clear()

        def sems(*names):
            return [sem(f"s_{n}") for n in names]

        def dram(name, shape, dt=F32):
            return nc.dram_tensor(name, shape, dt, kind="Internal").ap()

        tables = [dram(f"table{i}", (NODES, DIM)) for i in range(3)]
        wcol_dram = dram("wcol_dram", (SLOTS // P, P), I32)
        ccol_dram = dram("ccol_dram", (BSLOTS // P, P), I32)
        tile_dram = dram("tile_dram", (SLOTS // P, P), I32)
        x1_dram = dram("x1_dram", (NODES, DIM))
        counts = dram("counts", (P, (NARROWS + 1) * BLOCK), U8)

        def by_window(ap):
            return ap.rearrange("(w p) d -> p w d", p=WINDOW)

        bank = [whole.enter_context(nc.psum_tensor(f"bank{i}", [P, 512], F32)) for i in range(8)]
        ident = sb("ident", [P, P])
        ones = sb("ones", [P, P])
        node_iota = sb("node_iota", [P, CHUNK])
        acc2 = sb("acc2", [P, 2, COLS])
        acc, acc_edge = acc2[:, 0, :], acc2[:, 1, :]
        dinv = sb("dinv", [WINDOW, WINDOWS])
        indeg = sb("indeg", [WINDOW, WINDOWS])
        stat = sb("stat", [WINDOW, 2, WINDOWS])
        col = sb("col", [P, 16])
        rows = sb("rows", [P, len(ROWS), DIM])
        cols = sb("cols", [P, len(COLPARS)])
        mats = sb("mats", [P, len(MATS), DIM])
        ew1 = sb("ew1", [EDIM, DIM])
        edge_w = sb("edge_w", [BIASROW + 1, DIM])
        flags = sb("flags", [1, 2], I32)
        zeros_bf = sb("zeros_bf", [P, 4 * WINDOW], BF16)
        general_shift = sb("general_shift", [P, CHUNKS])
        piece_sums = sb("piece_sums", [P, -(-NODES // WIDE)])

        def rowpar(name, parts=WINDOW):
            return rows[0:parts, ROWS.index(name), :]

        def over_windows(ap):
            return ap.unsqueeze(1).broadcast_to([WINDOW, WINDOWS, DIM])

        def over_features(ap):
            return ap.unsqueeze(2).broadcast_to([WINDOW, WINDOWS, DIM])

        s_dve, s_var, s_root = (whole.enter_context(nc.semaphore(n)) for n in ("s_dve", "s_var", "s_root"))
        ended = {}

        def link(dve, ins, chain=s_dve):
            ended[chain.name] = ended.get(chain.name, 0) + 1
            ins.then_inc(chain, 1)
            dve.wait_ge(chain, ended[chain.name])

        v = nc.vector
        roots = []

        def rsqrt(dve, ap, scale, eps=EPS):
            v.tensor_scalar(ap, ap, scale, eps, ALU.mult, ALU.add).then_inc(s_var, 1)
            roots.append(ap)
            dve.wait_ge(s_root, len(roots))
            link(dve, v.reciprocal(ap, ap))

        def take_roots(act, first):
            for n in range(first, len(roots)):
                act.wait_ge(s_var, n + 1)
                nc.scalar.activation(roots[n], roots[n], ACT.Sqrt).then_inc(s_root, 1)

        def center(dve, t, tmp, sums, rstd):
            link(dve, v.tensor_reduce(sums, t, AX.X, ALU.add))
            link(dve, v.tensor_scalar(sums, sums, 1.0 / DIM, None, ALU.mult))
            link(dve, v.tensor_tensor(t, t, over_features(sums), ALU.subtract))
            link(dve, v.tensor_tensor(tmp, t, t, ALU.mult))
            link(dve, v.tensor_reduce(rstd, tmp, AX.X, ALU.add))
            rsqrt(dve, rstd, 1.0 / DIM)

        def relu_times(dve, t, factor):
            link(dve, v.scalar_tensor_tensor(t, t, 0.0, over_features(factor), ALU.max, ALU.mult))

        def split_windows(dve, dst, win, rest, whole_win, chain=s_dve):
            link(dve, v.tensor_scalar(win, dst, 0.5, 1.0 / WINDOW, ALU.add, ALU.mult), chain)
            link(dve, v.tensor_copy(whole_win, win), chain)
            link(dve, v.tensor_scalar(win, whole_win, -1.0, None, ALU.add), chain)
            link(dve, v.scalar_tensor_tensor(rest, win, -float(WINDOW), dst, ALU.mult, ALU.add), chain)
            link(dve, v.scalar_tensor_tensor(win, rest, float(WINDOW), win, ALU.is_ge, ALU.add), chain)
            link(dve, v.scalar_tensor_tensor(rest, win, -float(WINDOW), dst, ALU.mult, ALU.add), chain)

        first = ExitStack()
        wcol_row = sb("wcol_row", [1, GROUP + SLOTS], I32, first)
        tile_row = sb("tile_row", [1, SLOTS], I32, first)
        ccol_row = sb("ccol_row", [1, BSLOTS], I32, first)
        src_steps = sb("src_steps", [P, SLOTS, 2], I32, first)
        dst_steps = sb("dst_steps", [P, SLOTS, 2], F32, first)
        low_steps = sb("low_steps", [P, BSLOTS, 2], F32, first)
        key_steps = sb("key_steps", [P, BSLOTS, 2], F32, first)
        keep_steps = sb("keep_steps", [P, BSLOTS + BGROUP], F32, first)

        prelude = ExitStack()
        nodes = sb("nodes", [WINDOW, WINDOWS, DIM], F32, prelude)
        spare = sb("spare", [WINDOW, WINDOWS, DIM], F32, prelude)
        step_iota = sb("step_iota", [P, BSLOTS // P], F32, prelude)
        node_id = sb("node_id", [WINDOW, WINDOWS], F32, prelude)
        lookup = sb("lookup", [WINDOW, WINDOWS + 1], F32, prelude)
        next_node = sb("next_node", [WINDOW, 2, WINDOW], F32, prelude)
        tile_of = sb("tile_of", [WINDOW, WINDOWS], F32, prelude)
        tile_of_int = sb("tile_of_int", [WINDOW, WINDOWS], I32, prelude)

        dst_all = acc[0:WINDOW, 0:HROWS].bitcast(I32)
        dst_next = acc[0:WINDOW, HROWS:2 * HROWS].bitcast(I32)
        falls = acc[0:WINDOW, 2 * HROWS:3 * HROWS]
        one_row = spare[0:1].rearrange("p w d -> p (w d)")
        last_dst, end_wide, end_rest, end_narrow, tile_iota = (
            one_row[:, k * TILES:(k + 1) * TILES] for k in range(5))
        last_int, end_int = (acc_edge[0:1, k * TILES:(k + 1) * TILES].bitcast(I32) for k in range(2))
        s_const, s_par, s_x, s_dst, s_falls, s_falls_all = sems("const", "par", "x", "dst", "falls", "falls_all")
        with nc.Block() as block:
            @block.sync
            def _(sp):
                sp.dma_start(last_int, A["dst_last"]).then_inc(s_const, 16)
                sp.dma_start(tile_iota, A["tile_iota"]).then_inc(s_const, 16)
                sp.dma_start(dst_all, A["dst"].rearrange("(p c) -> p c", p=WINDOW)).then_inc(s_dst, 16)
                sp.dma_start(dst_next, A["dst_next"].rearrange("(p c) -> p c", p=WINDOW)).then_inc(s_dst, 16)
                for n, t in (("ident", ident), ("node_iota", node_iota), ("step_iota", step_iota),
                             ("node_id", node_id), ("next_node", next_node), ("general_shift", general_shift)):
                    sp.dma_start(t[:], A[n]).then_inc(s_par, 16)
                for k, n in enumerate(ROWS):
                    sp.dma_start(rows[:, k, :], A[n].unsqueeze(0).broadcast_to([P, DIM])).then_inc(s_par, 16)
                for k, n in enumerate(MATS):
                    sp.dma_start(mats[:, k, :], A[n]).then_inc(s_par, 16)
                sp.dma_start(ew1[:], A["L1_gnn_ee_w1"]).then_inc(s_par, 16)
                for k, n in enumerate(COLPARS):
                    sp.dma_start(cols[:, k:k + 1], A[n].unsqueeze(1)).then_inc(s_par, 16)
                sp.wait_ge(s_par, 16 * (6 + len(ROWS) + len(MATS) + 1 + len(COLPARS)))

            @block.vector
            def _(dve):
                v.memset(ones[:], 1.0)
                v.memset(edge_w[:], 0.0)
                link(dve, v.memset(zeros_bf[:], 0.0))
                dve.wait_ge(s_const, 32)
                link(dve, v.tensor_copy(last_dst, last_int))
                link(dve, v.tensor_scalar(last_dst, last_dst, float(NODES - 1), None, ALU.min))
                split_windows(dve, last_dst, end_wide, end_rest, end_int)
                link(dve, v.tensor_tensor(end_wide, end_wide, tile_iota, ALU.add))
                link(dve, v.memset(end_wide[:, TILES - 1:TILES], float(STEPS - 1)))
                link(dve, v.tensor_scalar(end_int, last_int, NARROW.bit_length() - 1, None, ALU.arith_shift_right))
                link(dve, v.tensor_copy(end_narrow, end_int))
                link(dve, v.tensor_tensor(end_narrow, end_narrow, tile_iota, ALU.add))
                link(dve, v.memset(end_narrow[:, TILES - 1:TILES], float(BSTEPS - 1)))
                dve.wait_ge(s_dst, 32)
                link(dve, v.tensor_tensor(falls, dst_all, dst_next, ALU.is_gt))
                v.tensor_reduce(col[0:WINDOW, 0:1], falls, AX.X, ALU.add).then_inc(s_falls, 1)
                dve.wait_ge(s_falls_all, 1)
                v.tensor_scalar(flags[:, 0:1], bank[0][0:1, 0:1], 0.0, None, ALU.is_equal)

            @block.tensor
            def _(pe):
                pe.wait_ge(s_falls, 1)
                nc.tensor.matmul(bank[0][0:1, 0:1], col[0:WINDOW, 0:1], ones[0:WINDOW, 0:1], start=True,
                                 stop=True).then_inc(s_falls_all, 1)

        last_all, wide_all, narrow_all = (acc[:, k * TILES:(k + 1) * TILES] for k in range(3))
        compared = acc[:, 3 * TILES:4 * TILES]
        plan = ExitStack()
        WB, CB = SLOTS // P, BSLOTS // P
        t_wide = sb("t_wide", [P, WB], F32, plan)
        t_narrow = sb("t_narrow", [P, 3, CB], F32, plan)
        step_next = sb("step_next", [P, CB], F32, plan)
        step_last = sb("step_last", [P, CB], F32, plan)
        keep = sb("keep", [P, CB], F32, plan)
        w_wide = sb("w_wide", [P, WB], F32, plan)
        w_narrow = sb("w_narrow", [P, CB], F32, plan)
        wcol = sb("wcol", [P, WB], F32, plan)
        ccol = sb("ccol", [P, CB], F32, plan)
        wide_idx = sb("wide_idx", [P, WB], I32, plan)
        narrow_idx = sb("narrow_idx", [P, CB], I32, plan)
        col_int = sb("col_int", [CB, 3, P], I32, plan)
        deg_rows = acc2[0:WINDOW].rearrange("p a n -> p (a n)")[:, 4 * TILES:4 * TILES + DEGBUFS * DEGWIN * SUPER]\
            .rearrange("p (b w e) -> p b w e", b=DEGBUFS, e=SUPER)
        x_sums, x_rstd = stat[:, 0, :], stat[:, 1, :]
        feat = [sb(f"feat{k}", [WINDOW, FROWS, EDIM], F32, plan) for k in range(FBUFS)]
        pilot = sb("pilot", [WINDOW, EDIM], F32, plan)
        block_mask = sb("block_mask", [P, P], F32, plan)
        fold = sb("fold", [P, EDIM], F32, plan)
        gram = sb("gram", [P, P], F32, plan)
        gram_fold = sb("gram_fold", [P, EDIM], F32, plan)
        cov = sb("cov", [EDIM, EDIM], F32, plan)
        cov_w = sb("cov_w", [EDIM, DIM], F32, plan)
        mean_row = sb("mean_row", [1, EDIM], F32, plan)
        mean_col = sb("mean_col", [EDIM, 2], F32, plan)
        mean_cols = sb("mean_cols", [EDIM, P], F32, plan)
        scale_rows = sb("scale_rows", [BIASROW + 1, DIM], F32, plan)
        shift_rows = sb("shift_rows", [BIASROW + 1, DIM], F32, plan)
        PACK = P // EDIM
        GRAMS = FROWS // PACK
        SUMS = 4
        SUMCOLS = FROWS * EDIM // SUMS
        attr_by_part = A["edge_attr_16"].rearrange("(p c r) f -> p c r f", p=WINDOW, c=FCHUNKS)
        s_feat = [sem(f"s_feat{k}") for k in range(FBUFS)]
        s_cent, s_gram, s_gmat, s_gval, s_mask = sems("cent", "gram", "gmat", "gval", "mask")
        s_all, s_tiles, s_degused, s_shift, s_deg, s_wt, s_wturn, s_wrow, s_back = sems(
            "all", "tiles", "degused", "shift", "deg", "wt", "wturn", "wrow", "back")
        s_idx_ready = sem("s_idx_ready")
        s_degrows = [sem(f"s_degrows{k}") for k in range(DEGBUFS)]
        pieces = [(k, min(512, TILES - k)) for k in range(0, TILES, 512)]
        assert len(pieces) == 2
        with nc.Block() as block:
            @block.sync
            def _(sp):
                for n in range(FBUFS):
                    sp.dma_start(feat[n][:], attr_by_part[:, n]).then_inc(s_feat[n], 16)
                sp.dma_start(block_mask[:], A["block_mask"]).then_inc(s_mask, 16)
                sp.dma_start(fold[:], A["fold"]).then_inc(s_mask, 16)
                sp.dma_start(nodes[:], by_window(A["x"])).then_inc(s_x, 16)
                for n in range(FBUFS, FCHUNKS):
                    sp.wait_ge(s_gram, n - FBUFS + 1)
                    sp.dma_start(feat[n % FBUFS][:], attr_by_part[:, n]).then_inc(s_feat[n % FBUFS], 16)
                for n, (r, t, blocks) in enumerate(((wcol_dram, 0, WB), (ccol_dram, 1, CB), (tile_dram, 2, WB))):
                    sp.wait_ge(s_wrow, n + 1)
                    sp.dma_start(r, col_int[0:blocks, t, :]).then_inc(s_back, 16)
                sp.wait_ge(s_back, 48)
                sp.dma_start(wcol_row[:, GROUP:], wcol_dram.rearrange("j p -> (j p)").unsqueeze(0)).then_inc(s_back, 16)
                sp.dma_start(ccol_row[:], ccol_dram.rearrange("j p -> (j p)").unsqueeze(0)).then_inc(s_back, 16)
                sp.dma_start(tile_row[:], tile_dram.rearrange("j p -> (j p)").unsqueeze(0)).then_inc(s_back, 16)
                sp.wait_ge(s_back, 96)

            @block.tensor
            def _(pe):
                for n, row in enumerate((last_dst, end_wide, end_narrow)):
                    for m, (k, size) in enumerate(pieces):
                        nc.tensor.matmul(bank[2 * n + m][:, 0:size], ones[0:1, :], row[:, k:k + size], start=True,
                                         stop=True).then_inc(s_all, 1)
                pe.wait_ge(s_gval, 1)
                nc.tensor.matmul(bank[0][0:WINDOW, 0:EDIM], ones[0:WINDOW, 0:WINDOW], pilot[:], start=True,
                                 stop=True).then_inc(s_gmat, 1)
                pe.wait_ge(s_gval, 2)
                nc.tensor.matmul(bank[0][0:EDIM, 0:1], pilot[0:1, :], ones[0:1, 0:1], start=True,
                                 stop=True).then_inc(s_gmat, 1)
                for n in range(FCHUNKS):
                    pe.wait_ge(s_cent, n + 1)
                    flat = feat[n % FBUFS][:].rearrange("p r f -> p (r f)")
                    for k in range(SUMS):
                        nc.tensor.matmul(bank[2][0:1, 0:SUMCOLS], ones[0:WINDOW, 0:1],
                                         flat[:, k * SUMCOLS:(k + 1) * SUMCOLS], start=(n == k == 0),
                                         stop=(n == FCHUNKS - 1 and k == SUMS - 1))
                    for k in range(GRAMS):
                        part = flat[:, k * P:(k + 1) * P]
                        last = nc.tensor.matmul(bank[1][:, 0:P], part, part, start=(n == k == 0),
                                                stop=(n == FCHUNKS - 1 and k == GRAMS - 1))
                    last.then_inc(s_gram, 1)
                    if n == FCHUNKS * 3 // 4:
                        for n, (c, blocks) in enumerate(((wcol, WB), (ccol, CB), (t_wide, WB))):
                            pe.wait_ge(s_wt, 2)
                            nc.tensor.transpose(bank[6][0:blocks, n * P:(n + 1) * P], c[:], ident[:]).then_inc(s_wturn, 1)
                pe.wait_ge(s_shift, 1)
                nc.tensor.matmul(bank[7][0:WINDOW, 0:WINDOWS], next_node[:, 0, :], lookup[:, 0:WINDOWS],
                                 start=True, stop=False)
                nc.tensor.matmul(bank[7][0:WINDOW, 0:WINDOWS], next_node[:, 1, :], lookup[:, 1:WINDOWS + 1],
                                 start=False, stop=True).then_inc(s_deg, 1)
                pe.wait_ge(s_gval, 3)
                nc.tensor.matmul(bank[3][:, 0:EDIM], gram[:], fold[:], start=True, stop=True)
                nc.tensor.matmul(bank[5][0:EDIM, 0:1], mean_row[:], ones[0:1, 0:1], start=True, stop=True).then_inc(s_gmat, 1)
                pe.wait_ge(s_gval, 4)
                nc.tensor.matmul(bank[1][0:EDIM, 0:EDIM], fold[:], gram_fold[:], start=True, stop=True)
                nc.tensor.matmul(bank[2][0:EDIM, 0:EDIM], mean_row[:], mean_row[:], start=True,
                                 stop=True).then_inc(s_gmat, 1)
                pe.wait_ge(s_gval, 5)
                nc.tensor.matmul(bank[3][0:EDIM, 0:DIM], cov[:], ew1[:], start=True, stop=True)
                nc.tensor.matmul(bank[4][:, 0:DIM], mean_cols[:], ew1[:], start=True, stop=True).then_inc(s_gmat, 1)
                pe.wait_ge(s_gval, 6)
                nc.tensor.matmul(bank[5][:, 0:DIM], ones[0:EDIM, :], cov_w[:], start=True, stop=True).then_inc(s_gmat, 1)

            @block.vector
            def _(dve):
                for n, t in enumerate((last_all, wide_all, narrow_all)):
                    for m, (k, size) in enumerate(pieces):
                        dve.wait_ge(s_all, 2 * n + m + 1)
                        v.tensor_copy(t[:, k:k + size], bank[2 * n + m][:, 0:size])
                v.tensor_scalar(step_last[:], step_iota[:], -1.0, None, ALU.add)
                link(dve, v.tensor_scalar(step_next[:], step_iota[:], 1.0, None, ALU.add))

                def count_tiles(table, parts, x, into):
                    link(dve, v.tensor_scalar(compared[0:parts], table[0:parts], x, None, ALU.is_lt, ALU.add,
                                              accum_out=into))

                for w in range(WINDOWS):
                    count_tiles(last_all, WINDOW, node_id[:, w:w + 1], tile_of[:, w:w + 1])
                    if w == 10:
                        dve.wait_ge(s_feat[0], 16)
                        link(dve, v.tensor_reduce(pilot[:], feat[0][:].rearrange("p r f -> p f r"), AX.X, ALU.add))
                        v.tensor_scalar(pilot[:], pilot[:], 1.0 / (WINDOW * FROWS), None, ALU.mult).then_inc(s_gval, 1)
                        dve.wait_ge(s_gmat, 1)
                        v.tensor_copy(pilot[:], bank[0][0:WINDOW, 0:EDIM]).then_inc(s_gval, 1)
                        dve.wait_ge(s_gmat, 2)
                        link(dve, v.tensor_copy(mean_col[:, 0:1], bank[0][0:EDIM, 0:1]))
                link(dve, v.tensor_scalar(tile_of[:], tile_of[:], float(TILES - 1), None, ALU.min))
                v.tensor_copy(tile_of_int[:], tile_of[:]).then_inc(s_tiles, 1)
                for j in range(WB):
                    count_tiles(wide_all, P, step_iota[:, j:j + 1], t_wide[:, j:j + 1])
                link(dve, v.tensor_scalar(t_wide[:], t_wide[:], float(TILES - 1), None, ALU.min))
                link(dve, v.tensor_copy(wide_idx[:], t_wide[:]))
                link(dve, v.tensor_tensor(w_wide[:], step_iota[:, 0:WB], t_wide[:], ALU.subtract))
                link(dve, v.tensor_scalar(w_wide[:], w_wide[:], float(WINDOW), None, ALU.mult))
                v.tensor_scalar(wcol[:], w_wide[:], float((WINDOWS - 1) * WINDOW), None, ALU.min).then_inc(s_wt, 1)
                for j in range(CB):
                    count_tiles(narrow_all, P, step_iota[:, j:j + 1], t_narrow[:, 0, j:j + 1])
                    count_tiles(narrow_all, P, step_next[:, j:j + 1], t_narrow[:, 1, j:j + 1])
                    count_tiles(narrow_all, P, step_last[:, j:j + 1], t_narrow[:, 2, j:j + 1])
                link(dve, v.tensor_scalar(t_narrow[:], t_narrow[:], float(TILES - 1), None, ALU.min))
                v.tensor_copy(narrow_idx[:], t_narrow[:, 0, :]).then_inc(s_idx_ready, 1)
                link(dve, v.tensor_tensor(w_narrow[:], step_iota[:], t_narrow[:, 0, :], ALU.subtract))
                link(dve, v.tensor_tensor(keep[:], t_narrow[:, 0, :], t_narrow[:, 2, :], ALU.not_equal))
                link(dve, v.tensor_tensor(ccol[:], t_narrow[:, 1, :], t_narrow[:, 0, :], ALU.not_equal))
                link(dve, v.scalar_tensor_tensor(ccol[:], ccol[:], float(NARROWS), w_narrow[:], ALU.mult, ALU.add))
                link(dve, v.tensor_scalar(ccol[:], ccol[:], float(NARROWS), float(BLOCK), ALU.min, ALU.mult))
                v.tensor_scalar(w_narrow[:], w_narrow[:], float(NARROW), None, ALU.mult).then_inc(s_wt, 1)
                v.memset(wcol_row[:, 0:GROUP], 0)
                dve.wait_ge(s_x, 16)
                center(dve, nodes[:], spare[:], x_sums, x_rstd)
                dve.wait_ge(s_wturn, 3)
                for n, blocks in ((0, WB), (1, CB), (2, WB)):
                    v.tensor_copy(col_int[0:blocks, n, :], bank[6][0:blocks, n * P:(n + 1) * P]).then_inc(s_wrow, 1)
                for k in range(WINDOWS // DEGWIN):
                    ws = slice(k * DEGWIN, (k + 1) * DEGWIN)
                    before = deg_rows[:, k % DEGBUFS]
                    dve.wait_ge(s_degrows[k % DEGBUFS], 16 * DEGWIN * (k // DEGBUFS + 1))
                    link(dve, v.tensor_tensor(before, before.bitcast(I32), node_id[:, ws].unsqueeze(2)
                                              .broadcast_to([WINDOW, DEGWIN, SUPER]), ALU.is_lt))
                    v.tensor_reduce(lookup[:, ws], before, AX.X, ALU.add).then_inc(s_degused, 1)
                dve.wait_ge(s_degused, WINDOWS // DEGWIN)
                link(dve, v.memset(lookup[:, WINDOWS:], float(EDGES)))
                v.scalar_tensor_tensor(lookup[:, 0:WINDOWS], tile_of[:], float(SUPER), lookup[:, 0:WINDOWS],
                                       ALU.mult, ALU.add).then_inc(s_shift, 1)
                dve.wait_ge(s_deg, 1)
                link(dve, v.tensor_copy(indeg[:], bank[7][0:WINDOW, 0:WINDOWS]))
                dve.wait_ge(s_gram, FCHUNKS)
                dve.wait_ge(s_mask, 32)
                link(dve, v.tensor_reduce(mean_row[:], bank[2][0:1, 0:SUMCOLS].rearrange("p (r f) -> p f r", f=EDIM),
                                          AX.X, ALU.add))
                link(dve, v.tensor_scalar(mean_row[:], mean_row[:], 1.0 / EDGES, None, ALU.mult))
                v.tensor_tensor(gram[:], bank[1][:, 0:P], block_mask[:], ALU.mult).then_inc(s_gval, 1)
                dve.wait_ge(s_gmat, 3)
                link(dve, v.tensor_tensor(mean_col[:, 1:2], bank[5][0:EDIM, 0:1], mean_col[:, 0:1], ALU.add))
                link(dve, v.tensor_copy(mean_cols[:], mean_col[:, 1:2].broadcast_to([EDIM, P])))
                v.tensor_copy(gram_fold[:], bank[3][:, 0:EDIM]).then_inc(s_gval, 1)
                dve.wait_ge(s_gmat, 4)
                link(dve, v.tensor_copy(cov[:], bank[2][0:EDIM, 0:EDIM]))
                v.scalar_tensor_tensor(cov[:], bank[1][0:EDIM, 0:EDIM], 1.0 / EDGES, cov[:], ALU.mult,
                                       ALU.subtract).then_inc(s_gval, 1)
                dve.wait_ge(s_gmat, 5)
                v.tensor_tensor(cov_w[:], bank[3][0:EDIM, 0:DIM], ew1[:], ALU.mult).then_inc(s_gval, 1)
                dve.wait_ge(s_gmat, 6)
                r = slice(0, BIASROW + 1)
                b1, g1, bb1 = (rowpar(n, BIASROW + 1) for n in ("L1_gnn_ee_b1", "L1_gnn_ee_g1", "L1_gnn_ee_bb1"))
                link(dve, v.tensor_scalar(scale_rows[:], bank[5][r, 0:DIM], 0.0, None, ALU.max))
                rsqrt(dve, scale_rows[:], 1.0)
                link(dve, v.tensor_tensor(scale_rows[:], scale_rows[:], g1, ALU.mult))
                link(dve, v.tensor_tensor(shift_rows[:], bank[4][r, 0:DIM], b1, ALU.add))
                link(dve, v.tensor_tensor(shift_rows[:], b1, shift_rows[:], ALU.subtract))
                link(dve, v.tensor_tensor(shift_rows[:], shift_rows[:], scale_rows[:], ALU.mult))
                link(dve, v.tensor_tensor(shift_rows[:], shift_rows[:], bb1, ALU.add))
                link(dve, v.tensor_tensor(edge_w[0:EDIM, :], ew1[:], scale_rows[0:EDIM, :], ALU.mult))
                link(dve, v.tensor_copy(edge_w[BIASROW:BIASROW + 1, :], shift_rows[BIASROW:BIASROW + 1, :]))

            @block.scalar
            def _(act):
                take_roots(act, 0)

            @block.gpsimd
            def _(pool):
                def get_tiles(w):
                    k = w // DEGWIN
                    if w % DEGWIN == 0 and k >= DEGBUFS:
                        pool.wait_ge(s_degused, k - DEGBUFS + 1)
                    nc.gpsimd.indirect_dma_start(
                        deg_rows[:, k % DEGBUFS, w % DEGWIN, :].bitcast(I32), None, A["dst_tiles"],
                        bass.IndirectOffsetOnAxis(ap=tile_of_int[:, w:w + 1], axis=0)).then_inc(s_degrows[k % DEGBUFS], 16)

                pool.wait_ge(s_gval, 2)
                for n in range(FCHUNKS):
                    pool.wait_ge(s_feat[n % FBUFS], 16 * (n // FBUFS + 1))
                    nc.gpsimd.tensor_tensor(feat[n % FBUFS][:], feat[n % FBUFS][:],
                                            pilot[:].unsqueeze(1).broadcast_to([WINDOW, FROWS, EDIM]),
                                            ALU.subtract).then_inc(s_cent, 1)
                    first_window = DEGBUFS * DEGWIN - 2 * (FCHUNKS - n)
                    if first_window == 0:
                        pool.wait_ge(s_tiles, 1)
                    if first_window >= 0:
                        get_tiles(first_window)
                        get_tiles(first_window + 1)
                for w in range(DEGBUFS * DEGWIN, WINDOWS):
                    get_tiles(w)

        arena = acc2[:].rearrange("p a n -> p (a n)")
        RB = 3

        def arena_part(at, shape):
            size = 1
            for n in shape:
                size *= n
            t = arena[:, at:at + size]
            return t.rearrange("p (a b c) -> p a b c", a=shape[0], b=shape[1]), at + size

        got_rows, at = arena_part(0, (RB, 2, SUPER))
        got_rows = got_rows.bitcast(I32)
        made_rows, at = arena_part(at, (RB, 2, SUPER))
        bits_rows, at = arena_part(at, (1, 2, SUPER))
        bits_rows = bits_rows.bitcast(I32)
        keep_rows, at = arena_part(at, (RB, 1, P))
        keep_rows = keep_rows[:, :, 0, :]
        assert at <= 2 * COLS
        blocks = [("wide", j) for j in range(WB)] + [("narrow", j) for j in range(CB)]
        s_got = [sem(f"s_got{k}") for k in range(RB)]
        s_made, s_rowturn, s_rowcopy = sems("made", "rowturn", "rowcopy")
        with nc.Block() as block:
            @block.gpsimd
            def _(pool):
                for n, (kind, j) in enumerate(blocks):
                    idx_all = wide_idx if kind == "wide" else narrow_idx
                    if n >= RB:
                        pool.wait_ge(s_made, n - RB + 1)
                    nc.gpsimd.indirect_dma_start(
                        got_rows[:, n % RB].rearrange("p m e -> p (m e)"), None, A["pair_tiles"],
                        bass.IndirectOffsetOnAxis(ap=idx_all[:, j:j + 1], axis=0)).then_inc(s_got[n % RB], 16)

            @block.vector
            def _(dve):
                for n, (kind, j) in enumerate(blocks):
                    b = n % RB
                    src, dst = got_rows[:, b, 0, :], got_rows[:, b, 1, :]
                    first_out, second_out = made_rows[:, b, 0, :], made_rows[:, b, 1, :]
                    dve.wait_ge(s_got[b], 16 * (n // RB + 1))
                    if n >= RB:
                        dve.wait_ge(s_rowturn, n - RB + 1)
                    if kind == "wide":
                        v.tensor_copy(first_out, src)
                        v.tensor_scalar(second_out, dst, w_wide[:, j:j + 1], None, ALU.subtract).then_inc(s_made, 1)
                        continue
                    low, high = bits_rows[:, 0, 0, :], bits_rows[:, 0, 1, :]
                    dve.wait_ge(s_made, n)
                    link(dve, v.tensor_scalar(low, src, P - 1, None, ALU.bitwise_and))
                    link(dve, v.tensor_scalar(high, src, P.bit_length() - 1, None, ALU.arith_shift_right))
                    link(dve, v.tensor_scalar(second_out, dst, w_narrow[:, j:j + 1], None, ALU.subtract))
                    link(dve, v.scalar_tensor_tensor(first_out, second_out, -(NARROW - 1.0), second_out, ALU.add, ALU.mult))
                    link(dve, v.tensor_scalar(first_out, first_out, 0.0, FAR, ALU.is_gt, ALU.mult))
                    link(dve, v.scalar_tensor_tensor(second_out, second_out, -float(MIDDLE), first_out, ALU.add, ALU.add))
                    link(dve, v.scalar_tensor_tensor(second_out, high, float(NARROW), second_out, ALU.mult, ALU.add))
                    v.tensor_copy(keep_rows[:, b, :], keep[:, j:j + 1].broadcast_to([P, P]))
                    v.tensor_copy(first_out, low).then_inc(s_made, 1)

            @block.tensor
            def _(pe):
                for n in range(len(blocks)):
                    pe.wait_ge(s_made, n + 1)
                    if n >= 2:
                        pe.wait_ge(s_rowcopy, 2 * (n - 1))
                    for m in range(2):
                        for c in range(2):
                            last = nc.tensor.transpose(bank[n % 2][:, (2 * m + c) * P:(2 * m + c + 1) * P],
                                                       made_rows[:, n % RB, m, c * P:(c + 1) * P], ident[:])
                    if blocks[n][0] == "narrow":
                        last = nc.tensor.transpose(bank[2 + n % 2][:, 0:P], keep_rows[:, n % RB, :], ident[:])
                    last.then_inc(s_rowturn, 1)

            @block.scalar
            def _(act):
                for n, (kind, j) in enumerate(blocks):
                    act.wait_ge(s_rowturn, n + 1)
                    if kind == "narrow":
                        nc.scalar.activation(keep_steps[:, j * P:(j + 1) * P], bank[2 + n % 2][:, 0:P], ACT.Copy)
                    for m, steps in enumerate((src_steps, dst_steps) if kind == "wide" else (low_steps, key_steps)):
                        nc.scalar.activation(steps[:, j * P:(j + 1) * P, :].rearrange("p s c -> p c s"),
                                             bank[n % 2][:, 2 * m * P:2 * (m + 1) * P].rearrange("p (c s) -> p c s", c=2),
                                             ACT.Copy).then_inc(s_rowcopy, 1)
        plan.close()

        tail = ExitStack()
        hot_node = sb("hot_node", [WINDOW, 2, HCOLS, WINDOW], BF16, tail)
        hot_win = sb("hot_win", [WINDOW, 2, HCOLS, WINDOWS], BF16, tail)
        node_of = sb("node_of", [WINDOW, HROWS], BF16, tail)
        win_of = sb("win_of", [WINDOW, HROWS], BF16, tail)
        iota_bf = sb("iota_bf", [WINDOW, WINDOW], BF16, tail)
        fdst, fwin, frest, iwin = (arena[0:WINDOW, k * HROWS:(k + 1) * HROWS] for k in range(4))
        iwin = iwin.bitcast(I32)
        s_dall, s_hist_end, s_gsplit = sems("dall", "hist_end", "gsplit")
        s_hot, s_hist = ([sem(f"s_{n}{h}") for h in range(2)] for n in ("hot", "hist"))

        def is_sorted(eng):
            return eng.value_load(flags[0:1, 0:1], min_val=0, max_val=1)

        def counts_fit(eng):
            return eng.value_load(flags[0:1, 1:2], min_val=0, max_val=1)

        with nc.Block() as block:
            @block.sync
            def _(sp):
                with sp.If(is_sorted(sp) < 1):
                    sp.dma_start(iwin, A["dst"].rearrange("(p c) -> p c", p=WINDOW)).then_inc(s_dall, 16)
                    sp.wait_ge(s_dall, 16)

            @block.vector
            def _(dve):
                with dve.If(is_sorted(dve) < 1):
                    g = s_gsplit
                    dve.wait_ge(s_dall, 16)
                    link(dve, v.tensor_copy(iota_bf[:], node_iota[0:WINDOW, 0:WINDOW]), g)
                    link(dve, v.tensor_copy(fdst, iwin), g)
                    split_windows(dve, fdst, fwin, frest, iwin, g)
                    link(dve, v.tensor_copy(win_of[:], fwin), g)
                    link(dve, v.tensor_copy(node_of[:], frest), g)
                    with dve.Fori(0, HROWS // HCOLS // 2) as i:
                        for h in range(2):
                            dve.wait_ge(s_hist[h], i + 1)
                            at = bass.ds(i * (2 * HCOLS) + h * HCOLS, HCOLS)
                            v.tensor_tensor(hot_node[:, h],
                                            iota_bf[:].unsqueeze(1).broadcast_to([WINDOW, HCOLS, WINDOW]),
                                            node_of[:, at].unsqueeze(2).broadcast_to([WINDOW, HCOLS, WINDOW]),
                                            ALU.is_equal).then_inc(s_hot[h], 1)
                            v.tensor_tensor(hot_win[:, h],
                                            iota_bf[:, 0:WINDOWS].unsqueeze(1).broadcast_to([WINDOW, HCOLS, WINDOWS]),
                                            win_of[:, at].unsqueeze(2).broadcast_to([WINDOW, HCOLS, WINDOWS]),
                                            ALU.is_equal).then_inc(s_hot[h], 1)
                    dve.wait_ge(s_hist_end, 1)
                    link(dve, v.tensor_copy(indeg[:], bank[0][0:WINDOW, 0:WINDOWS]), g)

            @block.tensor
            def _(pe):
                with pe.If(is_sorted(pe) < 1):
                    degrees = bank[0][0:WINDOW, 0:WINDOWS]
                    for s in s_hist:
                        pe.sem_inc(s, 1)
                    nc.tensor.matmul(degrees, zeros_bf[0:WINDOW, 0:WINDOW], zeros_bf[0:WINDOW, 0:WINDOWS], start=True,
                                     stop=False)
                    with pe.Fori(0, HROWS // HCOLS // 2) as i:
                        for h in range(2):
                            pe.wait_ge(s_hot[h], i * 2 + 2)
                            for c in range(HCOLS):
                                last = nc.tensor.matmul(degrees, hot_node[:, h, c, :], hot_win[:, h, c, :],
                                                        start=False, stop=False)
                            last.then_inc(s_hist[h], 1)
                    nc.tensor.matmul(degrees, zeros_bf[0:WINDOW, 0:WINDOW], zeros_bf[0:WINDOW, 0:WINDOWS], start=False,
                                     stop=True).then_inc(s_hist_end, 1)
        tail.close()

        def start_layer(layer, nodes):
            s_tab, s_turned, s_copied = sems(f"tab{layer}", f"turned{layer}", f"copied{layer}")
            with nc.Block() as block:
                @block.sync
                def _(sp):
                    sp.dma_start(by_window(tables[layer]), nodes[:]).then_inc(s_tab, 16)
                    sp.wait_ge(s_tab, 16)

                @block.tensor
                def _(pe):
                    for k, ws in quads():
                        if k >= 2:
                            pe.wait_ge(s_copied, k - 1)
                        for q, w in enumerate(ws):
                            last = nc.tensor.transpose(bank[6 + k % 2][:, q * WINDOW:(q + 1) * WINDOW], nodes[:, w, :],
                                                       ident[0:WINDOW, 0:WINDOW])
                        last.then_inc(s_turned, 1)

                @block.scalar
                def _(act):
                    for k, ws in quads():
                        act.wait_ge(s_turned, k + 1)
                        nc.scalar.activation(acc[:, ws[0] * WINDOW:(ws[-1] + 1) * WINDOW],
                                             bank[6 + k % 2][:, 0:len(ws) * WINDOW], ACT.Copy).then_inc(s_copied, 1)

                @block.vector
                def _(dve):
                    if layer == 0:
                        v.memset(acc_edge, 0.0)
                    v.memset(acc[:, NODES:], 0.0)

        first_root = len(roots)
        with nc.Block() as block:
            @block.vector
            def _(dve):
                link(dve, v.tensor_scalar(dinv[:], indeg[:], 1.0, None, ALU.add))
                rsqrt(dve, dinv[:], 1.0, 0.0)
                link(dve, v.tensor_tensor(x_rstd, x_rstd, dinv[:], ALU.mult))
                relu_times(dve, nodes[:], x_rstd)

            @block.scalar
            def _(act):
                take_roots(act, first_root)
        start_layer(0, nodes)
        prelude.close()
        end_phase()

        def general_buffers(scope, layer):
            return {n: sb(f"{n}_{layer}", shape, dt, scope) for n, shape, dt in (
                ("g_src", [P, 2, 1], I32), ("g_dst", [P, 2, 1], I32), ("g_row", [P, 2, DIM], F32),
                ("g_shift", [P, 2, CHUNKS], F32), ("g_dstf", [P, 2, 1], F32), ("g_hot", [P, 2, CHUNK], F32),
                ("g_attr", [BIASROW + 1, 2, P], F32), ("g_edge", [P, 2, DIM], F32))}

        def general_pass(layer, with_edges, B):
            g_src, g_dst, g_row, g_shift, g_dstf, g_hot, g_attr, g_edge = (
                B[n] for n in ("g_src", "g_dst", "g_row", "g_shift", "g_dstf", "g_hot", "g_attr", "g_edge"))
            s_in, s_row, s_free, s_hotg = ([sem(f"s_g{n}{layer}_{h}") for h in range(2)]
                                                   for n in ("in", "row", "free", "hot"))
            s_go, s_prod, s_edge, s_sum, s_add, s_chain, s_zero = sems(*(f"g{n}{layer}" for n in (
                "go", "prod", "edge", "sum", "add", "chain", "zero")))
            loads = 3 if with_edges else 2
            PAIRS = (SLICES if with_edges else ALL_SLICES) // 2
            widths = [min(CHUNK, NODES - c * CHUNK) for c in range(CHUNKS)]

            def gpsimd(pool):
                with pool.Fori(0, PAIRS) as i:
                    for h in range(2):
                        pool.wait_ge(s_in[h], i * (16 * loads) + 16 * loads)
                        pool.sem_inc(s_go, 1)
                        nc.gpsimd.indirect_dma_start(
                            g_row[:, h, :], None, tables[layer],
                            bass.IndirectOffsetOnAxis(ap=g_src[:, h, :], axis=0)).then_inc(s_row[h], 16)

            def sync(sp):
                with sp.Fori(0, PAIRS) as i:
                    for h in range(2):
                        sp.wait_ge(s_free[h], i + 1)
                        t = i * 2 + h
                        sp.dma_start(g_src[:, h, :], A["src_slices"][bass.ds(t, 1), :].rearrange("o e -> e o"))\
                            .then_inc(s_in[h], 16)
                        sp.dma_start(g_dst[:, h, :], A["dst_slices"][bass.ds(t, 1), :].rearrange("o e -> e o"))\
                            .then_inc(s_in[h], 16)
                        if with_edges:
                            sp.dma_start(g_attr[0:EDIM, h, :], A["attr_tiles"].rearrange(
                                "t (f c e) -> t c f e", f=EDIM, c=2)[bass.ds(i, 1), h]
                                .rearrange("o f e -> f (o e)")).then_inc(s_in[h], 16)

            def tensor(pe):
                with pe.Fori(0, PAIRS) as i:
                    for h in range(2):
                        pe.wait_ge(s_row[h], i * 16 + 16)
                        if with_edges:
                            nc.tensor.matmul(bank[4 + h][:, 0:DIM], g_attr[:, h, :], edge_w[:], start=True,
                                             stop=True).then_inc(s_prod, 1)
                            pe.wait_ge(s_edge, i * 2 + (h + 1))
                        for c, width in enumerate(widths):
                            n = CHUNKS * h + c
                            pe.wait_ge(s_hotg[n % 2], i * CHUNKS + (n // 2 + 1))
                            last = nc.tensor.matmul(bank[n % 2][:, 0:width], g_row[:, h, :], g_hot[:, n % 2, 0:width],
                                                    start=True, stop=True)
                            if with_edges:
                                last = nc.tensor.matmul(bank[2 + n % 2][:, 0:width], g_edge[:, h, :],
                                                        g_hot[:, n % 2, 0:width], start=True, stop=True)
                            last.then_inc(s_sum, 1)

            def scalar(act):
                if with_edges:
                    with act.Fori(0, PAIRS) as i:
                        for h in range(2):
                            act.wait_ge(s_prod, i * 2 + (h + 1))
                            nc.scalar.activation(g_edge[:, h, :], bank[4 + h][:, 0:DIM], ACT.Relu).then_inc(s_edge, 1)

            def vector(dve):
                for s in s_free:
                    dve.sem_inc(s, 1)
                if not with_edges:
                    v.memset(acc, 0.0).then_inc(s_zero, 1)
                    dve.wait_ge(s_zero, 1)
                with dve.Fori(0, PAIRS) as i:
                    for h in range(2):
                        dve.wait_ge(s_in[h], i * (16 * loads) + 16 * loads)
                        v.tensor_copy(g_dstf[:, h, :], g_dst[:, h, :]).then_inc(s_chain, 1)
                        dve.wait_ge(s_chain, i * 4 + (2 * h + 1))
                        v.tensor_scalar(g_shift[:, h, :], general_shift[:], g_dstf[:, h, :], None,
                                        ALU.add).then_inc(s_chain, 1)
                        dve.wait_ge(s_chain, i * 4 + (2 * h + 2))
                        for c, width in enumerate(widths):
                            n = CHUNKS * h + c
                            v.tensor_scalar(g_hot[:, n % 2, 0:width], node_iota[:, 0:width], g_shift[:, h, c:c + 1],
                                            None, ALU.is_equal).then_inc(s_hotg[n % 2], 1)
                            dve.wait_ge(s_sum, i * (2 * CHUNKS) + (n + 1))
                            part = acc[:, c * CHUNK:c * CHUNK + width]
                            last = v.tensor_tensor(part, part, bank[n % 2][:, 0:width], ALU.add)
                            if with_edges:
                                part = acc_edge[:, c * CHUNK:c * CHUNK + width]
                                last = v.tensor_tensor(part, part, bank[2 + n % 2][:, 0:width], ALU.add)
                            last.then_inc(s_add, 1)
                            dve.wait_ge(s_add, i * (2 * CHUNKS) + (n + 1))
                        dve.sem_inc(s_free[h], 1)

            return dict(gpsimd=gpsimd, sync=sync, tensor=tensor, scalar=scalar, vector=vector)

        tail = ExitStack()
        B = general_buffers(tail, 0)
        idx = sb("idx", [P, 2, 2 * GROUP], I32, tail)
        msg = sb("msg", [P, 2, 2 * GROUP, DIM], F32, tail)
        onehot = sb("onehot", [P, 2, 2 * GROUP, WINDOW], F32, tail)
        attr_ring = sb("attr_ring", [BIASROW + 1, 2, GROUP, SUPER], F32, tail)
        edge_msg = sb("edge_msg", [P, 2 * GROUP, DIM], F32, tail)
        hot_low = sb("hot_low", [P, RING, 2, P], BF16, tail)
        hot_key = sb("hot_key", [P, RING, 2, BLOCK], BF16, tail)
        staged = sb("staged", [P, 2, BGROUP, BLOCK], F8, tail)
        key_iota = sb("key_iota", [P, BLOCK], BF16, tail)
        low_iota = sb("low_iota", [P, P], BF16, tail)
        ident_bf = sb("ident_bf", [P, P], BF16, tail)
        hot_keep = sb("hot_keep", [P, 2, BGROUP, P], BF16, tail)
        with nc.Block() as block:
            @block.vector
            def _(dve):
                v.memset(attr_ring[:], 1.0)
                v.memset(B["g_attr"][:], 1.0)
                v.memset(staged[:, 1, BGROUP - 1, :].bitcast(U8), 0)
                v.memset(keep_steps[:, BSLOTS:], 0.0)
                v.tensor_copy(ident_bf[:], ident[:])
                v.tensor_copy(low_iota[:], node_iota[:, 0:P])
                v.tensor_scalar(key_iota[:], node_iota[:, 0:BLOCK], -float(MIDDLE), None, ALU.add)

        s_used, s_gather, s_attr_in, s_out = ([sem(f"s_{n}1_{h}") for h in range(2)]
                                              for n in ("used", "gather", "attr_in", "out"))
        s_idx, s_go, s_prod, s_emsg, s_eused, s_onehot, s_taken, s_add, s_hotb, s_run, s_copy, s_copygo, s_keepgo = sems(
            "idx1", "go1", "prod1", "emsg1", "eused1", "onehot1", "taken1", "add1", "hotb", "run", "copy",
            "copygo", "keepgo")
        general = general_pass(0, True, B)
        with nc.Block() as block:
            @block.gpsimd
            def _(pool):
                with pool.If(is_sorted(pool) > 0):
                    with pool.Fori(0, ITERS) as i:
                        for h in range(2):
                            pool.wait_ge(s_used[h], i + 1)
                            nc.gpsimd.tensor_copy(
                                idx[:, h, :], src_steps[:, bass.ds(i * (2 * GROUP) + h * GROUP, GROUP), :]
                                .rearrange("p s c -> p (s c)")).then_inc(s_idx, 1)
                            pool.wait_ge(s_idx, i * 2 + (h + 1))
                            pool.sem_inc(s_go, 1)
                            for k in range(2 * GROUP):
                                nc.gpsimd.indirect_dma_start(
                                    msg[:, h, k, :], None, tables[0],
                                    bass.IndirectOffsetOnAxis(ap=idx[:, h, k:k + 1], axis=0)
                                ).then_inc(s_gather[h], 16)
                with pool.Else():
                    general["gpsimd"](pool)

            @block.sync
            def _(sp):
                def load_features(h, tiles):
                    for s, tile in enumerate(tiles):
                        sp.dma_start(attr_ring[0:EDIM, h, s, :], A["attr_tiles"][bass.ds(tile, 1), :]
                                     .rearrange("o (f e) -> f (o e)", f=EDIM)).then_inc(s_attr_in[h], 16)

                with sp.If(is_sorted(sp) > 0):
                    tile_regs = [sp.alloc_register(f"tile_{k}") for k in range(2 * GROUP)]
                    sp.reg_load(tile_regs[:GROUP], tile_row[0:1, 0:GROUP])
                    load_features(0, [sp.snap(r, min_val=0, max_val=TILES - 1) for r in tile_regs[:GROUP]])
                    regs = [sp.alloc_register(f"ccol_{k}") for k in range(BGROUP)]
                    with sp.Fori(0, ITERS) as i:
                        sp.reg_load(tile_regs, tile_row[0:1, bass.ds(i * (2 * GROUP) + GROUP, 2 * GROUP)])
                        for h in range(2):
                            tiles = [sp.snap(r, min_val=0, max_val=TILES - 1)
                                     for r in tile_regs[h * GROUP:(h + 1) * GROUP]]
                            sp.reg_load(regs, ccol_row[0:1, bass.ds(i * (2 * BGROUP) + h * BGROUP, BGROUP)])
                            sp.wait_ge(s_prod, i * 4 + (2 * h + 1))
                            load_features(1 - h, tiles)
                            for k in range(BGROUP):
                                to = sp.snap(regs[k], min_val=0, max_val=NARROWS * BLOCK)
                                window_ends = sp.snap(to < NARROWS * BLOCK)
                                sp.wait_ge(s_copy, i * (2 * BGROUP) + (h * BGROUP + k + 2))
                                sp.dma_start(counts[:, bass.ds(to, BLOCK)], staged[:, h, k, :].bitcast(U8),
                                             cond=window_ends).then_inc(s_out[h], 16)
                    for h in range(2):
                        sp.wait_ge(s_out[h], ITERS * BGROUP * 16 + 1)
                    sp.wait_ge(s_attr_in[0], (ITERS + 1) * GROUP * 16)
                with sp.Else():
                    general["sync"](sp)

            @block.scalar
            def _(act):
                with act.If(is_sorted(act) > 0):
                    for s, n in ((s_emsg, 2), (s_out[0], 1), (s_out[1], 1)):
                        act.sem_inc(s, n)

                    def make_keep(h, k, step):
                        return nc.scalar.activation(hot_keep[:, h, k, :], ident_bf[:], ACT.Copy,
                                                    scale=keep_steps[:, step])

                    for k in range(BGROUP):
                        last = make_keep(0, k, slice(k, k + 1))
                    last.then_inc(s_copy, 1)
                    with act.Fori(0, ITERS) as i:
                        for h in range(2):
                            act.wait_ge(s_out[h], i * (BGROUP * 16) + 1)
                            for k in range(BGROUP):
                                n = h * BGROUP + k + 1
                                act.wait_ge(s_run, i * (2 * BGROUP) + (n + RING))
                                act.sem_inc(s_copygo, 1)
                                nc.scalar.activation(staged[:, h, k, :], bank[k % 2][:, 0:BLOCK], ACT.Copy,
                                                     saturate=True).then_inc(s_copy, 1)
                                for to in KEEPS[k]:
                                    make_keep(1 - h, to, bass.ds(i * (2 * BGROUP) + ((h + 1) * BGROUP + to), 1))
                                if k in (2, 4):
                                    q = k // 2 - 1
                                    act.wait_ge(s_prod, i * 4 + (2 * h + q + 2))
                                    act.wait_ge(s_eused, i * 4 + (2 * h + q + 1))
                                    nc.scalar.activation(
                                        edge_msg[:, 4 * q:4 * q + 4, :].rearrange("p k d -> p (k d)"),
                                        bank[2 + q][:, :], ACT.Relu).then_inc(s_emsg, 1)
                with act.Else():
                    general["scalar"](act)

            @block.tensor
            def _(pe):
                def add_counts(i, h, k, between):
                    n = h * BGROUP + k + 1
                    pe.wait_ge(s_hotb, i * (2 * BGROUP) + n)
                    for c in range(2):
                        nc.tensor.matmul(bank[k % 2][:, 0:BLOCK], hot_low[:, k % RING, c, :],
                                         hot_key[:, k % RING, c, :], start=(c == 0), stop=False)
                    for work, step, c in between:
                        work(i, h, step, c)
                    pe.wait_ge(s_copy, i * (2 * BGROUP) + n)
                    pe.sem_inc(s_keepgo, 1)
                    before = staged[:, h, k - 1, :] if k else staged[:, 1 - h, BGROUP - 1, :]
                    nc.tensor.matmul(bank[k % 2][:, 0:BLOCK], hot_keep[:, h, k, :], before, start=False,
                                     stop=True).then_inc(s_run, 1)

                def feature_product(i, h, step, c):
                    q, k = step // 2, 2 * (step % 2) + c
                    if step == c == 0:
                        pe.wait_ge(s_attr_in[h], i * (16 * GROUP) + 16 * GROUP)
                    if k == 0:
                        pe.wait_ge(s_emsg, i * 4 + (2 * h + q + 1))
                    last = nc.tensor.matmul(bank[2 + q][:, k * P:(k + 1) * P],
                                            attr_ring[:, h, step, c * P:(c + 1) * P], edge_w[:],
                                            start=True, stop=True)
                    if k == 3:
                        last.then_inc(s_prod, 1)

                def sum_slice(lhs, h, step, c, is_message):
                    at = (2 * (step % 2) + is_message) * WINDOW
                    return nc.tensor.matmul(bank[4 + 2 * h + step // 2][:, at:at + WINDOW], lhs[:, 2 * step + c, :],
                                            onehot[:, h, 2 * step + c, :], start=(c == 0), stop=(c == 1))

                def sum_rows(i, h, step, c):
                    if step == c == 0:
                        pe.wait_ge(s_gather[h], i * (32 * GROUP) + 32 * GROUP)
                        pe.wait_ge(s_onehot, i * 2 + (h + 1))
                        pe.wait_ge(s_taken, i * 2 + (h + 1))
                    last = sum_slice(msg[:, h], h, step, c, 0)
                    if (step, c) == (GROUP - 1, 1):
                        last.then_inc(s_used[h], 1)

                def sum_messages(i, h, step, c):
                    if step % 2 == c == 0:
                        pe.wait_ge(s_emsg, i * 4 + (2 * h + step // 2 + 3))
                    last = sum_slice(edge_msg, h, step, c, 1)
                    if step % 2 == c == 1:
                        last.then_inc(s_eused, 1)

                products = [(work, step, c) for work in (feature_product, sum_rows, sum_messages)
                            for step in range(GROUP) for c in range(2)]
                SHARE = len(products) // BGROUP

                with pe.If(is_sorted(pe) > 0):
                    for s, n in ((s_used[0], 1), (s_used[1], 1), (s_prod, 1), (s_run, RING)):
                        pe.sem_inc(s, n)
                    for b in range(2):
                        nc.tensor.matmul(bank[6 + b][:, 0:4 * WINDOW], zeros_bf[:, 0:P], zeros_bf[:], start=True,
                                         stop=True).then_inc(s_eused, 1)
                    with pe.Fori(0, ITERS) as i:
                        for h in range(2):
                            for k in range(BGROUP):
                                add_counts(i, h, k, products[k * SHARE:(k + 1) * SHARE])
                with pe.Else():
                    general["tensor"](pe)

            @block.vector
            def _(dve):
                def make_onehot(h, steps):
                    v.tensor_tensor(
                        onehot[:, h], node_iota[:, 0:WINDOW].unsqueeze(1).broadcast_to([P, 2 * GROUP, WINDOW]),
                        dst_steps[:, steps, :].rearrange("p s c -> p (s c)").unsqueeze(2)
                        .broadcast_to([P, 2 * GROUP, WINDOW]), ALU.is_equal).then_inc(s_onehot, 1)

                def make_count_onehots(i, h, k):
                    dve.wait_ge(s_run, i * (2 * BGROUP) + (h * BGROUP + k + 1))
                    step = i * (2 * BGROUP) + (h * BGROUP + k)
                    for c in range(2):
                        v.tensor_scalar(hot_low[:, k % RING, c, :], low_iota[:],
                                        low_steps[:, bass.ds(step, 1), c], None, ALU.is_equal)
                        last = v.tensor_scalar(hot_key[:, k % RING, c, :], key_iota[:],
                                               key_steps[:, bass.ds(step, 1), c], None, ALU.is_equal)
                    last.then_inc(s_hotb, 1)

                def add_sum(done, h, step, at):
                    part = acc2[:, :, bass.ds(at, WINDOW)]
                    dve.wait_ge(s_add, done + (step + 1))
                    v.tensor_tensor(part, part, bank[4 + 2 * h + step // 2][:, 2 * (step % 2) * WINDOW:
                                                                            (2 * (step % 2) + 2) * WINDOW]
                                    .rearrange("p (a n) -> p a n", a=2), ALU.add).then_inc(s_add, 1)

                with dve.If(is_sorted(dve) > 0):
                    for s in (s_add, s_taken):
                        dve.sem_inc(s, 1)
                    make_onehot(0, slice(0, GROUP))
                    regs = [dve.alloc_register(f"wcol_{k}") for k in range(2 * GROUP)]
                    with dve.Fori(0, ITERS) as i:
                        dve.reg_load(regs, wcol_row[0:1, bass.ds(i * (2 * GROUP), 2 * GROUP)])
                        at = [dve.snap(r, min_val=0, max_val=NODES - WINDOW) for r in regs]
                        for h in range(2):
                            for k in range(4):
                                make_count_onehots(i, h, k)
                            dve.wait_ge(s_eused, i * 4 + (2 * h + 2))
                            for k in range(GROUP):
                                add_sum(i * (2 * GROUP) + h * GROUP, 1 - h, k, at[h * GROUP + k])
                                if k < GROUP - 1:
                                    make_count_onehots(i, h, 4 + k)
                            dve.wait_ge(s_add, i * (2 * GROUP) + (h * GROUP + GROUP + 1))
                            dve.sem_inc(s_taken, 1)
                            make_onehot(1 - h, bass.ds(i * (2 * GROUP) + (h + 1) * GROUP, GROUP))
                            make_count_onehots(i, h, BGROUP - 1)
                    dve.reg_load(regs[:GROUP], wcol_row[0:1, ITERS * 2 * GROUP:ITERS * 2 * GROUP + GROUP])
                    dve.wait_ge(s_eused, ITERS * 4 + 2)
                    for k in range(GROUP):
                        add_sum(ITERS * 2 * GROUP, 1, k, dve.snap(regs[k], min_val=0, max_val=NODES - WINDOW))
                with dve.Else():
                    general["vector"](dve)
        tail.close()
        first.close()
        end_phase()

        def dense_pass(layer):
            tail = ExitStack()
            raw = [sb(f"raw{h}_{layer}", [P, GWIN * BLOCK], U8, tail) for h in range(2)]
            packed = sb(f"packed_{layer}", [P, 2, SRCS, GCOLS], U8, tail)
            table = sb(f"table_sb{layer}", [P, SRCS, DIM], F32, tail)
            parts = sb(f"parts{layer}", [P, SRCS, 3, DIM], BF16, tail)
            rest = sb(f"rest{layer}", [P, 2, SPLIT, DIM], F32, tail)
            top = sb(f"top{layer}", [P, GROUPS + 1], F32, tail)
            s_raw = [sem(f"s_raw{h}_{layer}") for h in range(2)]
            s_looked, s_pad, s_high, s_mid, s_left, s_parts, s_packed, s_summed, s_into, s_go, s_start, s_top, s_topt = sems(
                *(f"{n}{layer}" for n in ("looked", "pad", "high", "mid", "left", "parts", "packed", "summed", "into",
                                          "dense_go", "sum_start", "top", "topt")))
            pieces = [slice(k, k + SPLIT) for k in range(0, SRCS, SPLIT)]
            assert SRCS % SPLIT == 0
            s_table = [sem(f"s_table{k}_{layer}") for k in range(len(pieces))]
            PAIRS = (GROUPS - 1) // 2
            whole_rows = (NODES // P) * P
            assert GROUPS % 2 == 1
            goes = is_sorted if layer == 1 else counts_fit

            with nc.Block() as block:
                @block.sync
                def _(sp):
                    with sp.If(goes(sp) > 0):
                        for k, ss in enumerate(pieces):
                            full = min(ss.stop, NODES // P)
                            sp.dma_start(table[:, ss.start:full, :], tables[layer][ss.start * P:full * P, :]
                                         .rearrange("(s p) d -> p s d", p=P)).then_inc(s_table[k], 16)
                            if k == 0:
                                sp.dma_start(raw[0][:], counts[:, 0:GWIN * BLOCK]).then_inc(s_raw[0], 16)
                        sp.wait_ge(s_pad, 1)
                        sp.dma_start(table[0:NODES - whole_rows, SRCS - 1, :], tables[layer][whole_rows:, :])\
                            .then_inc(s_table[-1], 16)
                        with sp.Fori(0, PAIRS) as i:
                            for b in (1, 0):
                                start = i * (2 * GWIN * BLOCK) + (2 - b) * GWIN * BLOCK
                                sp.wait_ge(s_packed, i * 2 + (2 - b))
                                sp.sem_inc(s_go, 1)
                                sp.dma_start(raw[b][:], counts[:, bass.ds(start, GWIN * BLOCK)]).then_inc(s_raw[b], 16)

                @block.scalar
                def _(act):
                    with act.If(goes(act) > 0):
                        for k, ss in enumerate(pieces):
                            act.wait_ge(s_table[k], 16 if ss.stop < SRCS else 32)
                            nc.scalar.activation(parts[:, ss, 0, :], table[:, ss, :], ACT.Copy).then_inc(s_high, 1)
                            if k:
                                act.wait_ge(s_left, k)
                                before = pieces[k - 1]
                                nc.scalar.activation(parts[:, before, 1, :], rest[:, (k - 1) % 2],
                                                     ACT.Copy).then_inc(s_mid, 1)
                        act.wait_ge(s_left, len(pieces))
                        nc.scalar.activation(parts[:, pieces[-1], 1, :], rest[:, (len(pieces) - 1) % 2],
                                             ACT.Copy).then_inc(s_mid, 1)

                @block.vector
                def _(dve):
                    def pack(g, b):
                        if g is not None:
                            dve.wait_ge(s_summed, g)
                            if layer == 1:
                                dve.wait_ge(s_looked, g)
                        v.tensor_copy(packed[:, b].bitcast(I32).rearrange("p s (u n) -> p s u n", u=GWIN),
                                      raw[b][:].bitcast(I32).rearrange("p (u s n) -> p s u n", u=GWIN, s=SRCS))\
                            .then_inc(s_packed, 1)

                    def look(g, b):
                        if layer == 1:
                            dve.wait_ge(s_packed, g + 2)
                            v.tensor_reduce(top[:, bass.ds(g + 1, 1)], packed[:, b].rearrange("p s c -> p (s c)"), AX.X,
                                            ALU.max).then_inc(s_looked, 1)

                    def add_group(g, b):
                        dve.wait_ge(s_summed, g + 2)
                        part = acc[:, bass.ds(g * GCOLS, GCOLS)]
                        v.tensor_tensor(part, part, bank[b][:, 0:GCOLS], ALU.add).then_inc(s_into, 1)

                    with dve.If(goes(dve) > 0):
                        v.memset(table[P - 32:, SRCS - 1, :], 0.0).then_inc(s_pad, 1)
                        dve.sem_inc(s_packed, 1)
                        dve.sem_inc(s_into, 1)
                        dve.sem_inc(s_looked, 1)
                        for k, ss in enumerate(pieces):
                            if k >= 2:
                                dve.wait_ge(s_parts, k - 1)
                            dve.wait_ge(s_high, k + 1)
                            v.tensor_tensor(rest[:, k % 2], table[:, ss, :], parts[:, ss, 0, :],
                                            ALU.subtract).then_inc(s_left, 1)
                            if k:
                                before = pieces[k - 1]
                                dve.wait_ge(s_mid, k)
                                v.tensor_tensor(parts[:, before, 2, :], rest[:, (k - 1) % 2], parts[:, before, 1, :],
                                                ALU.subtract).then_inc(s_parts, 1)
                            if k == 0:
                                dve.wait_ge(s_raw[0], 16)
                                pack(None, 0)
                        dve.wait_ge(s_mid, len(pieces))
                        v.tensor_tensor(parts[:, pieces[-1], 2, :], rest[:, (len(pieces) - 1) % 2],
                                        parts[:, pieces[-1], 1, :], ALU.subtract).then_inc(s_parts, 1)
                        with dve.Fori(0, PAIRS) as i:
                            dve.wait_ge(s_raw[1], i * 16 + 16)
                            pack(i * 2 + 1, 1)
                            look(i * 2, 0)
                            add_group(i * 2, 0)
                            dve.wait_ge(s_raw[0], i * 16 + 32)
                            pack(i * 2 + 2, 0)
                            look(i * 2 + 1, 1)
                            add_group(i * 2 + 1, 1)
                        look(GROUPS - 1, 0)
                        dve.wait_ge(s_summed, GROUPS + 1)
                        part = acc[:, (GROUPS - 1) * GCOLS:]
                        v.tensor_tensor(part, part, bank[0][:, 0:GCOLS], ALU.add).then_inc(s_into, 1)
                        if layer == 1:
                            dve.wait_ge(s_into, GROUPS + 1)
                            v.tensor_reduce(top[:, 0:1], top[:, 1:], AX.X, ALU.max).then_inc(s_top, 1)
                            dve.wait_ge(s_topt, 1)
                            v.tensor_reduce(col[0:1, 0:1], bank[2][0:1, 0:P], AX.X, ALU.max).then_inc(s_top, 1)
                            dve.wait_ge(s_top, 2)
                            v.tensor_scalar(flags[:, 1:2], col[0:1, 0:1], float(F8_15), None, ALU.is_le)
                    if layer == 1:
                        with dve.Else():
                            v.memset(flags[:, 1:2], 0)

                @block.tensor
                def _(pe):
                    def sum_group(b, first=False):
                        counts_8 = packed[:, b].bitcast(F8)
                        for s in range(SRCS):
                            if first and s % SPLIT == 0:
                                pe.wait_ge(s_parts, s // SPLIT + 1)
                            for part in range(3):
                                last = nc.tensor.matmul(bank[b][:, 0:GCOLS], parts[:, s, part, :], counts_8[:, s, :],
                                                        start=(s == part == 0), stop=(s == SRCS - 1 and part == 2))
                        last.then_inc(s_summed, 1)

                    with pe.If(goes(pe) > 0):
                        pe.sem_inc(s_summed, 1)
                        pe.wait_ge(s_packed, 2)
                        sum_group(0, first=True)
                        with pe.Fori(0, PAIRS) as i:
                            for b in (1, 0):
                                pe.wait_ge(s_packed, i * 2 + (4 - b))
                                pe.wait_ge(s_into, i * 2 + (2 - b))
                                pe.sem_inc(s_start, 1)
                                sum_group(b)
                        if layer == 1:
                            pe.wait_ge(s_top, 1)
                            nc.tensor.transpose(bank[2][0:1, 0:P], top[:, 0:1], ident[:]).then_inc(s_topt, 1)
            tail.close()

            tail = ExitStack()
            general = general_pass(layer, False, general_buffers(tail, layer))
            with nc.Block() as block:
                @block.sync
                def _(sp):
                    with sp.If(counts_fit(sp) < 1):
                        general["sync"](sp)

                @block.gpsimd
                def _(pool):
                    with pool.If(counts_fit(pool) < 1):
                        general["gpsimd"](pool)

                @block.vector
                def _(dve):
                    with dve.If(counts_fit(dve) < 1):
                        general["vector"](dve)

                @block.tensor
                def _(pe):
                    with pe.If(counts_fit(pe) < 1):
                        general["tensor"](pe)
            tail.close()
            end_phase()

        def gcn_nodes(layer, nodes, spare, x_rows, edge_bias):
            b, g, be = (rowpar(f"L0_gnn_{n}{layer + 1}") for n in ("b", "g", "be"))
            s_prod, s_took, s_sums, s_total, s_mean, s_x1, s_x1_out, s_ready = (
                sem(f"s_{n}_gcn{layer}") for n in ("prod", "took", "sums", "total", "mean", "x1", "x1_out", "ready"))
            first_root = len(roots)
            with nc.Block() as block:
                @block.tensor
                def _(pe):
                    for k, ws in quads():
                        if k >= 2:
                            pe.wait_ge(s_took, ws[0] - QUAD)
                        for q, w in enumerate(ws):
                            nc.tensor.matmul(bank[k % 2][0:WINDOW, q * DIM:(q + 1) * DIM],
                                             acc[:, w * WINDOW:(w + 1) * WINDOW], mats[:, layer, :],
                                             start=True, stop=True).then_inc(s_prod, 1)
                    for n in range(2):
                        pe.wait_ge(s_sums, n + 1)
                        nc.tensor.matmul(bank[2][0:WINDOW, n:n + 1], ones[0:WINDOW, 0:WINDOW], col[0:WINDOW, n:n + 1],
                                         start=True, stop=True).then_inc(s_total, 1)

                @block.vector
                def _(dve):
                    flat = nodes[:].rearrange("p w d -> p (w d)")
                    for w in range(WINDOWS):
                        dve.wait_ge(s_prod, min((w // QUAD + 1) * QUAD, WINDOWS))
                        v.scalar_tensor_tensor(nodes[:, w, :],
                                               bank[w // QUAD % 2][0:WINDOW, (w % QUAD) * DIM:(w % QUAD + 1) * DIM],
                                               dinv[:, w:w + 1], b, ALU.mult, ALU.add).then_inc(s_took, 1)
                    dve.wait_ge(s_took, WINDOWS)
                    v.tensor_reduce(col[0:WINDOW, 0:1], flat, AX.X, ALU.add).then_inc(s_sums, 1)
                    dve.wait_ge(s_total, 1)
                    mean, rstd = col[0:WINDOW, 2:3], col[0:WINDOW, 3:4]
                    link(dve, v.tensor_scalar(mean, bank[2][0:WINDOW, 0:1], 1.0 / (NODES * DIM), None, ALU.mult))
                    v.tensor_scalar(col[0:WINDOW, 4:5], mean, -1.0, None, ALU.mult).then_inc(s_mean, 1)
                    dve.wait_ge(s_total, 2)
                    link(dve, v.tensor_copy(rstd, bank[2][0:WINDOW, 1:2]))
                    rsqrt(dve, rstd, 1.0 / (NODES * DIM))
                    link(dve, v.scalar_tensor_tensor(nodes[:], nodes[:], mean, over_windows(g), ALU.subtract, ALU.mult))
                    link(dve, v.scalar_tensor_tensor(nodes[:], nodes[:], rstd, over_windows(be), ALU.mult, ALU.add))
                    if layer == 0:
                        link(dve, v.scalar_tensor_tensor(nodes[:], nodes[:], 0.0, over_features(dinv[:]),
                                                                ALU.max, ALU.mult))
                    else:
                        dve.wait_ge(s_x1, 16)
                        link(dve, v.scalar_tensor_tensor(nodes[:], nodes[:], 0.0, x_rows[:], ALU.max, ALU.add))
                        dve.sem_inc(s_ready, 1)
                        dve.wait_ge(s_x1_out, 16)
                        center(dve, nodes[:], spare[:], stat[:, 0, :], stat[:, 1, :])
                        relu_times(dve, nodes[:], stat[:, 1, :])

                @block.scalar
                def _(act):
                    act.wait_ge(s_mean, 1)
                    nc.scalar.activation(spare[:], nodes[:], ACT.Square, bias=col[0:WINDOW, 4:5],
                                         accum_out=col[0:WINDOW, 1:2]).then_inc(s_sums, 1)
                    take_roots(act, first_root)

                if layer == 1:
                    @block.gpsimd
                    def _(pool):
                        nc.gpsimd.tensor_tensor(edge_bias[:], over_windows(rowpar("L1_gnn_ee_b2")),
                                                over_features(indeg[:]), ALU.mult)

                    @block.sync
                    def _(sp):
                        sp.dma_start(x_rows[:], by_window(A["x"])).then_inc(s_x1, 16)
                        sp.wait_ge(s_ready, 1)
                        sp.dma_start(by_window(x1_dram), nodes[:]).then_inc(s_x1_out, 16)
                        sp.wait_ge(s_x1_out, 16)

        def add_edges(nodes, edge_bias):
            s_prod, s_took = sem("s_prod_edges"), sem("s_took_edges")
            with nc.Block() as block:
                @block.tensor
                def _(pe):
                    for k, ws in quads():
                        if k >= 2:
                            pe.wait_ge(s_took, ws[0] - QUAD)
                        for q, w in enumerate(ws):
                            nc.tensor.matmul(bank[k % 2][0:WINDOW, q * DIM:(q + 1) * DIM],
                                             acc_edge[:, w * WINDOW:(w + 1) * WINDOW], mats[:, MATS.index("L1_gnn_ee_w2"), :],
                                             start=True, stop=True).then_inc(s_prod, 1)

                @block.vector
                def _(dve):
                    link(dve, v.tensor_tensor(nodes[:], nodes[:], edge_bias[:], ALU.add))
                    for k, ws in quads():
                        dve.wait_ge(s_prod, ws[-1] + 1)
                        part = nodes[:, ws[0]:ws[-1] + 1, :]
                        v.tensor_tensor(part, part, bank[k % 2][0:WINDOW, 0:len(ws) * DIM]
                                        .rearrange("p (w d) -> p w d", d=DIM), ALU.add).then_inc(s_took, len(ws))
                    dve.wait_ge(s_took, WINDOWS)

        def gin_mlp(n):
            s_prod, s_took, s_mean, s_square, s_scale = sems(*(f"{m}_mlp{n}" for m in (
                "prod", "took", "mean", "square", "scale")))
            w = mats[:, MATS.index(f"L1_gnn_mlp_w{n}"), :]
            b, g, bb = (cols[:, k:k + 1] for k in range(3 * n - 3, 3 * n))
            pieces = range(0, NODES, WIDE)
            z, y = acc[:, 0:NODES], acc_edge[:, 0:NODES]
            total, mean, variance, scale, shift = (col[:, k:k + 1] for k in range(5))
            first_root = len(roots)
            with nc.Block() as block:
                @block.tensor
                def _(pe):
                    for k, at in enumerate(pieces):
                        m = min(WIDE, NODES - at)
                        if k >= 4:
                            pe.wait_ge(s_took, k - 3)
                        nc.tensor.matmul(bank[k % 4][:, 0:m], w, z[:, at:at + m], start=True,
                                         stop=True).then_inc(s_prod, 1)

                @block.vector
                def _(dve):
                    dve.wait_ge(s_took, len(pieces))
                    link(dve, v.tensor_reduce(total, piece_sums[:], AX.X, ALU.add))
                    v.tensor_scalar(mean, total, -1.0 / NODES, None, ALU.mult).then_inc(s_mean, 1)
                    dve.wait_ge(s_square, 1)
                    rsqrt(dve, variance, 1.0 / NODES)
                    link(dve, v.tensor_tensor(scale, variance, g, ALU.mult))
                    v.scalar_tensor_tensor(shift, mean, scale, bb, ALU.mult, ALU.add).then_inc(s_scale, 1)

                @block.scalar
                def _(act):
                    for k, at in enumerate(pieces):
                        m = min(WIDE, NODES - at)
                        act.wait_ge(s_prod, k + 1)
                        nc.scalar.activation(y[:, at:at + m], bank[k % 4][:, 0:m], ACT.Identity, bias=b,
                                             accum_out=piece_sums[:, k:k + 1]).then_inc(s_took, 1)
                    act.wait_ge(s_mean, 1)
                    nc.scalar.activation(z, y, ACT.Square, bias=mean, accum_out=variance).then_inc(s_square, 1)
                    take_roots(act, first_root)
                    act.wait_ge(s_scale, 1)
                    nc.scalar.activation(z, y, ACT.Relu, scale=scale, bias=shift)

        def finish(nodes):
            s_x1, s_turned, s_added, s_out = (sem(f"s_{n}_end") for n in ("x1", "turned", "added", "out"))
            with nc.Block() as block:
                @block.sync
                def _(sp):
                    sp.dma_start(nodes[:], by_window(x1_dram)).then_inc(s_x1, 16)
                    parts = 5
                    for k in range(parts):
                        ws = slice(k * WINDOWS // parts, (k + 1) * WINDOWS // parts)
                        sp.wait_ge(s_added, ws.stop)
                        sp.dma_start(by_window(out)[:, ws, :], nodes[:, ws, :]).then_inc(s_out, 16)
                    sp.wait_ge(s_out, 16 * parts)

                @block.tensor
                def _(pe):
                    for k, ws in quads():
                        if k >= 2:
                            pe.wait_ge(s_added, ws[0] - QUAD)
                        for q, w in enumerate(ws):
                            last = nc.tensor.transpose(bank[k % 2][0:WINDOW, q * DIM:(q + 1) * DIM],
                                                       acc[:, w * WINDOW:(w + 1) * WINDOW], ident[:])
                        last.then_inc(s_turned, 1)

                @block.vector
                def _(dve):
                    dve.wait_ge(s_x1, 16)
                    for k, ws in quads():
                        dve.wait_ge(s_turned, k + 1)
                        part = nodes[:, ws[0]:ws[-1] + 1, :]
                        v.tensor_tensor(part, part, bank[k % 2][0:WINDOW, 0:len(ws) * DIM]
                                        .rearrange("p (w d) -> p w d", d=DIM), ALU.add).then_inc(s_added, len(ws))

        for layer in (0, 1):
            tail = ExitStack()
            nodes = sb(f"nodes{layer}", [WINDOW, WINDOWS, DIM], F32, tail)
            spare = sb(f"spare{layer}", [WINDOW, WINDOWS, DIM], F32, tail)
            x_rows = sb(f"x_rows{layer}", [WINDOW, WINDOWS, DIM], F32, tail)
            edge_bias = sb(f"edge_bias{layer}", [WINDOW, WINDOWS, DIM], F32, tail)
            gcn_nodes(layer, nodes, spare, x_rows, edge_bias)
            if layer == 1:
                add_edges(nodes, edge_bias)
            start_layer(layer + 1, nodes)
            tail.close()
            dense_pass(layer + 1)
        gin_mlp(1)
        gin_mlp(2)
        tail = ExitStack()
        finish(sb("out_rows", [WINDOW, WINDOWS, DIM], F32, tail))
        tail.close()


def kernel(x, src, dst, edge_attr_16, **params):
    import numpy as np
    import concourse.bacc as bacc
    from concourse.bass_utils import run_bass_kernel_spmd

    x, src, dst, attr = (np.asarray(a) for a in (x, src, dst, edge_attr_16))
    pad = TILES * SUPER - EDGES
    src_pad = np.concatenate([src, np.zeros(pad, src.dtype)])
    dst_pad = np.concatenate([dst, np.full(pad, NOWHERE, dst.dtype)])
    attr_tiles = np.concatenate([attr, np.zeros((pad, EDIM), attr.dtype)]).reshape(TILES, SUPER, EDIM)
    more = (ALL_SLICES - SLICES) * P - NODES
    own = [np.concatenate([np.arange(NODES, dtype=src.dtype), np.full(more, fill, src.dtype)]) for fill in (0, NOWHERE)]
    next_node = np.zeros((WINDOW, 2, WINDOW), np.float32)
    next_node[:, 0, :] = np.eye(WINDOW, k=-1) - np.eye(WINDOW)
    next_node[0, 1, WINDOW - 1] = 1.0
    arrays = {
        "x": x, "dst": dst, "dst_next": dst_pad[1:EDGES + 1], "edge_attr_16": attr,
        "pair_tiles": np.stack([src_pad.reshape(TILES, SUPER), dst_pad.reshape(TILES, SUPER)], 1).reshape(TILES, -1),
        "dst_tiles": dst_pad.reshape(TILES, SUPER),
        "src_slices": np.concatenate([src_pad, own[0]]).reshape(ALL_SLICES, P),
        "dst_slices": np.concatenate([dst_pad, own[1]]).reshape(ALL_SLICES, P),
        "dst_last": dst_pad[SUPER - 1::SUPER][None, :],
        "attr_tiles": attr_tiles.transpose(0, 2, 1).reshape(TILES, EDIM * SUPER),
        "L0_gnn_W1T": np.asarray(params["L0_gnn_W1"]).T, "L0_gnn_W2T": np.asarray(params["L0_gnn_W2"]).T,
        "ident": np.eye(P, dtype=np.float32),
        "node_iota": np.tile(np.arange(CHUNK, dtype=np.float32), (P, 1)),
        "step_iota": np.arange(BSLOTS, dtype=np.float32).reshape(BSLOTS // P, P).T,
        "node_id": np.arange(NODES, dtype=np.float32).reshape(WINDOWS, WINDOW).T,
        "next_node": next_node,
        "tile_iota": np.arange(TILES, dtype=np.float32)[None, :],
        "general_shift": np.tile(-CHUNK * np.arange(CHUNKS, dtype=np.float32), (P, 1)),
        "block_mask": np.kron(np.eye(P // EDIM), np.ones((EDIM, EDIM))).astype(np.float32),
        "fold": np.tile(np.eye(EDIM, dtype=np.float32), (P // EDIM, 1)),
    }
    for name in ROWS + COLPARS + MATS[2:] + ("L1_gnn_ee_w1",):
        arrays[name] = np.asarray(params[name])
    arrays = {n: np.ascontiguousarray(a) for n, a in arrays.items()}

    nc = bacc.Bacc("TRN2", target_bir_lowering=False, num_devices=1)
    A = {n: nc.dram_tensor(f"in_{n}", a.shape, mybir.dt.from_np(a.dtype), kind="ExternalInput").ap()
         for n, a in arrays.items()}
    out = nc.dram_tensor("out", (NODES, DIM), F32, kind="ExternalOutput").ap()
    program(nc, A, out)
    r = run_bass_kernel_spmd(nc, [{f"in_{n}": a for n, a in arrays.items()}], core_ids=[0])
    return r.results[0]["out"]
```
